# Optimizing a Trainium2 kernel written in Bass

```python
import numpy as np
import jax
import jax.numpy as jnp

def _softmax(x, axis=-1):
    return jax.nn.softmax(x, axis=axis)

def _gelu(x):
    return jax.nn.gelu(x, approximate=True)

def _silu(x):
    return jax.nn.silu(x)

def _sigmoid(x):
    return jax.nn.sigmoid(x)

def _layernorm(x, axis=-1, eps=1e-05):
    m = jnp.mean(x, axis=axis, keepdims=True)
    v = jnp.var(x, axis=axis, keepdims=True)
    return (x - m) / jnp.sqrt(v + eps)

def _scatter_add(tgt, idx, src, axis=0):
    return tgt.at[idx].add(src)

def _segment_sum(src, seg, n):
    return jax.ops.segment_sum(src, seg, n)
kernel_name = 'mk_decoder_preln_d1_seqx_r8_e34ec3'

def setup_inputs(seed: int=0):
    np.random.seed(seed)
    _w = jnp.asarray

    def _rec_inputs():
        import jax
        import jax.numpy as jnp
        _rk = jax.random.key(seed)
        x = -0.0002928 + 1 * jax.random.normal(jax.random.fold_in(_rk, 1), (16, 128, 256), jnp.float32)
        _lenS = 128 - jax.random.randint(jax.random.fold_in(_rk, 7), (16,), 0, max(1, 128 // 4) + 1, jnp.int32)
        _lenS2 = 128 - jax.random.randint(jax.random.fold_in(_rk, 8), (16,), 0, max(1, 128 // 4) + 1, jnp.int32)
        _ctx_512P = jax.random.normal(jax.random.fold_in(_rk, 11), (16, 16, 64), jnp.float32)
        _ctx_512c = jax.random.dirichlet(jax.random.fold_in(_rk, 511), 0.3 * jnp.ones((16,), jnp.float32), (16, 128))
        _ctx_512t = jnp.einsum('bsk,bkd->bsd', _ctx_512c, _ctx_512P)
        _ctx_512t = _ctx_512t * jax.lax.rsqrt(jnp.mean(jnp.square(_ctx_512t)) + 1e-12) * 0.953939
        ctx_512 = 0.000227908 + 0.99994 * (_ctx_512t + 0.3 * jax.random.normal(jax.random.fold_in(_rk, 611), (16, 128, 64), jnp.float32))
        return (x, ctx_512)
    x, ctx_512 = _rec_inputs()

    def _L0_attn_setup():
        import jax, jax.numpy as jnp
        import numpy as np
        NQ, NKV, HD, SW = (32, 8, 64, 64)
        QM = NQ // NKV

        def _rope_tables(L):
            inv_freq = (1.0 / 1024.0) ** jnp.linspace(0.0, 1.0, HD // 4)
            inv_freq = jnp.concatenate([inv_freq, jnp.zeros(HD // 4)])
            theta = jnp.arange(L, dtype=jnp.float32)[:, None] * inv_freq[None, :]
            return (jnp.cos(theta), jnp.sin(theta))

        def _apply_rope(x, cos, sin):
            x1, x2 = jnp.split(x, 2, axis=-1)
            return jnp.concatenate([x1 * cos + x2 * sin, -x1 * sin + x2 * cos], axis=-1)
        key = jax.random.key(seed)
        k1, k2, k3 = jax.random.split(key, 3)
        B, L, D = (1, 256, 256)
        x = jax.random.normal(k1, (B, L, D), jnp.float32)
        W_qkv = jax.random.normal(k2, (D, (NQ + 2 * NKV) * HD), jnp.float32) * 0.02
        W_out = jax.random.normal(k3, (NQ * HD, D), jnp.float32) * 0.02
        s = jnp.zeros((1, NKV, QM), jnp.float32)
        return {'x': x, 'W_qkv': W_qkv, 'W_out': W_out, 's': s}
    _L0_attn_all = _L0_attn_setup()
    _L0_attn_in = {k: v for k, v in _L0_attn_all.items() if k in ('W_qkv', 'W_out', 's')}
    del _L0_attn_all

    def _L0_xattn_setup():
        import jax, jax.numpy as jnp
        import numpy as np
        B, S, L = (2, 128, 128)
        DIM_Q, H, K, D_C, D_CQ, R = (256, 16, 128, 64, 192, 64)

        def _rope_tables(seq_len, dim, dtype):
            inv_freq = 1.0 / 10000.0 ** (jnp.arange(0, dim, 2, dtype=dtype) / dim)
            t = jnp.arange(seq_len, dtype=dtype)
            freqs = t[:, None] * inv_freq[None, :]
            sin = jnp.repeat(jnp.sin(freqs), 2, axis=-1)
            cos = jnp.repeat(jnp.cos(freqs), 2, axis=-1)
            return (sin, cos)

        def _rotate_half(x):
            h = x.shape[-1] // 2
            return jnp.concatenate([-x[..., h:], x[..., :h]], axis=-1)
        key = jax.random.key(seed)
        ks = jax.random.split(key, 8)
        s_in = 1.0 / np.sqrt(DIM_Q)
        s_k = 1.0 / np.sqrt(K)
        s_cq = 1.0 / np.sqrt(D_CQ)
        s_c = 1.0 / np.sqrt(D_C)
        return {'hidden_q': jax.random.normal(ks[0], (B, S, DIM_Q), jnp.float32), 'kv_c': jax.random.normal(ks[1], (B, L, D_C), jnp.float32), 'Wq': jax.random.normal(ks[2], (H * K, DIM_Q), jnp.float32) * s_in, 'w_kc_q': jax.random.normal(ks[3], (H, K, D_CQ), jnp.float32) * s_k, 'w_kc_kv': jax.random.normal(ks[4], (H, K, D_C), jnp.float32) * s_k, 'W_qr': jax.random.normal(ks[5], (H, D_CQ, R), jnp.float32) * s_cq / np.sqrt(R), 'W_kr': jax.random.normal(ks[6], (H, D_C, R), jnp.float32) * s_c, 'Wo': jax.random.normal(ks[7], (DIM_Q, H * K), jnp.float32) * s_k}
    _L0_xattn_all = _L0_xattn_setup()
    _L0_xattn_in = {k: v for k, v in _L0_xattn_all.items() if k in ('Wq', 'w_kc_q', 'w_kc_kv', 'W_qr', 'W_kr', 'Wo')}
    del _L0_xattn_all

    def _L0_ffn_setup():
        import jax, jax.numpy as jnp
        import numpy as np
        E = 8
        TOP_K = 2
        D = 256
        F_E = 1024 // E
        EPS = 1e-06
        SCALE = E / TOP_K
        key = jax.random.key(seed)
        ks = jax.random.split(key, 6)
        B, S = (2, 256)
        std = 0.02
        return {'hidden_states': jax.random.normal(ks[0], (B, S, D), jnp.float32), 'router_w': jax.random.normal(ks[1], (E, D), jnp.float32) * std, 'norm_w': jnp.ones((D,), jnp.float32), 'gate_w': jax.random.normal(ks[2], (E, D, F_E), jnp.float32) * std, 'up_w': jax.random.normal(ks[3], (E, D, F_E), jnp.float32) * std, 'down_w': jax.random.normal(ks[4], (E, F_E, D), jnp.float32) * std}
    _L0_ffn_all = _L0_ffn_setup()
    _L0_ffn_in = {k: v for k, v in _L0_ffn_all.items() if k in ('router_w', 'norm_w', 'gate_w', 'up_w', 'down_w')}
    del _L0_ffn_all
    return {'x': x, 'ctx_512': ctx_512, 'L0_attn_W_qkv': _L0_attn_in['W_qkv'], 'L0_attn_W_out': _L0_attn_in['W_out'], 'L0_attn_s': _L0_attn_in['s'], 'L0_xattn_Wq': _L0_xattn_in['Wq'], 'L0_xattn_w_kc_q': _L0_xattn_in['w_kc_q'], 'L0_xattn_w_kc_kv': _L0_xattn_in['w_kc_kv'], 'L0_xattn_W_qr': _L0_xattn_in['W_qr'], 'L0_xattn_W_kr': _L0_xattn_in['W_kr'], 'L0_xattn_Wo': _L0_xattn_in['Wo'], 'L0_ffn_router_w': _L0_ffn_in['router_w'], 'L0_ffn_norm_w': _L0_ffn_in['norm_w'], 'L0_ffn_gate_w': _L0_ffn_in['gate_w'], 'L0_ffn_up_w': _L0_ffn_in['up_w'], 'L0_ffn_down_w': _L0_ffn_in['down_w']}

def reference(x, ctx_512, L0_attn_W_qkv, L0_attn_W_out, L0_attn_s, L0_xattn_Wq, L0_xattn_w_kc_q, L0_xattn_w_kc_kv, L0_xattn_W_qr, L0_xattn_W_kr, L0_xattn_Wo, L0_ffn_router_w, L0_ffn_norm_w, L0_ffn_gate_w, L0_ffn_up_w, L0_ffn_down_w):
    import jax
    import jax.numpy as jnp

    def _L0_attn_ref(x, W_qkv, W_out, s):
        import jax, jax.numpy as jnp
        import numpy as np
        NQ, NKV, HD, SW = (32, 8, 64, 64)
        QM = NQ // NKV

        def _rope_tables(L):
            inv_freq = (1.0 / 1024.0) ** jnp.linspace(0.0, 1.0, HD // 4)
            inv_freq = jnp.concatenate([inv_freq, jnp.zeros(HD // 4)])
            theta = jnp.arange(L, dtype=jnp.float32)[:, None] * inv_freq[None, :]
            return (jnp.cos(theta), jnp.sin(theta))

        def _apply_rope(x, cos, sin):
            x1, x2 = jnp.split(x, 2, axis=-1)
            return jnp.concatenate([x1 * cos + x2 * sin, -x1 * sin + x2 * cos], axis=-1)
        B, L, D = x.shape
        proj = x @ W_qkv
        q, k, v = jnp.split(proj, (NQ * HD, (NQ + NKV) * HD), axis=-1)
        cos, sin = _rope_tables(L)
        q = _apply_rope(q.reshape(B, L, NKV, QM, HD), cos[None, :, None, None, :], sin[None, :, None, None, :])
        k = _apply_rope(k.reshape(B, L, NKV, HD), cos[None, :, None, :], sin[None, :, None, :])
        v = v.reshape(B, L, NKV, HD)
        sm_scale = 1.0 / jnp.sqrt(jnp.float32(HD))
        attn = jnp.einsum('bqhmd,bkhd->bhmqk', q, k) * sm_scale
        q_pos = jnp.arange(L)[:, None]
        k_pos = jnp.arange(L)[None, :]
        mask = (q_pos >= k_pos) & (q_pos < k_pos + SW)
        attn = jnp.where(mask, -jnp.inf, attn)
        sink = jnp.broadcast_to(s[:, :, :, None, None], attn.shape[:-1] + (1,))
        w = jax.nn.softmax(jnp.concatenate([attn, sink], axis=-1), axis=-1)[..., :-1]
        out = jnp.einsum('bhmqk,bkhd->bqhmd', w, v).reshape(B, L, NQ * HD)
        return out @ W_out

    def _L0_xattn_ref(hidden_q, kv_c, Wq, w_kc_q, w_kc_kv, W_qr, W_kr, Wo):
        import jax, jax.numpy as jnp
        import numpy as np
        B, S, L = (2, 128, 128)
        DIM_Q, H, K, D_C, D_CQ, R = (256, 16, 128, 64, 192, 64)

        def _rope_tables(seq_len, dim, dtype):
            inv_freq = 1.0 / 10000.0 ** (jnp.arange(0, dim, 2, dtype=dtype) / dim)
            t = jnp.arange(seq_len, dtype=dtype)
            freqs = t[:, None] * inv_freq[None, :]
            sin = jnp.repeat(jnp.sin(freqs), 2, axis=-1)
            cos = jnp.repeat(jnp.cos(freqs), 2, axis=-1)
            return (sin, cos)

        def _rotate_half(x):
            h = x.shape[-1] // 2
            return jnp.concatenate([-x[..., h:], x[..., :h]], axis=-1)
        b, s, _ = hidden_q.shape
        l = kv_c.shape[1]
        q_hk = (hidden_q @ Wq.T).reshape(b, s, H, K)
        q_big = jnp.einsum('bshk,hkq->bshq', q_hk, w_kc_q)
        sin, cos = _rope_tables(l, D_C, kv_c.dtype)
        kv_rope = kv_c * cos[None] + _rotate_half(kv_c) * sin[None]
        q_r = jnp.einsum('bshq,hqr->bhsr', q_big, W_qr)
        k_r = jnp.einsum('bld,hdr->bhlr', kv_rope, W_kr)
        scores = jnp.einsum('bhsr,bhlr->bhsl', q_r, k_r)
        attn = jax.nn.softmax(scores, axis=-1)
        ctx_c = jnp.einsum('bhsl,bld->bhsd', attn, kv_rope)
        ctx_lat = jnp.einsum('bhsd,hkd->bshk', ctx_c, w_kc_kv)
        out = ctx_lat.reshape(b, s, H * K) @ Wo.T
        return out

    def _L0_ffn_ref(hidden_states, router_w, norm_w, gate_w, up_w, down_w):
        import jax, jax.numpy as jnp
        import numpy as np
        E = 8
        TOP_K = 2
        D = 256
        F_E = 1024 // E
        EPS = 1e-06
        SCALE = E / TOP_K
        B, S, Dm = hidden_states.shape
        T = B * S
        flat = hidden_states.reshape(T, Dm)
        xf = flat.astype(jnp.float32)
        var = jnp.mean(xf * xf, axis=-1, keepdims=True)
        router_in = norm_w * (xf * jax.lax.rsqrt(var + EPS)).astype(flat.dtype)
        logits = router_in @ router_w.T
        probs = jax.nn.softmax(logits, axis=-1)
        topw, topi = jax.lax.top_k(probs, TOP_K)
        topw = topw / jnp.sum(topw, axis=-1, keepdims=True)
        cw = jnp.zeros((T, E), flat.dtype).at[jnp.arange(T)[:, None], topi].add(topw)
        g = jnp.einsum('td,edf->tef', flat, gate_w)
        u = jnp.einsum('td,edf->tef', flat, up_w)
        a = jax.nn.silu(g) * u
        expert_out = jnp.einsum('tef,efd->ted', a, down_w)
        y = jnp.einsum('ted,te->td', expert_out, cw) * SCALE
        return y.reshape(B, S, Dm)
    x = x + _L0_attn_ref(_layernorm(x, axis=-1), L0_attn_W_qkv, L0_attn_W_out, L0_attn_s)
    x = x + _L0_xattn_ref(_layernorm(x, axis=-1), ctx_512, L0_xattn_Wq, L0_xattn_w_kc_q, L0_xattn_w_kc_kv, L0_xattn_W_qr, L0_xattn_W_kr, L0_xattn_Wo)
    x = x + _L0_ffn_ref(_layernorm(x, axis=-1), L0_ffn_router_w, L0_ffn_norm_w, L0_ffn_gate_w, L0_ffn_up_w, L0_ffn_down_w)
    return x

_drawn_inputs = setup_inputs


def setup_inputs(seed=0):
    import zlib

    import numpy as np

    out = dict(_drawn_inputs(seed))
    spreads = {'L0_attn_s': (0.0, 2.0), 'L0_ffn_norm_w': (1.0, 0.6)}
    factors = {'L0_ffn_router_w': 8.285}
    for name, (base, spread) in spreads.items():
        noise = np.random.default_rng([zlib.crc32(name.encode()), seed]).standard_normal(out[name].shape)
        drawn = base * np.exp(spread * noise) if base else spread * noise
        out[name] = jnp.asarray(drawn.astype(out[name].dtype))
    for name, factor in factors.items():
        out[name] = (out[name] * factor).astype(out[name].dtype)
    return out
```

```python
import numpy as np
import concourse.bass as bass
from concourse import mybir
from contextlib import ExitStack

F32 = mybir.dt.float32
ALU = mybir.AluOpType
ACT = mybir.ActivationFunctionType
AX = mybir.AxisListType

P = 128
NB = 16
D = 256
DC = D // P
HD = 64
LN_EPS = 1e-5
RMS_EPS = 1e-6
MASKED = -3.0e38

PROJ = ["k", "q0", "q1", "v", "q2", "q3"]
ROPED = ["k", "q0", "q1", "q2", "q3"]
NPROJ, NROPE = len(PROJ), len(ROPED)


class Batch:

    def __init__(self, turn, c):
        self.turn, self.c = turn, c

    def __add__(self, k):
        return Batch(self.turn, self.c + k)

    def at(self, per, k):
        fixed = self.c * per + k
        return fixed if self.turn is None else self.turn * (2 * per) + fixed

    @property
    def parity(self):
        return self.c % 2

    def after(self, first):
        return self.turn is not None or self.c >= first


def decoder_layer(nc, x, ctx, wqkv, wout, sink, wqr_t, wkr_t, wkcq_t, wq, wkckv, wo_t, router, norm_w,
                  gate_w, up_w, down_w, ident, mask, rope, rope_c, tri, out):
    with ExitStack() as stack:
        def sb(name, shape, dt=F32):
            return stack.enter_context(nc.sbuf_tensor(name, shape, dt))

        def sem(name):
            return stack.enter_context(nc.semaphore(name))

        def bank(name):
            return stack.enter_context(nc.psum_tensor(name, [P, 512], F32))

        X = sb("X", [P, NB * D])
        big_w = sb("big_w", [P, 6144])
        wqkv_sb = big_w[:].rearrange("p (s c n) -> p s c n", s=NPROJ, c=DC)
        gate_sb = big_w[:, 0:2048].rearrange("p (c n) -> p c n", c=DC)
        up_sb = big_w[:, 2048:4096].rearrange("p (c n) -> p c n", c=DC)
        down_sb = big_w[:, 4096:6144].rearrange("p (e n) -> p e n", e=8)
        ctx_sb = big_w[:, 4096:5120].rearrange("p (b d) -> p b d", b=NB)
        wout_sb = sb("wout_sb", [P, 16, D])
        kv_rope = sb("kv_rope", [P, NB * HD])
        fold_a = sb("fold_a", [P, DC, 8, P])
        fold_n = sb("fold_n", [P, 8, D])
        wqr_sb = sb("wqr_sb", [P, 8, 192])
        wkr_sb = sb("wkr_sb", [P, 8, HD])
        wkcq_sb = sb("wkcq_sb", [96, 2, 16, P])
        wq_sb = sb("wq_sb", [P, 16, D])
        wkckv_sb = sb("wkckv_sb", [P, 16, HD])
        wo_sb = sb("wo_sb", [P, 16, D])
        ident_sb = sb("ident_sb", [P, P])
        mask_sb = sb("mask_sb", [P, P])
        zero_sb = sb("zero_sb", [P, P])
        sink_sb = sb("sink_sb", [P, 32])
        rope_sb = sb("rope_sb", [P, 2, 2, 16])
        rope_c_sb = sb("rope_c_sb", [P, 2, HD])
        router_sb = sb("router_sb", [P, DC, 8])
        norm_sb = sb("norm_sb", [P, DC])
        router_w = sb("router_w", [P, DC, 8])
        tri_sb = sb("tri_sb", [P, 8, 8])

        xn = [sb(f"xn{i}", [P, D]) for i in range(2)]
        xn_t = [sb(f"xn_t{i}", [P, DC, P]) for i in range(2)]
        ln_st = sb("ln_st", [P, NB * 6])
        ln_mv = sb("ln_mv", [P, NB, 2])
        ln_var = sb("ln_var", [P, NB])
        ln_std = sb("ln_std", [P, NB])
        ln_tmp = sb("ln_tmp", [P, NB])
        ln_rs = sb("ln_rs", [P, NB])
        rms_rs = sb("rms_rs", [P, NB])
        q_t = [sb(f"q_t{i}", [P, 4, 4, P]) for i in range(2)]
        k_bd = [sb(f"k_bd{i}", [P, 4, 2, P]) for i in range(2)]
        v_n = [sb(f"v_n{i}", [P, 8, HD]) for i in range(2)]
        roped = [sb(f"roped{i}", [P, 8, 4, 16]) for i in range(2)]
        rot_a = [sb(f"rot_a{i}", [P, 8, 2, 16]) for i in range(2)]
        rot_b = [sb(f"rot_b{i}", [P, 8, 2, 16]) for i in range(2)]
        probs = [sb(f"probs{i}", [P, 8, P]) for i in range(4)]
        gate_keeper = sb("gate_keeper", [P, 8])
        peak = sb("peak", [P, 4, 8])
        neg_peak = sb("neg_peak", [P, 4, 8])
        sink_arg = sb("sink_arg", [P, 4, 8])
        sink_exp = sb("sink_exp", [P, 4, 8])
        row_sum = sb("row_sum", [P, 4, 8])
        denom = sb("denom", [P, 4, 8])
        inv_sum = sb("inv_sum", [P, 4, 8])
        probs_t = [sb(f"probs_t{j}", [P, 512]) for j in range(2)]
        head_out = [sb(f"head_out{i}", [P, 4, P]) for i in range(2)]
        kv_dup = [sb(f"kv_dup{i}", [P, 2, HD]) for i in range(2)]
        fold_b1 = [roped[i][0:96].rearrange("p a b c -> p (a b c)") for i in range(2)]
        fold_b2 = [rot_a[i][:].rearrange("p a b c -> p (a b c)") for i in range(2)]
        gate_t = [probs[i][:].rearrange("p a b -> p (a b)")[:, 0:512] for i in range(2)]
        gate_s = [probs[i][:].rearrange("p a b -> p (a b)")[:, 512:1024] for i in range(2)]
        hidden = [probs[2 + i][:].rearrange("p a b -> p (a b)")[:, 0:512] for i in range(2)]
        hidden_t = [probs[2 + i][:].rearrange("p a b -> p (a b)")[:, 512:1024] for i in range(2)]
        r_log = sb("r_log", [P, 8])
        r_max = sb("r_max", [P, 1])
        r_arg = sb("r_arg", [P, 8])
        r_exp = sb("r_exp", [P, 8])
        r_gt = sb("r_gt", [P, 8, 8])
        r_eq = sb("r_eq", [P, 8, 8])
        r_rank = sb("r_rank", [P, 8])
        r_sel = sb("r_sel", [P, 8])
        r_sum = sb("r_sum", [P, 1])
        r_inv = sb("r_inv", [P, 1])
        r_cw = [sb(f"r_cw{i}", [P, 8]) for i in range(2)]

        proj_ps = [bank("proj_ps0"), bank("proj_ps1")]
        score_ps = [bank("score_ps0"), bank("score_ps1")]
        turn_ps = [bank("turn_ps0"), bank("turn_ps1")]
        pv_ps = bank("pv_ps")
        y_ps = bank("y_ps")

        ld_const, ld_x0, ld_x, ld_ctx = sem("ld_const"), sem("ld_x0"), sem("ld_x"), sem("ld_ctx")
        ld_w = [sem(f"ld_w_{s}") for s in PROJ]
        ld_wout, ld_fold, ld_ffn = sem("ld_wout"), sem("ld_fold"), sem("ld_ffn")
        stored = sem("stored")
        zeroed = sem("zeroed")
        kv_part, kv_done = sem("kv_part"), sem("kv_done")

        class Sems:

            def __init__(self, name, units, masked):
                self.U, self.masked = units, masked
                s = lambda what: sem(f"{name}_{what}")
                self.stats = s("stats")
                self.xn_ready = s("xn_ready")
                self.ln_turned = s("ln_turned")
                self.xn_t_ready = s("xn_t_ready")
                self.x_added = s("x_added")
                if units:
                    self.scored = s("scored")
                    self.peaked = s("peaked")
                    self.shift_ready = s("shift_ready")
                    self.exped = s("exped")
                    self.summed = s("summed")
                    self.inv_ready = s("inv_ready")
                    self.normed = s("normed")
                    self.p_turned = s("p_turned")
                    self.p_t0_ready = s("p_t0_ready")
                    self.p_t1_ready = s("p_t1_ready")
                    self.pv_done = s("pv_done")
                    self.o_ready = s("o_ready")
                    self.o_used = s("o_used")

        A = Sems("self", 4, True)
        C = Sems("cross", 2, False)
        F = Sems("ffn", 0, False)
        projected = sem("self_projected")
        proj_out = sem("self_proj_out")
        rot_done = sem("self_rot_done")
        roped_done = sem("self_roped_done")
        qk_turned = sem("self_qk_turned")
        k_ready = sem("self_k_ready")
        q_ready = sem("self_q_ready")
        f1_done, f1_out = sem("fold_b1_done"), sem("fold_b1_out")
        f2_done, f2_out = sem("fold_b2_done"), sem("fold_b2_out")
        f3_done, f3_out = sem("fold_a_done"), sem("fold_a_out")
        f4_done, f4_out = sem("fold_n_done"), sem("fold_n_out")
        kv_copied = sem("cross_kv_copied")
        v_copied = sem("cross_v_copied")
        kv_turned = sem("cross_kv_turned")
        kv_t_ready = sem("cross_kv_t_ready")
        cq_done = sem("cross_cq_done")
        cq_ready = sem("cross_cq_ready")
        logit_done = sem("ffn_logit_done")
        logit_read = sem("ffn_logit_read")
        norm_step = sem("norm_step")
        var_ready = sem("var_ready")
        std_ready = sem("std_ready")
        r_step = sem("ffn_router_step")
        r_arg_ready = sem("ffn_arg_ready")
        r_exped = sem("ffn_r_exped")
        gate_done = sem("ffn_gate_done")
        up_done = sem("ffn_up_done")
        gate_tanh = sem("ffn_gate_tanh")
        silu_ready = sem("ffn_silu_ready")
        hidden_ready = sem("ffn_hidden_ready")
        h_turned = sem("ffn_h_turned")
        h_t_ready = sem("ffn_h_t_ready")
        down_done = sem("ffn_down_done")
        r_ready = sem("ffn_r_ready")
        rw_ready = sem("ffn_rw_ready")
        RSTEPS = 8

        def x_of(b):
            if b.turn is None:
                return X[:, b.c * D:(b.c + 1) * D]
            return X[:, bass.ds(b.turn * (2 * D) + b.c * D, D)]

        def loop(eng, body, first, last):
            with eng.Fori(first // 2, last // 2) as turn:
                for c in range(2):
                    body(Batch(turn, c))

        SELF_TURNS = [("p0", 0), ("p1", 0), ("q3", 0),
                      ("p0", 1), ("p1", 1), ("k", 1), ("q0", 1),
                      ("p0", 2), ("p1", 2), ("q1", 2),
                      ("p0", 3), ("p1", 3), ("q2", 3), ("ln", 3)]
        CROSS_TURNS = [("p0", 0), ("p1", 0), ("kv", 0), ("p0", 1), ("p1", 1), ("ln", 1)]

        def turn_bank(turns, kind, u):
            return turn_ps[turns.index((kind, u)) % 2]

        def wait_turn_bank(eng, s, turns, b, kind, u, exists):
            i = turns.index((kind, u))
            while True:
                i -= 2
                if i < 0:
                    i += len(turns)
                    b = b + -1
                k, w = turns[i]
                if b.turn is None and not exists(b.c, k, w):
                    if b.c < -1:
                        return
                    continue
                break
            if k == "p0":
                eng.wait_ge(s.p_t0_ready, b.at(s.U, w - 2 + 1))
            elif k == "p1":
                eng.wait_ge(s.p_t1_ready, b.at(s.U, w - 2 + 1))
            elif k == "ln":
                eng.wait_ge(s.xn_t_ready, b.at(1, 3))
            elif k == "kv":
                eng.wait_ge(kv_t_ready, b.at(1, 2))
            elif k == "k":
                eng.wait_ge(k_ready, b.at(1, 2))
            elif k == "q3":
                eng.wait_ge(q_ready, b.at(4, 4))
            else:
                eng.wait_ge(q_ready, b.at(4, 4 + int(k[1]) + 1))

        def self_exists(c, kind, u):
            if kind in ("p0", "p1"):
                return 4 * c + u - 2 >= 0
            if kind == "ln":
                return 0 <= c + 2 < NB
            if kind == "q3":
                return 0 <= c < NB
            return 0 <= c + 1 < NB

        def cross_exists(c, kind, u):
            if kind in ("p0", "p1"):
                return 2 * c + u - 2 >= 0
            return 0 <= c + (2 if kind == "ln" else 1) < NB

        def unit_buf(s, b, u):
            return (u if s.U == 4 else 2 * b.parity + u) % 4

        block = stack.enter_context(nc.Block())

        @block.sync
        def _(sp):
            x_v = x.rearrange("b s d -> s b d")
            X_v = X[:].rearrange("p (b d) -> p b d", d=D)
            sp.dma_start(X_v[:, 0:2], x_v[:, 0:2]).then_inc(ld_x0, 16)
            sp.dma_start(ident_sb[:], ident).then_inc(ld_const, 16)
            sp.dma_start(wqkv_sb[:, 0], wqkv[:, 0]).then_inc(ld_w[0], 16)
            sp.dma_start(rope_sb[:], rope).then_inc(ld_const, 16)
            sp.dma_start(mask_sb[:], mask).then_inc(ld_const, 16)
            sp.dma_start(sink_sb[:], sink.partition_broadcast(P)).then_inc(ld_const, 16)
            for s in range(1, NPROJ):
                sp.dma_start(wqkv_sb[:, s], wqkv[:, s]).then_inc(ld_w[s], 16)
            sp.dma_start(X_v[:, 2:NB], x_v[:, 2:NB]).then_inc(ld_x, 16)
            sp.dma_start(wout_sb[:], wout).then_inc(ld_wout, 16)
            sp.dma_start(rope_c_sb[:], rope_c).then_inc(ld_ctx, 16)
            for dst, src in ((wqr_sb, wqr_t), (wkr_sb, wkr_t), (wkcq_sb, wkcq_t), (wq_sb, wq),
                             (wkckv_sb, wkckv), (wo_sb, wo_t)):
                sp.dma_start(dst[:], src).then_inc(ld_fold, 16)
            sp.wait_ge(projected, NPROJ * NB)
            sp.dma_start(ctx_sb, ctx.rearrange("b l d -> l b d")).then_inc(ld_ctx, 16)
            sp.dma_start(gate_sb, gate_w).then_inc(ld_ffn, 16)
            sp.dma_start(up_sb, up_w).then_inc(ld_ffn, 16)
            sp.dma_start(router_sb[:], router).then_inc(ld_ffn, 16)
            sp.dma_start(norm_sb[:], norm_w).then_inc(ld_ffn, 16)
            sp.dma_start(tri_sb[:], tri).then_inc(ld_ffn, 16)
            sp.wait_ge(kv_done, 1)
            sp.dma_start(down_sb, down_w).then_inc(ld_ffn, 16)

            def store(b):
                sp.wait_ge(F.x_added, b.at(1, 1))
                if b.turn is None:
                    dst = out[b.c]
                else:
                    dst = out[bass.ds(b.turn * 2 + b.c, 1)].rearrange("a s d -> (a s) d")
                sp.dma_start(dst, x_of(b)).then_inc(stored, 16)

            loop(sp, store, 0, NB)
            sp.wait_ge(stored, 16 * NB)

        @block.tensor
        def _(pe):
            def turn(dst, src):
                return nc.tensor.transpose(dst, src, ident_sb[:])

            def layernorm_turn(s, b, ps):
                pe.wait_ge(s.xn_ready, b.at(1, 1))
                for c in range(DC):
                    last = turn(ps[:, c * P:(c + 1) * P], xn[b.parity][:, c * P:(c + 1) * P])
                last.then_inc(s.ln_turned, 1)

            def scores(s, b, u, queries, keys):
                for half in range(2):
                    if b.after(1) or u:
                        pe.wait_ge(s.peaked, b.at(2 * s.U, 2 * u - 1 + half))
                    for m in (2 * half, 2 * half + 1):
                        last = nc.tensor.matmul(score_ps[half][:, (m % 2) * D:(m % 2 + 1) * D],
                                                queries[:, m, :], keys, start=True, stop=True)
                    last.then_inc(s.scored, 1)

            def turn_weights(s, b, u, turns, exists):
                pe.wait_ge(s.normed, b.at(s.U, u - 2 + 1))
                for j in range(2):
                    wait_turn_bank(pe, s, turns, b, f"p{j}", u, exists)
                    ps = turn_bank(turns, f"p{j}", u)
                    for m in range(4):
                        last = turn(ps[:, m * P:(m + 1) * P], probs[unit_buf(s, b, u - 2)][:, 2 * m + j, :])
                    last.then_inc(s.p_turned, 1)

            def weigh_values(s, b, u, values):
                pe.wait_ge(s.p_t0_ready, b.at(s.U, u - 1))
                pe.wait_ge(s.p_t1_ready, b.at(s.U, u - 1))
                if b.c * s.U + u - 2 > 0 or b.turn is not None:
                    pe.wait_ge(s.o_ready, b.at(s.U, u - 2))
                for j in range(2):
                    last = nc.tensor.matmul(pv_ps[j * HD:(j + 1) * HD, :], values(j), probs_t[j][:],
                                            start=True, stop=True)
                last.then_inc(s.pv_done, 1)

            def project_out(s, b, u, weights):
                first, w = (u - 3) % s.U == 0, (u - 3) % s.U
                pe.wait_ge(s.o_ready, b.at(s.U, u - 2))
                if first:
                    done = (u - 3) // s.U
                    if b.c + done > 0 or b.turn is not None:
                        pe.wait_ge(s.x_added, b.at(1, done))
                for m in range(4):
                    last = nc.tensor.matmul(y_ps[:, 0:D], head_out[(u - 3) % 2][:, m, :],
                                            weights[:, 4 * w + m, :], start=(first and m == 0),
                                            stop=(w == s.U - 1 and m == 3))
                last.then_inc(s.o_used, 1)

            def project(b, seq, wait_load=False):
                if seq == 0:
                    pe.wait_ge(A.xn_t_ready, b.at(1, 1))
                if wait_load:
                    pe.wait_ge(ld_w[seq], 16)
                if b.after(1) or seq >= 2:
                    pe.wait_ge(proj_out, b.at(NPROJ, seq - 1))
                for c in range(DC):
                    last = nc.tensor.matmul(proj_ps[seq % 2][:], xn_t[b.parity][:, c, :],
                                            wqkv_sb[:, seq, c, :], start=(c == 0), stop=(c == DC - 1))
                last.then_inc(projected, 1)

            def turn_qk(b, what, step_b, u):
                r = ROPED.index(what)
                pe.wait_ge(roped_done, b.at(NROPE, r + 1))
                wait_turn_bank(pe, A, SELF_TURNS, step_b, what, u, self_exists)
                ps = turn_bank(SELF_TURNS, what, u)
                src = roped[(b.parity + r) % 2][:].rearrange("p a b c -> p (a b c)")
                for m in range(4):
                    last = turn(ps[:, m * P:(m + 1) * P], src[:, m * P:(m + 1) * P])
                last.then_inc(qk_turned, 1)

            def self_step(b, u, more=True, more2=True):
                pe.wait_ge(q_ready, b.at(4, u + 1))
                if u == 0:
                    pe.wait_ge(k_ready, b.at(1, 1))
                scores(A, b, u, q_t[b.parity][:, u], k_bd[b.parity][:, u].rearrange("p j k -> p (j k)"))
                if more:
                    project(b + 1, (0, 2, 4, 5)[u])
                if b.after(1) or u >= 2:
                    turn_weights(A, b, u, SELF_TURNS, self_exists)
                if b.after(1) or u >= 3:
                    project_out(A, b, u, wout_sb)
                if u == 0:
                    turn_qk(b, "q3", b, u)
                elif more:
                    for what in ({1: ("k", "q0"), 2: ("q1",), 3: ("q2",)}[u]):
                        turn_qk(b + 1, what, b, u)
                if b.after(1) or u >= 2:
                    vb = b if u >= 2 else b + -1
                    w = (u - 2) % 4
                    weigh_values(A, b, u, lambda j: v_n[vb.parity][:, 2 * w + j, :])
                if more and u < 2:
                    project(b + 1, (1, 3)[u])
                if u == 3 and more2:
                    wait_turn_bank(pe, A, SELF_TURNS, b, "ln", 3, self_exists)
                    layernorm_turn(A, b + 2, turn_bank(SELF_TURNS, "ln", 3))

            def self_batch(b, more=True, more2=True):
                for u in range(4):
                    self_step(b, u, more, more2)

            b0, before = Batch(None, 0), Batch(None, -1)
            pe.wait_ge(ld_const, 16 * 4)
            layernorm_turn(A, b0, turn_bank(SELF_TURNS, "ln", 3))
            project(b0, 0, True)
            project(b0, 1, True)
            turn_qk(b0, "k", before, 1)
            project(b0, 2, True)
            turn_qk(b0, "q0", before, 1)
            project(b0, 3, True)
            turn_qk(b0, "q1", before, 2)
            project(b0, 4, True)
            project(b0, 5, True)
            turn_qk(b0, "q2", before, 3)
            wait_turn_bank(pe, A, SELF_TURNS, before, "ln", 3, self_exists)
            layernorm_turn(A, b0 + 1, turn_bank(SELF_TURNS, "ln", 3))
            pe.wait_ge(zeroed, 1)
            pe.wait_ge(ld_wout, 16)
            self_batch(b0)
            self_batch(b0 + 1)
            loop(pe, self_batch, 2, NB - 2)
            self_batch(Batch(None, NB - 2), True, False)
            self_batch(Batch(None, NB - 1), False, False)
            end = Batch(None, NB)
            for u in range(3):
                if u < 2:
                    turn_weights(A, end, u, SELF_TURNS, self_exists)
                project_out(A, end, u, wout_sb)
                if u < 2:
                    weigh_values(A, end, u, lambda j: v_n[(NB - 1) % 2][:, 2 * (u + 2) + j, :])

            pe.wait_ge(ld_fold, 16 * 6)
            pe.wait_ge(A.p_t0_ready, 4 * NB)
            pe.wait_ge(A.p_t1_ready, 4 * NB)
            pe.wait_ge(A.o_ready, 4 * NB)
            for t in range(4):
                v, e = t // 2, t % 2
                heads = [8 * v + e + 2 * i for i in range(4)]
                if t >= 2:
                    pe.wait_ge(f1_out, t - 1)
                for i, h in enumerate(heads):
                    rows = slice(e * HD, (e + 1) * HD)
                    for c in range(2):
                        last = nc.tensor.matmul(score_ps[e][0:96, (2 * i + c) * HD:(2 * i + c + 1) * HD],
                                                wqr_sb[rows, h // 2, c * 96:(c + 1) * 96],
                                                wkr_sb[rows, h // 2, :], start=True, stop=True)
                last.then_inc(f1_done, 1)
                if t >= 2:
                    pe.wait_ge(f4_out, t - 1)
                for i in range(2):
                    m = 2 * e + i
                    for j in range(2):
                        h = 8 * v + 4 * j + m
                        last = nc.tensor.matmul(turn_ps[e][j * HD:(j + 1) * HD, i * D:(i + 1) * D],
                                                wkckv_sb[:, h, :], wo_sb[:, h, :], start=True, stop=True)
                last.then_inc(f4_done, 1)
                pe.wait_ge(f1_out, t + 1)
                if t >= 2:
                    pe.wait_ge(f2_out, t - 1)
                for i, h in enumerate(heads):
                    for c in range(2):
                        last = nc.tensor.matmul(proj_ps[e][:, i * HD:(i + 1) * HD], wkcq_sb[:, c, h, :],
                                                fold_b1[e][:, (2 * i + c) * HD:(2 * i + c + 1) * HD],
                                                start=(c == 0), stop=(c == 1))
                last.then_inc(f2_done, 1)
                pe.wait_ge(f2_out, t + 1)
                if t >= 1:
                    pe.wait_ge(f3_out, t)
                for c in range(DC):
                    for i, h in enumerate(heads):
                        last = nc.tensor.matmul(pv_ps[:, (4 * c + i) * HD:(4 * c + i + 1) * HD],
                                                wq_sb[:, h, c * P:(c + 1) * P],
                                                fold_b2[e][:, i * HD:(i + 1) * HD], start=True, stop=True)
                last.then_inc(f3_done, 1)

            def latent_queries(b, u):
                if u == 0:
                    pe.wait_ge(C.xn_t_ready, b.at(1, 1))
                if b.after(1):
                    pe.wait_ge(cq_ready, b.at(2, u - 1))
                for m in range(4):
                    for c in range(DC):
                        last = nc.tensor.matmul(proj_ps[u][:, m * P:(m + 1) * P],
                                                fold_a[:, c, 4 * u + m, :], xn_t[b.parity][:, c, :],
                                                start=(c == 0), stop=(c == DC - 1))
                last.then_inc(cq_done, 1)

            def turn_latents(b, step_b):
                pe.wait_ge(kv_copied, b.at(1, 1))
                wait_turn_bank(pe, C, CROSS_TURNS, step_b, "kv", 0, cross_exists)
                turn(turn_bank(CROSS_TURNS, "kv", 0)[:, 0:P],
                     kv_dup[b.parity][:].rearrange("p a b -> p (a b)")).then_inc(kv_turned, 1)

            def cross_step(b, u, more=True, more2=True):
                pe.wait_ge(cq_ready, b.at(2, u + 1))
                if u == 0:
                    pe.wait_ge(kv_t_ready, b.at(1, 1))
                scores(C, b, u, q_t[b.parity][:, u], k_bd[b.parity][:, 0].rearrange("p j k -> p (j k)"))
                if more:
                    latent_queries(b + 1, u)
                if b.after(1):
                    turn_weights(C, b, u, CROSS_TURNS, cross_exists)
                if b.after(2) or (b.after(1) and u >= 1):
                    project_out(C, b, u, fold_n)
                if u == 0 and more:
                    turn_latents(b + 1, b)
                if b.after(1):
                    pe.wait_ge(v_copied, b.at(1, 0))
                    weigh_values(C, b, u, lambda j: v_n[(b + -1).parity][:, 0, :])
                if u == 1 and more2:
                    wait_turn_bank(pe, C, CROSS_TURNS, b, "ln", 1, cross_exists)
                    layernorm_turn(C, b + 2, turn_bank(CROSS_TURNS, "ln", 1))

            def cross_batch(b, more=True, more2=True):
                for u in range(2):
                    cross_step(b, u, more, more2)

            pe.wait_ge(f4_out, 4)
            layernorm_turn(C, b0, turn_bank(CROSS_TURNS, "ln", 1))
            turn_latents(b0, before)
            pe.wait_ge(f3_out, 4)
            latent_queries(b0, 0)
            latent_queries(b0, 1)
            wait_turn_bank(pe, C, CROSS_TURNS, before, "ln", 1, cross_exists)
            layernorm_turn(C, b0 + 1, turn_bank(CROSS_TURNS, "ln", 1))
            cross_batch(b0)
            cross_batch(b0 + 1)
            loop(pe, cross_batch, 2, NB - 2)
            cross_batch(Batch(None, NB - 2), True, False)
            cross_batch(Batch(None, NB - 1), False, False)
            for u in range(3):
                if u < 2:
                    turn_weights(C, end, u, CROSS_TURNS, cross_exists)
                project_out(C, end, u, fold_n)
                if u < 2:
                    pe.wait_ge(v_copied, NB)
                    weigh_values(C, end, u, lambda j: v_n[(NB - 1) % 2][:, 0, :])

            def ffn_turn(b):
                if b.after(1):
                    pe.wait_ge(logit_read, b.at(1, 0))
                layernorm_turn(F, b, pv_ps[:, P:3 * P])

            def experts_in(b, half):
                cols = slice(half * 512, (half + 1) * 512)
                if b.after(1):
                    pe.wait_ge(silu_ready, b.at(2, half - 1))
                for c in range(DC):
                    last = nc.tensor.matmul(score_ps[half][:], xn_t[b.parity][:, c, :],
                                            gate_sb[:, c, cols], start=(c == 0), stop=(c == DC - 1))
                last.then_inc(gate_done, 1)
                if b.after(1):
                    pe.wait_ge(hidden_ready, b.at(2, half - 1))
                for c in range(DC):
                    last = nc.tensor.matmul(proj_ps[half][:], xn_t[b.parity][:, c, :],
                                            up_sb[:, c, cols], start=(c == 0), stop=(c == DC - 1))
                last.then_inc(up_done, 1)

            def experts_out(b, half):
                pe.wait_ge(hidden_ready, b.at(2, half + 1))
                if b.after(1):
                    pe.wait_ge(h_t_ready, b.at(2, half - 1))
                for e in range(4):
                    last = turn(turn_ps[half][:, e * P:(e + 1) * P], hidden[half][:, e * P:(e + 1) * P])
                last.then_inc(h_turned, 1)
                pe.wait_ge(h_t_ready, b.at(2, half + 1))
                if half == 0 and b.after(1):
                    pe.wait_ge(F.x_added, b.at(1, 0))
                for e in range(4):
                    last = nc.tensor.matmul(y_ps[:, 0:D], hidden_t[half][:, e * P:(e + 1) * P],
                                            down_sb[:, 4 * half + e, :], start=(half == 0 and e == 0),
                                            stop=(half == 1 and e == 3))
                last.then_inc(down_done, 1)

            def ffn_batch(b, more=True):
                pe.wait_ge(F.xn_t_ready, b.at(1, 1))
                for c in range(DC):
                    last = nc.tensor.matmul(pv_ps[:, 0:8], xn_t[b.parity][:, c, :], router_w[:, c, :],
                                            start=(c == 0), stop=(c == DC - 1))
                last.then_inc(logit_done, 1)
                experts_in(b, 0)
                if b.after(1):
                    experts_out(b + -1, 1)
                experts_in(b, 1)
                if more:
                    ffn_turn(b + 1)
                experts_out(b, 0)

            pe.wait_ge(C.x_added, NB)
            pe.wait_ge(ld_ffn, 16 * 6)
            pe.wait_ge(rw_ready, 2)
            ffn_turn(b0)
            ffn_batch(b0)
            ffn_batch(b0 + 1)
            loop(pe, ffn_batch, 2, NB - 2)
            ffn_batch(Batch(None, NB - 2))
            ffn_batch(Batch(None, NB - 1), False)
            experts_out(Batch(None, NB - 1), 1)

        @block.vector
        def _(dve):
            steps = [0]

            def then(ins):
                steps[0] += 1
                ins.then_inc(norm_step, 1)
                dve.wait_ge(norm_step, steps[0])

            def statistics(s, b):
                dst = (ln_st[:, b.c * 6:(b.c + 1) * 6] if b.turn is None else
                       ln_st[:, bass.ds(b.turn * 12 + b.c * 6, 6)])
                nc.vector.bn_stats(dst, x_of(b)).then_inc(s.stats, 1)

            def inverse_root(group, cols, dst):
                steps[0] += 1
                nc.vector.tensor_copy(ln_tmp[:, cols], ln_var[:, cols]).then_inc(norm_step, 1)
                dve.wait_ge(std_ready, group + 1)
                then(nc.vector.reciprocal(dst[:, cols], ln_std[:, cols]))
                then(nc.vector.tensor_tensor(ln_tmp[:, cols], ln_tmp[:, cols], dst[:, cols], ALU.mult))
                then(nc.vector.tensor_tensor(ln_tmp[:, cols], ln_tmp[:, cols], dst[:, cols], ALU.mult))
                then(nc.vector.tensor_scalar(ln_tmp[:, cols], ln_tmp[:, cols], -0.5, 1.5, ALU.mult, ALU.add))
                then(nc.vector.tensor_tensor(dst[:, cols], dst[:, cols], ln_tmp[:, cols], ALU.mult))

            def deviations(s, group, first, last):
                dve.wait_ge(s.stats, last)
                for b in range(first, last):
                    ins = nc.vector.bn_aggr(ln_mv[:, b, :], ln_st[:, b * 6:(b + 1) * 6])
                then(ins)
                cols = slice(first, last)
                nc.vector.tensor_scalar(ln_var[:, cols], ln_mv[:, cols, 1], LN_EPS, None, ALU.add)\
                    .then_inc(var_ready, 1)
                dve.wait_ge(var_ready, group + 1)
                inverse_root(group, cols, ln_rs)

            def layernorm(s, b):
                p = b.parity
                if b.turn is None:
                    mean, rs = ln_mv[:, b.c, 0:1], ln_rs[:, b.c:b.c + 1]
                else:
                    mean = ln_mv[:].rearrange("p b k -> p (b k)")[:, bass.ds(b.turn * 4 + b.c * 2, 1)]
                    rs = ln_rs[:, bass.ds(b.turn * 2 + b.c, 1)]
                if b.after(2):
                    dve.wait_ge(s.ln_turned, b.at(1, -1))
                nc.vector.tensor_scalar(xn[p][:], x_of(b), mean, rs, ALU.subtract, ALU.mult)\
                    .then_inc(s.xn_ready, 1)

            def peaks(s, b, u):
                buf = unit_buf(s, b, u)
                if b.after(1 if s.U == 4 else 2):
                    dve.wait_ge(s.p_turned, b.at(2 * s.U, 2 * (u - 3)))
                for half in range(2):
                    dve.wait_ge(s.scored, b.at(2 * s.U, 2 * u + half + 1))
                    nc.vector.memset(gate_keeper[:, 2 * buf + half:2 * buf + half + 1], 0.0)
                    for i in range(4):
                        h = 4 * half + i
                        start = sink_sb[:, 8 * u + h:8 * u + h + 1] if s.masked else MASKED
                        last = nc.vector.tensor_tensor_reduce(
                            out=probs[buf][:, h, :], in0=score_ps[half][:, i * P:(i + 1) * P],
                            in1=(mask_sb if s.masked else zero_sb)[:], scale=1.0, scalar=start,
                            op0=ALU.add, op1=ALU.max, accum_out=peak[:, buf, h:h + 1])
                    last.then_inc(s.peaked, 1)
                dve.wait_ge(s.peaked, b.at(2 * s.U, 2 * u + 2))
                last = nc.vector.tensor_scalar(neg_peak[:, buf, :], peak[:, buf, :], -1.0, None, ALU.mult)
                if s.masked:
                    last = nc.vector.tensor_tensor(sink_arg[:, buf, :], sink_sb[:, 8 * u:8 * u + 8],
                                                   peak[:, buf, :], ALU.subtract)
                last.then_inc(s.shift_ready, 1)

            def inverse_sums(s, b, u):
                buf = unit_buf(s, b, u)
                dve.wait_ge(s.exped, b.at(s.U, u + 1))
                if s.masked:
                    nc.vector.tensor_tensor(denom[:, buf, :], row_sum[:, buf, :], sink_exp[:, buf, :],
                                            ALU.add).then_inc(s.summed, 1)
                    dve.wait_ge(s.summed, b.at(s.U, u + 1))
                nc.vector.reciprocal(inv_sum[:, buf, :], (denom if s.masked else row_sum)[:, buf, :])\
                    .then_inc(s.inv_ready, 1)

            def take_weights(s, b, u, turns):
                dve.wait_ge(s.p_turned, b.at(2 * s.U, 2 * (u - 2) + 1))
                if b.turn is not None or b.c * s.U + u - 3 >= 0:
                    dve.wait_ge(s.pv_done, b.at(s.U, u - 2))
                nc.vector.tensor_copy(probs_t[0][:], turn_bank(turns, "p0", u)[:]).then_inc(s.p_t0_ready, 1)

            def take_heads(s, b, u):
                dve.wait_ge(s.pv_done, b.at(s.U, u - 1))
                if b.turn is not None or b.c * s.U + u - 4 >= 0:
                    dve.wait_ge(s.o_used, b.at(s.U, u - 3))
                nc.vector.tensor_copy(head_out[u % 2][:].rearrange("p a b -> p (a b)"), pv_ps[:])\
                    .then_inc(s.o_ready, 1)

            def add_residual(s, after, b):
                dve.wait_ge(s.o_used, b.at(s.U, s.U))
                nc.vector.tensor_tensor(x_of(b), y_ps[:, 0:D], x_of(b), ALU.add).then_inc(s.x_added, 1)
                dve.wait_ge(s.x_added, b.at(1, 1))
                statistics(after, b)

            def rotate(b, what):
                r, seq = ROPED.index(what), PROJ.index(what)
                buf = (b.parity + r) % 2
                src = roped[buf][:].rearrange("p h (t a) d -> p h t a d", a=2)[:, :, :, 0, :]
                dve.wait_ge(proj_out, b.at(NPROJ, seq + 1))
                if b.turn is not None or b.c * NROPE + r >= 2:
                    dve.wait_ge(roped_done, b.at(NROPE, r - 1))
                nc.vector.tensor_tensor(rot_a[buf][:], src, rope_sb[:, 0][:, None].to_broadcast([P, 8, 2, 16]),
                                        ALU.mult)
                nc.vector.tensor_tensor(rot_b[buf][:], src, rope_sb[:, 1][:, None].to_broadcast([P, 8, 2, 16]),
                                        ALU.mult).then_inc(rot_done, 1)

            def self_step(b, u, more=True, more2=True):
                peaks(A, b, u)
                if b.after(1) or u >= 2:
                    take_weights(A, b, u, SELF_TURNS)
                    take_heads(A, b, u)
                inverse_sums(A, b, u)
                if u == 2 and b.after(1):
                    add_residual(A, C, b + -1)
                if more:
                    rotate(b + 1, ("k", "q1", "q2", "q3")[u])
                    if u == 0:
                        rotate(b + 1, "q0")
                if u == 2 and more2:
                    layernorm(A, b + 2)

            def self_batch(b, more=True, more2=True):
                for u in range(4):
                    self_step(b, u, more, more2)

            b0 = Batch(None, 0)
            for p in range(2):
                nc.vector.memset(k_bd[p][:], 0.0)
            nc.vector.memset(zero_sb[:], 0.0).then_inc(zeroed, 1)
            dve.wait_ge(ld_x0, 16)
            statistics(A, b0)
            statistics(A, b0 + 1)
            deviations(A, 0, 0, 2)
            layernorm(A, b0)
            layernorm(A, b0 + 1)
            dve.wait_ge(ld_const, 16 * 4)
            for what in ROPED:
                rotate(b0, what)
            dve.wait_ge(ld_x, 16)
            for b in range(2, NB):
                statistics(A, Batch(None, b))
            deviations(A, 1, 2, NB)
            self_batch(b0)
            self_batch(b0 + 1)
            loop(dve, self_batch, 2, NB - 2)
            self_batch(Batch(None, NB - 2), True, False)
            self_batch(Batch(None, NB - 1), False, False)
            end = Batch(None, NB)
            for u in range(2):
                take_weights(A, end, u, SELF_TURNS)
                take_heads(A, end, u)
            add_residual(A, C, end + -1)

            for t in range(4):
                v, e = t // 2, t % 2
                dve.wait_ge(f4_done, t + 1)
                nc.vector.tensor_copy(fold_n[:, 2 * t:2 * t + 2, :].rearrange("p a b -> p (a b)"),
                                      turn_ps[e][:]).then_inc(f4_out, 1)
                dve.wait_ge(f2_done, t + 1)
                if t >= 2:
                    dve.wait_ge(f3_done, t - 1)
                nc.vector.tensor_copy(fold_b2[e], proj_ps[e][:, 0:4 * HD]).then_inc(f2_out, 1)

            def cross_step(b, u, more=True, more2=True):
                peaks(C, b, u)
                if b.after(1):
                    take_weights(C, b, u, CROSS_TURNS)
                    take_heads(C, b, u)
                if u == 0 and b.after(2):
                    add_residual(C, F, b + -2)
                if u == 0 and more2:
                    layernorm(C, b + 2)
                inverse_sums(C, b, u)

            def cross_batch(b, more=True, more2=True):
                for u in range(2):
                    cross_step(b, u, more, more2)

            deviations(C, 2, 0, NB)
            layernorm(C, b0)
            layernorm(C, b0 + 1)
            cross_batch(b0)
            cross_batch(b0 + 1)
            loop(dve, cross_batch, 2, NB - 2)
            cross_batch(Batch(None, NB - 2), True, False)
            cross_batch(Batch(None, NB - 1), False, False)
            for u in range(2):
                take_weights(C, end, u, CROSS_TURNS)
                take_heads(C, end, u)
                if u == 0:
                    add_residual(C, F, end + -2)
            add_residual(C, F, end + -1)

            def router(b):
                p = b.parity
                k = [0]
                rs = (rms_rs[:, b.c:b.c + 1] if b.turn is None else
                      rms_rs[:, bass.ds(b.turn * 2 + b.c, 1)])

                def then(ins):
                    k[0] += 1
                    ins.then_inc(r_step, 1)
                    dve.wait_ge(r_step, b.at(RSTEPS, k[0]))

                dve.wait_ge(logit_done, b.at(1, 1))
                nc.vector.tensor_scalar(r_log[:], pv_ps[:, 0:8], rs, None, ALU.mult).then_inc(logit_read, 1)
                dve.wait_ge(logit_read, b.at(1, 1))
                then(nc.vector.reduce_max(r_max[:], r_log[:], AX.X))
                nc.vector.tensor_scalar(r_arg[:], r_log[:], r_max[:], None, ALU.subtract)\
                    .then_inc(r_arg_ready, 1)
                other = r_log[:, None, :].to_broadcast([P, 8, 8])
                own = r_log[:, :, None].to_broadcast([P, 8, 8])
                nc.vector.tensor_tensor(r_gt[:], other, own, ALU.is_gt)
                then(nc.vector.tensor_tensor(r_eq[:], other, own, ALU.is_equal))
                then(nc.vector.tensor_tensor(r_eq[:], r_eq[:], tri_sb[:], ALU.mult))
                then(nc.vector.tensor_tensor(r_gt[:], r_gt[:], r_eq[:], ALU.add))
                then(nc.vector.reduce_sum(r_rank[:], r_gt[:], AX.X))
                dve.wait_ge(r_exped, b.at(1, 1))
                then(nc.vector.scalar_tensor_tensor(out=r_sel[:], in0=r_rank[:], scalar=2.0, in1=r_exp[:],
                                                    op0=ALU.is_lt, op1=ALU.mult))
                then(nc.vector.reduce_sum(r_sum[:], r_sel[:], AX.X))
                then(nc.vector.reciprocal(r_inv[:], r_sum[:]))
                assert k[0] == RSTEPS
                nc.vector.tensor_scalar(r_cw[p][:], r_sel[:], r_inv[:], 2.0, ALU.mult, ALU.mult)\
                    .then_inc(r_ready, 1)

            def expert_act(b, half):
                dve.wait_ge(gate_tanh, b.at(2, half + 1))
                if b.after(1):
                    dve.wait_ge(hidden_ready, b.at(2, half - 1))
                nc.vector.scalar_tensor_tensor(out=gate_s[half], in0=gate_t[half], scalar=1.0,
                                               in1=score_ps[half][:], op0=ALU.add, op1=ALU.mult)\
                    .then_inc(silu_ready, 1)
                dve.wait_ge(silu_ready, b.at(2, half + 1))
                dve.wait_ge(up_done, b.at(2, half + 1))
                dve.wait_ge(r_ready, b.at(1, 1))
                if b.after(1):
                    dve.wait_ge(h_turned, b.at(2, half - 1))
                for e in range(4):
                    cols = slice(e * P, (e + 1) * P)
                    last = nc.vector.scalar_tensor_tensor(
                        out=hidden[half][:, cols], in0=gate_s[half][:, cols],
                        scalar=r_cw[b.parity][:, 4 * half + e:4 * half + e + 1],
                        in1=proj_ps[half][:, cols], op0=ALU.mult, op1=ALU.mult)
                last.then_inc(hidden_ready, 1)

            def take_hidden(b, half):
                dve.wait_ge(h_turned, b.at(2, half + 1))
                if b.after(1):
                    dve.wait_ge(down_done, b.at(2, half - 1))
                nc.vector.tensor_copy(hidden_t[half], turn_ps[half][:]).then_inc(h_t_ready, 1)

            def ffn_residual(b):
                dve.wait_ge(down_done, b.at(2, 2))
                nc.vector.tensor_tensor(x_of(b), y_ps[:, 0:D], x_of(b), ALU.add).then_inc(F.x_added, 1)

            def ffn_batch(b, more=True):
                router(b)
                if b.after(1):
                    take_hidden(b + -1, 1)
                    ffn_residual(b + -1)
                expert_act(b, 0)
                if more:
                    layernorm(F, b + 1)
                take_hidden(b, 0)
                expert_act(b, 1)

            dve.wait_ge(ld_ffn, 16 * 6)
            for c in range(DC):
                nc.vector.tensor_scalar(router_w[:, c, :], router_sb[:, c, :], norm_sb[:, c:c + 1], None,
                                        ALU.mult).then_inc(rw_ready, 1)
            deviations(F, 3, 0, NB)
            then(nc.vector.tensor_tensor(ln_var[:], ln_mv[:, :, 1], ln_rs[:], ALU.mult))
            then(nc.vector.tensor_tensor(ln_var[:], ln_var[:], ln_rs[:], ALU.mult))
            nc.vector.tensor_scalar(ln_var[:], ln_var[:], RMS_EPS, None, ALU.add).then_inc(var_ready, 1)
            dve.wait_ge(var_ready, 5)
            inverse_root(4, slice(0, NB), rms_rs)
            layernorm(F, b0)
            ffn_batch(b0)
            ffn_batch(b0 + 1)
            loop(dve, ffn_batch, 2, NB - 2)
            ffn_batch(Batch(None, NB - 2))
            ffn_batch(Batch(None, NB - 1), False)
            take_hidden(Batch(None, NB - 1), 1)
            ffn_residual(Batch(None, NB - 1))

        @block.scalar
        def _(act):
            def take_tokens(s, b, ps):
                act.wait_ge(s.ln_turned, b.at(1, 1))
                nc.scalar.activation(xn_t[b.parity][:].rearrange("p a b -> p (a b)"), ps, ACT.Copy)\
                    .then_inc(s.xn_t_ready, 1)

            def exponentials(s, b, u, between):
                buf = unit_buf(s, b, u)
                act.wait_ge(s.shift_ready, b.at(s.U, u + 1))
                if s.masked:
                    nc.scalar.activation(sink_exp[:, buf, :], sink_arg[:, buf, :], ACT.Exp)
                for h in range(8):
                    if h == 4:
                        between()
                    last = nc.scalar.activation(probs[buf][:, h, :], probs[buf][:, h, :], ACT.Exp,
                                                bias=neg_peak[:, buf, h:h + 1],
                                                accum_out=row_sum[:, buf, h:h + 1])
                last.then_inc(s.exped, 1)

            def take_weights(s, b, u, turns):
                act.wait_ge(s.p_turned, b.at(2 * s.U, 2 * (u - 2) + 2))
                if b.turn is not None or b.c * s.U + u - 3 >= 0:
                    act.wait_ge(s.pv_done, b.at(s.U, u - 2))
                nc.scalar.activation(probs_t[1][:], turn_bank(turns, "p1", u)[:], ACT.Copy)\
                    .then_inc(s.p_t1_ready, 1)

            def take_plain(b, seq):
                act.wait_ge(projected, b.at(NPROJ, seq + 1))
                what = PROJ[seq]
                if what == "v":
                    if b.after(2):
                        act.wait_ge(A.pv_done, b.at(4, -4))
                    nc.scalar.activation(v_n[b.parity][:].rearrange("p a b -> p (a b)"), proj_ps[seq % 2][:],
                                         ACT.Copy).then_inc(proj_out, 1)
                    return
                r = ROPED.index(what)
                if b.turn is not None or b.c * NROPE + r >= 2:
                    act.wait_ge(qk_turned, b.at(NROPE, r - 1))
                nc.scalar.activation(roped[(b.parity + r) % 2][:].rearrange("p a b c -> p (a b c)"),
                                     proj_ps[seq % 2][:], ACT.Copy, scale=1.0 if what == "k" else HD ** -0.5)\
                    .then_inc(proj_out, 1)

            def take_qk(b, what, u):
                r = ROPED.index(what)
                act.wait_ge(qk_turned, b.at(NROPE, r + 1))
                ps = turn_bank(SELF_TURNS, what, u)
                if what == "k":
                    if b.after(2):
                        act.wait_ge(A.scored, b.at(8, -8))
                    src = ps[:].rearrange("p (g k) -> p g k", g=4)
                    nc.scalar.activation(k_bd[b.parity][0:HD, :, 0, :], src[0:HD], ACT.Copy)
                    nc.scalar.activation(k_bd[b.parity][HD:P, :, 1, :], src[HD:P], ACT.Copy)\
                        .then_inc(k_ready, 1)
                else:
                    g = int(what[1])
                    if b.after(2):
                        act.wait_ge(A.scored, b.at(8, -16 + 2 * g + 2))
                    nc.scalar.activation(q_t[b.parity][:, g].rearrange("p a b -> p (a b)"), ps[:], ACT.Copy)\
                        .then_inc(q_ready, 1)

            def self_step(b, u, more=True, more2=True):
                def between():
                    if b.after(1) or u >= 2:
                        take_weights(A, b, u, SELF_TURNS)
                exponentials(A, b, u, between)
                if more:
                    take_plain(b + 1, (0, 2, 4, 5)[u])
                if u == 0:
                    take_qk(b, "q3", 0)
                elif more:
                    for what in ({1: ("k", "q0"), 2: ("q1",), 3: ("q2",)}[u]):
                        take_qk(b + 1, what, u)
                if more and u < 2:
                    take_plain(b + 1, (1, 3)[u])
                if u == 3 and more2:
                    act.wait_ge(projected, b.at(NPROJ, NPROJ))
                    take_tokens(A, b + 2, turn_bank(SELF_TURNS, "ln", 3)[:, 0:D])

            def self_batch(b, more=True, more2=True):
                for u in range(4):
                    self_step(b, u, more, more2)

            def roots(group, cols):
                act.wait_ge(var_ready, group + 1)
                nc.scalar.activation(ln_std[:, cols], ln_var[:, cols], ACT.Sqrt).then_inc(std_ready, 1)

            b0 = Batch(None, 0)
            roots(0, slice(0, 2))
            take_tokens(A, b0, turn_bank(SELF_TURNS, "ln", 3)[:, 0:D])
            act.wait_ge(zeroed, 1)
            take_plain(b0, 0)
            take_plain(b0, 1)
            take_qk(b0, "k", 1)
            take_plain(b0, 2)
            take_qk(b0, "q0", 1)
            take_plain(b0, 3)
            take_qk(b0, "q1", 2)
            take_plain(b0, 4)
            take_plain(b0, 5)
            take_qk(b0, "q2", 3)
            take_tokens(A, b0 + 1, turn_bank(SELF_TURNS, "ln", 3)[:, 0:D])
            roots(1, slice(2, NB))
            self_batch(b0)
            self_batch(b0 + 1)
            loop(act, self_batch, 2, NB - 2)
            self_batch(Batch(None, NB - 2), True, False)
            self_batch(Batch(None, NB - 1), False, False)
            end = Batch(None, NB)
            for u in range(2):
                take_weights(A, end, u, SELF_TURNS)

            for t in range(4):
                v, e = t // 2, t % 2
                act.wait_ge(f1_done, t + 1)
                if t >= 2:
                    act.wait_ge(f2_done, t - 1)
                nc.scalar.activation(fold_b1[e], score_ps[e][0:96, :], ACT.Copy).then_inc(f1_out, 1)
                act.wait_ge(f3_done, t + 1)
                for c in range(DC):
                    dst = fold_a[:, c, 4 * v:4 * v + 4, :].rearrange("p (a e) (j d) -> p e j a d", e=2, j=2)[:, e]
                    src = pv_ps[:, c * D:(c + 1) * D].rearrange("p (j a d) -> p j a d", j=2, a=2)
                    last = nc.scalar.activation(dst, src, ACT.Copy)
                last.then_inc(f3_out, 1)

            def take_latents(b):
                act.wait_ge(kv_turned, b.at(1, 1))
                if b.after(2):
                    act.wait_ge(C.scored, b.at(4, -4))
                ps = turn_bank(CROSS_TURNS, "kv", 0)
                nc.scalar.activation(k_bd[b.parity][0:HD, 0, 0, :], ps[0:HD, 0:P], ACT.Copy)
                nc.scalar.activation(k_bd[b.parity][HD:P, 0, 1, :], ps[HD:P, 0:P], ACT.Copy)\
                    .then_inc(kv_t_ready, 1)

            def take_queries(b, u):
                act.wait_ge(cq_done, b.at(2, u + 1))
                if b.after(2):
                    act.wait_ge(C.scored, b.at(4, -8 + 2 * u + 2))
                nc.scalar.activation(q_t[b.parity][:, u].rearrange("p a b -> p (a b)"), proj_ps[u][:], ACT.Copy)\
                    .then_inc(cq_ready, 1)

            def cross_step(b, u, more=True, more2=True):
                def between():
                    if b.after(1):
                        take_weights(C, b, u, CROSS_TURNS)
                exponentials(C, b, u, between)
                if more:
                    take_queries(b + 1, u)
                    if u == 0:
                        take_latents(b + 1)
                if u == 1 and more2:
                    act.wait_ge(cq_done, b.at(2, 2))
                    take_tokens(C, b + 2, turn_bank(CROSS_TURNS, "ln", 1)[:, 0:D])

            def cross_batch(b, more=True, more2=True):
                for u in range(2):
                    cross_step(b, u, more, more2)

            roots(2, slice(0, NB))
            take_tokens(C, b0, turn_bank(CROSS_TURNS, "ln", 1)[:, 0:D])
            take_latents(b0)
            take_queries(b0, 0)
            take_queries(b0, 1)
            take_tokens(C, b0 + 1, turn_bank(CROSS_TURNS, "ln", 1)[:, 0:D])
            cross_batch(b0)
            cross_batch(b0 + 1)
            loop(act, cross_batch, 2, NB - 2)
            cross_batch(Batch(None, NB - 2), True, False)
            cross_batch(Batch(None, NB - 1), False, False)
            for u in range(2):
                take_weights(C, end, u, CROSS_TURNS)

            def ffn_tokens(b):
                if b.after(2):
                    act.wait_ge(up_done, b.at(2, -2))
                take_tokens(F, b, pv_ps[:, P:3 * P])

            def gate_tanhs(b, half):
                act.wait_ge(gate_done, b.at(2, half + 1))
                if b.after(1):
                    act.wait_ge(silu_ready, b.at(2, half - 1))
                nc.scalar.activation(gate_t[half], score_ps[half][:], ACT.Tanh, scale=0.5)\
                    .then_inc(gate_tanh, 1)

            def ffn_batch(b, more=True):
                act.wait_ge(r_arg_ready, b.at(1, 1))
                if b.after(1):
                    act.wait_ge(r_ready, b.at(1, 0))
                nc.scalar.activation(r_exp[:], r_arg[:], ACT.Exp).then_inc(r_exped, 1)
                gate_tanhs(b, 0)
                gate_tanhs(b, 1)
                if more:
                    ffn_tokens(b + 1)

            act.wait_ge(C.x_added, NB)
            roots(3, slice(0, NB))
            roots(4, slice(0, NB))
            ffn_tokens(b0)
            ffn_batch(b0)
            ffn_batch(b0 + 1)
            loop(act, ffn_batch, 2, NB - 2)
            ffn_batch(Batch(None, NB - 2))
            ffn_batch(Batch(None, NB - 1), False)

        @block.gpsimd
        def _(pool):
            def normalise(s, b, u):
                buf = unit_buf(s, b, u)
                pool.wait_ge(s.inv_ready, b.at(s.U, u + 1))
                nc.gpsimd.tensor_tensor(probs[buf][:], probs[buf][:],
                                        inv_sum[:, buf, :][:, :, None].to_broadcast([P, 8, P]), ALU.mult)\
                    .then_inc(s.normed, 1)

            def add_rotated(b, what):
                r = ROPED.index(what)
                buf = (b.parity + r) % 2
                pool.wait_ge(rot_done, b.at(NROPE, r + 1))
                if b.turn is not None or b.c * NROPE + r >= 2:
                    pool.wait_ge(qk_turned, b.at(NROPE, r - 1))
                dst = roped[buf][:].rearrange("p h (t a) d -> p h t a d", a=2)[:, :, :, 0, :]
                for t in range(2):
                    last = nc.gpsimd.tensor_tensor(dst[:, :, t, :], rot_a[buf][:, :, t, :],
                                                   rot_b[buf][:, :, 1 - t, :], ALU.add)
                last.then_inc(roped_done, 1)

            def self_step(b, u, more=True):
                if b.after(1) or u:
                    normalise(A, b, u - 1)
                if more:
                    add_rotated(b + 1, ("k", "q1", "q2", "q3")[u])
                    if u == 0:
                        add_rotated(b + 1, "q0")

            def self_batch(b, more=True):
                for u in range(4):
                    self_step(b, u, more)

            b0 = Batch(None, 0)
            for what in ROPED:
                add_rotated(b0, what)
            self_batch(b0)
            self_batch(b0 + 1)
            loop(pool, self_batch, 2, NB - 2)
            self_batch(Batch(None, NB - 2))
            self_batch(Batch(None, NB - 1), False)
            end = Batch(None, NB)
            normalise(A, end, -1)

            pool.wait_ge(ld_ctx, 32)
            kv_v = kv_rope[:].rearrange("p (b d) -> p b d", d=HD)
            half = HD // 2
            wide = [P, NB, half]
            nc.gpsimd.tensor_tensor(kv_v, ctx_sb, rope_c_sb[:, 0][:, None].to_broadcast([P, NB, HD]),
                                    ALU.mult).then_inc(kv_part, 1)
            pool.wait_ge(kv_part, 1)
            nc.gpsimd.tensor_tensor(ctx_sb, ctx_sb, rope_c_sb[:, 1][:, None].to_broadcast([P, NB, HD]),
                                    ALU.mult).then_inc(kv_part, 1)
            pool.wait_ge(kv_part, 2)
            nc.gpsimd.tensor_tensor(kv_v[:, :, 0:half], kv_v[:, :, 0:half], ctx_sb[:, :, half:HD], ALU.add)
            nc.gpsimd.tensor_tensor(kv_v[:, :, half:HD], kv_v[:, :, half:HD], ctx_sb[:, :, 0:half], ALU.add)\
                .then_inc(kv_done, 1)

            def latents_of(b):
                if b.turn is None:
                    return kv_rope[:, b.c * HD:(b.c + 1) * HD]
                return kv_rope[:, bass.ds(b.turn * (2 * HD) + b.c * HD, HD)]

            def copy_keys(b):
                if b.after(2):
                    pool.wait_ge(kv_turned, b.at(1, -1))
                nc.gpsimd.tensor_copy(kv_dup[b.parity][:, 0, :], latents_of(b))
                nc.gpsimd.tensor_copy(kv_dup[b.parity][:, 1, :], latents_of(b)).then_inc(kv_copied, 1)

            def copy_values(b):
                if b.after(2):
                    pool.wait_ge(C.pv_done, b.at(2, -2))
                nc.gpsimd.tensor_copy(v_n[b.parity][:, 0, :], latents_of(b)).then_inc(v_copied, 1)

            def cross_step(b, u, more2=True):
                if b.after(1) or u:
                    normalise(C, b, u - 1)
                if u == 0:
                    copy_values(b)
                elif more2:
                    copy_keys(b + 2)

            def cross_batch(b, more2=True):
                for u in range(2):
                    cross_step(b, u, more2)

            pool.wait_ge(kv_done, 1)
            copy_keys(b0)
            copy_keys(b0 + 1)
            cross_batch(b0)
            cross_batch(b0 + 1)
            loop(pool, cross_batch, 2, NB - 2)
            cross_batch(Batch(None, NB - 2), False)
            cross_batch(Batch(None, NB - 1), False)
            normalise(C, end, -1)


def _rope_tables():
    inv = np.power(np.float32(1.0 / 1024.0), np.linspace(0.0, 1.0, 16, dtype=np.float32)).astype(np.float32)
    theta = (np.arange(P, dtype=np.float32)[:, None] * inv[None, :]).astype(np.float32)
    cos, sin = np.cos(theta.astype(np.float64)), np.sin(theta.astype(np.float64))
    rope = np.stack([np.stack([cos, cos], 1), np.stack([-sin, sin], 1)], 1)
    inv_c = (np.float32(1.0) / np.power(np.float32(10000.0), np.arange(0, HD, 2, dtype=np.float32)
                                        / np.float32(HD))).astype(np.float32)
    freqs = (np.arange(P, dtype=np.float32)[:, None] * inv_c[None, :]).astype(np.float32).astype(np.float64)
    sin_c, cos_c = np.repeat(np.sin(freqs), 2, -1), np.repeat(np.cos(freqs), 2, -1)
    signed = np.concatenate([sin_c[:, HD // 2:], -sin_c[:, :HD // 2]], -1)
    return (rope.astype(np.float32),
            np.stack([cos_c, signed], 1).astype(np.float32))


def _layouts(x, ctx_512, L0_attn_W_qkv, L0_attn_W_out, L0_attn_s, L0_xattn_Wq, L0_xattn_w_kc_q,
             L0_xattn_w_kc_kv, L0_xattn_W_qr, L0_xattn_W_kr, L0_xattn_Wo, L0_ffn_router_w,
             L0_ffn_norm_w, L0_ffn_gate_w, L0_ffn_up_w, L0_ffn_down_w):
    def rows(w):
        return w.reshape(-1, P, *w.shape[1:]).swapaxes(0, 1)

    wq = L0_attn_W_qkv[:, :2048].reshape(D, 4, 2, 4, HD).transpose(0, 1, 3, 2, 4).reshape(D, 4, 512)
    wk, wv = L0_attn_W_qkv[:, 2048:2560], L0_attn_W_qkv[:, 2560:3072]
    banks = np.stack([{"k": wk, "v": wv}.get(s) if s in "kv" else wq[:, int(s[1])] for s in PROJ], 1)
    wqkv = banks.reshape(DC, P, NPROJ, 512).transpose(1, 2, 0, 3)
    wout = L0_attn_W_out.reshape(4, 2, 4, HD, D).transpose(0, 2, 1, 3, 4).reshape(2048, D)
    sink = L0_attn_s.reshape(4, 2, 4).transpose(0, 2, 1).reshape(32)
    rope, rope_c = _rope_tables()
    pos = np.arange(P)
    q, k = pos[:, None], pos[None, :]
    mask = np.where((q >= k) & (q < k + 64), MASKED, 0.0).astype(np.float32)
    by_head = lambda w: w.transpose(2, 0, 1)
    pairs = lambda w: by_head(w).reshape(HD, 8, 2, -1).transpose(2, 0, 1, 3).reshape(P, 8, -1)
    wkcq = by_head(L0_xattn_w_kc_q).reshape(2, 96, 16, P).transpose(1, 0, 2, 3)
    experts = lambda w: rows(w.transpose(1, 0, 2).reshape(D, 1024))
    tri = np.broadcast_to((pos[None, :8] < pos[:8, None]).astype(np.float32), (P, 8, 8))
    return dict(
        x=x, ctx=ctx_512, wqkv=wqkv, wout=rows(wout), sink=sink, wqr_t=pairs(L0_xattn_W_qr),
        wkr_t=pairs(L0_xattn_W_kr), wkcq_t=wkcq, wq=rows(L0_xattn_Wq),
        wkckv=L0_xattn_w_kc_kv.transpose(1, 0, 2), wo_t=rows(L0_xattn_Wo.T),
        router=rows(L0_ffn_router_w.T), norm_w=rows(L0_ffn_norm_w), gate_w=experts(L0_ffn_gate_w),
        up_w=experts(L0_ffn_up_w), down_w=L0_ffn_down_w.transpose(1, 0, 2),
        ident=np.eye(P, dtype=np.float32), mask=mask, rope=rope, rope_c=rope_c,
        tri=tri)


def kernel(**inputs):
    import concourse.bacc as bacc
    from concourse.bass_utils import run_bass_kernel_spmd

    nc = bacc.Bacc("TRN2", target_bir_lowering=False, num_devices=1)
    arrays, args = {}, {}
    for name, a in _layouts(**{k: np.asarray(v) for k, v in inputs.items()}).items():
        a = np.ascontiguousarray(a)
        arrays[f"in_{name}"] = a
        args[name] = nc.dram_tensor(f"in_{name}", a.shape, mybir.dt.from_np(a.dtype), kind="ExternalInput").ap()
    args["out"] = nc.dram_tensor("out_y", (NB, P, D), F32, kind="ExternalOutput").ap()
    decoder_layer(nc, **args)
    return run_bass_kernel_spmd(nc, [arrays], core_ids=[0]).results[0]["out_y"]
```

```python
import numpy as np
import concourse.bass as bass
from concourse import mybir
from contextlib import ExitStack

F32 = mybir.dt.float32
ALU = mybir.AluOpType
ACT = mybir.ActivationFunctionType
AX = mybir.AxisListType

F32R = mybir.dt.float32r
P = 128
NB = 16
D = 256
DC = D // P
HD = 64
LN_EPS = 1e-5
RMS_EPS = 1e-6
MASKED = -3.0e38
NSTAGE = 3
SPLIT_OUT, SPLIT_FFN, NSPLIT = 6, 10, 16

PROJ = ["k", "q0", "q1", "q2", "q3", "v"]
ROPED = ["k", "q0", "q1", "q2", "q3"]
NPROJ, NROPE = len(PROJ), len(ROPED)
ROPE_BUF = {"k": 0, "q0": 1, "q1": 2, "q2": 0, "q3": 2}
ROPE_BEFORE = {"k": 3 - NROPE, "q0": 1 - NROPE, "q1": 4 - NROPE, "q2": 0, "q3": 2}


class Batch:

    def __init__(self, turn, c):
        self.turn, self.c = turn, c

    def __add__(self, k):
        return Batch(self.turn, self.c + k)

    def at(self, per, k):
        fixed = self.c * per + k
        return fixed if self.turn is None else self.turn * (2 * per) + fixed

    @property
    def parity(self):
        return self.c % 2

    def after(self, first):
        return self.turn is not None or self.c >= first


def decoder_layer(nc, x, ctx, wqkv, wout, sink, wqr_t, wkr_t, wkcq_t, wq, wkckv, wo_t, router, norm_w,
                  experts, ident, mask, rope, rope_c, tri, out):
    with ExitStack() as stack:
        def sb(name, shape, dt=F32):
            return stack.enter_context(nc.sbuf_tensor(name, shape, dt))

        def sem(name):
            return stack.enter_context(nc.semaphore(name))

        def bank(name):
            return stack.enter_context(nc.psum_tensor(name, [P, 512], F32))

        X = sb("X", [P, NB * D])
        stage = [sb(f"stage{i}", [P, 1024]) for i in range(NSTAGE)]
        big_w = [sb(f"big_w_{x}", [P, 6144], F32R) for x in ("hi", "lo")]
        wqkv_sb = [w[:].rearrange("p (s c n) -> p s c n", s=NPROJ, c=DC) for w in big_w]
        gate_sb = [w[:, 0:2048].rearrange("p (c n) -> p c n", c=DC) for w in big_w]
        up_sb = [w[:, 2048:4096].rearrange("p (c n) -> p c n", c=DC) for w in big_w]
        down_sb = [w[:, 4096:6144].rearrange("p (e n) -> p e n", e=8) for w in big_w]
        wout_sb = [sb(f"wout_{x}", [P, 16, D], F32R) for x in ("hi", "lo")]
        ctx_sb = stage[SPLIT_FFN % NSTAGE][:].rearrange("p (b d) -> p b d", b=NB)
        kv_rope = sb("kv_rope", [P, NB * HD])
        wqr_sb = sb("wqr_sb", [P, 8, 192])
        wkr_sb = sb("wkr_sb", [P, 8, HD])
        wkckv_sb = sb("wkckv_sb", [P, 16, HD])

        def over(name, shape, dt, host, skip):
            return nc.alloc_sbuf_tensor_at(name, shape, dt, offset=nc.lookup_mloc(host).addr + skip)

        KB16 = 16 * D * 4
        wkcq_sb = over("wkcq_sb", [96, 2, 16, P], F32, "big_w_hi", 0)
        wq_sb = over("wq_sb", [P, 16, D], F32, "big_w_hi", KB16)
        wo_sb = over("wo_sb", [P, 16, D], F32, "big_w_hi", 2 * KB16)
        fold_a = over("fold_a", [P, DC, 8, P], F32, "wout_hi", 0)
        fold_n = [over("fold_n_hi", [P, 8, D], F32R, "wout_hi", KB16 // 2),
                  over("fold_n_lo", [P, 8, D], F32R, "wout_lo", 0)]
        ident_sb = sb("ident_sb", [P, P])
        mask_sb = sb("mask_sb", [P, P])
        sink_sb = sb("sink_sb", [P, 32])
        rope_sb = sb("rope_sb", [P, 2, 2, 16])
        rope_c_sb = sb("rope_c_sb", [P, 2, HD])
        router_sb = sb("router_sb", [P, DC, 8])
        norm_sb = sb("norm_sb", [P, DC])
        router_f = sb("router_f", [P, DC, 8])
        router_w = [sb(f"router_w_{x}", [P, DC, 8], F32R) for x in ("hi", "lo")]
        tri_sb = sb("tri_sb", [P, 8, 8])

        xn = [sb(f"xn{i}", [P, D]) for i in range(2)]
        xn_t = [[sb(f"xn_t{i}_{x}", [P, DC, P], F32R) for x in ("hi", "lo")] for i in range(2)]
        xn_tf = [over(f"xn_tf{i}", [P, DC, P], F32, f"xn_t{i}_hi", 0) for i in range(2)]
        ln_st = sb("ln_st", [P, NB * 6])
        ln_mv = sb("ln_mv", [P, NB, 2])
        ln_var = sb("ln_var", [P, NB])
        ln_std = sb("ln_std", [P, NB])
        ln_tmp = sb("ln_tmp", [P, NB])
        ln_rs = sb("ln_rs", [P, NB])
        rms_rs = sb("rms_rs", [P, NB])
        q_t = [[sb(f"q_t{i}_{x}", [P, 4, P], F32R) for x in ("hi", "lo")] for i in range(2)]
        k_bd = [[sb(f"k_bd{i}_{x}", [P, 4, 2, P], F32R) for x in ("hi", "lo")] for i in range(2)]
        v_n = [sb(f"v_n{i}", [P, 8, HD]) for i in range(2)]
        roped = [sb(f"roped{i}", [P, 8, 4, 16]) for i in range(3)]
        rot_a = [sb(f"rot_a{i}", [P, 8, 2, 16]) for i in range(2)]
        rot_b = [sb(f"rot_b{i}", [P, 8, 2, 16]) for i in range(2)]
        probs = [sb(f"probs{i}", [P, 8, P]) for i in range(4)]
        gate_keeper = sb("gate_keeper", [P, 8])
        peak = sb("peak", [P, 4, 8])
        neg_peak = sb("neg_peak", [P, 4, 8])
        sink_arg = sb("sink_arg", [P, 4, 8])
        sink_exp = sb("sink_exp", [P, 4, 8])
        row_sum = sb("row_sum", [P, 4, 8])
        denom = sb("denom", [P, 4, 8])
        inv_sum = sb("inv_sum", [P, 4, 8])
        probs_t = [sb(f"probs_t{j}", [P, 512]) for j in range(2)]
        head_out = [[sb(f"head_out{i}_{x}", [P, 4, P], F32R) for x in ("hi", "lo")] for i in range(2)]
        kv_dup = [over(f"kv_dup{i}", [P, 2, HD], F32, f"rot_b{i}", 0) for i in range(2)]
        fold_b1 = [roped[i][0:96].rearrange("p a b c -> p (a b c)") for i in range(2)]
        fold_b2 = [rot_a[i][:].rearrange("p a b c -> p (a b c)") for i in range(2)]
        gate_t = [probs[i][:].rearrange("p a b -> p (a b)")[:, 0:512] for i in range(2)]
        gate_s = [probs[i][:].rearrange("p a b -> p (a b)")[:, 512:1024] for i in range(2)]
        hidden = [probs[2 + i][:].rearrange("p a b -> p (a b)")[:, 0:512] for i in range(2)]
        hidden_t = head_out
        r_log = sb("r_log", [P, 8])
        r_max = sb("r_max", [P, 1])
        r_arg = sb("r_arg", [P, 8])
        r_exp = sb("r_exp", [P, 8])
        r_gt = sb("r_gt", [P, 8, 8])
        r_eq = sb("r_eq", [P, 8, 8])
        r_rank = sb("r_rank", [P, 8])
        r_sel = sb("r_sel", [P, 8])
        r_sum = sb("r_sum", [P, 1])
        r_inv = sb("r_inv", [P, 1])
        r_cw = [sb(f"r_cw{i}", [P, 8]) for i in range(2)]

        proj_ps = [bank("proj_ps0"), bank("proj_ps1")]
        score_ps = [bank("score_ps0"), bank("score_ps1")]
        turn_ps = [bank("turn_ps0"), bank("turn_ps1")]
        pv_ps = bank("pv_ps")
        y_ps = bank("y_ps")

        ld_const, ld_x0, ld_x = sem("ld_const"), sem("ld_x0"), sem("ld_x")
        ld_stage = [sem(f"ld_stage{i}") for i in range(NSTAGE)]
        ld_fold, ld_small, ld_ffn = sem("ld_fold"), sem("ld_small"), sem("ld_ffn")
        w_hi, w_lo = sem("w_hi"), sem("w_lo")
        stored = sem("stored")
        zeroed = sem("zeroed")
        kv_part, kv_done = sem("kv_part"), sem("kv_done")

        class Sems:

            def __init__(self, name, units, masked):
                self.U, self.masked = units, masked
                s = lambda what: sem(f"{name}_{what}")
                self.stats = s("stats")
                self.xn_ready = s("xn_ready")
                self.ln_turned = s("ln_turned")
                self.xn_t_hi = s("xn_t_hi")
                self.xn_t_ready = s("xn_t_ready")
                self.x_added = s("x_added")
                if units:
                    self.scored = s("scored")
                    self.peaked = s("peaked")
                    self.shift_ready = s("shift_ready")
                    self.exped = s("exped")
                    self.summed = s("summed")
                    self.inv_ready = s("inv_ready")
                    self.normed = s("normed")
                    self.p_turned = s("p_turned")
                    self.p_t0_ready = s("p_t0_ready")
                    self.p_t1_ready = s("p_t1_ready")
                    self.pv_done = s("pv_done")
                    self.o_hi = s("o_hi")
                    self.o_ready = s("o_ready")
                    self.o_used = s("o_used")

        A = Sems("self", 4, True)
        C = Sems("cross", 2, False)
        F = Sems("ffn", 0, False)
        projected = sem("self_projected")
        proj_out = sem("self_proj_out")
        rot_done = sem("self_rot_done")
        roped_done = sem("self_roped_done")
        qk_turned = sem("self_qk_turned")
        k_hi = sem("self_k_hi")
        q_hi = sem("self_q_hi")
        k_ready = sem("self_k_ready")
        q_ready = sem("self_q_ready")
        f1_done, f1_out = sem("fold_b1_done"), sem("fold_b1_out")
        f2_done, f2_out = sem("fold_b2_done"), sem("fold_b2_out")
        f3_done, f3_out = sem("fold_a_done"), sem("fold_a_out")
        f4_done, f4_hi, f4_out = sem("fold_n_done"), sem("fold_n_hi"), sem("fold_n_out")
        kv_copied = sem("cross_kv_copied")
        v_copied = sem("cross_v_copied")
        kv_turned = sem("cross_kv_turned")
        kv_t_hi = sem("cross_kv_t_hi")
        kv_t_ready = sem("cross_kv_t_ready")
        cq_done = sem("cross_cq_done")
        cq_hi = sem("cross_cq_hi")
        cq_ready = sem("cross_cq_ready")
        logit_done = sem("ffn_logit_done")
        logit_read = sem("ffn_logit_read")
        norm_step = sem("norm_step")
        var_ready = sem("var_ready")
        std_ready = sem("std_ready")
        r_step = sem("ffn_router_step")
        r_arg_ready = sem("ffn_arg_ready")
        r_exped = sem("ffn_r_exped")
        gate_done = sem("ffn_gate_done")
        up_done = sem("ffn_up_done")
        gate_tanh = sem("ffn_gate_tanh")
        silu_ready = sem("ffn_silu_ready")
        hidden_ready = sem("ffn_hidden_ready")
        h_turned = sem("ffn_h_turned")
        h_t_hi = sem("ffn_h_t_hi")
        h_t_ready = sem("ffn_h_t_ready")
        down_done = sem("ffn_down_done")
        r_ready = sem("ffn_r_ready")
        rw_ready = sem("ffn_rw_ready")
        RSTEPS = 8

        def flat(t):
            return t[:].rearrange("p a b -> p (a b)")

        def split_place(k):
            if SPLIT_OUT <= k < SPLIT_FFN:
                return [flat(w)[:, (k - SPLIT_OUT) * 1024:(k - SPLIT_OUT + 1) * 1024] for w in wout_sb]
            k = k if k < SPLIT_OUT else k - SPLIT_FFN
            return [w[:, k * 1024:(k + 1) * 1024] for w in big_w]

        def staged(k):
            return k if k < SPLIT_FFN else k + 1

        def wait_staged(eng, n):
            eng.wait_ge(ld_stage[n % NSTAGE], 16 * (n // NSTAGE + 1))

        def x_of(b):
            if b.turn is None:
                return X[:, b.c * D:(b.c + 1) * D]
            return X[:, bass.ds(b.turn * (2 * D) + b.c * D, D)]

        def loop(eng, body, first, last):
            with eng.Fori(first // 2, last // 2) as turn:
                for c in range(2):
                    body(Batch(turn, c))

        SELF_TURNS = [("q1", 0), ("ln", 0), ("p0", 0), ("p1", 0),
                      ("q2", 1), ("p0", 1), ("p1", 1),
                      ("q3", 2), ("p0", 2), ("p1", 2),
                      ("k", 3), ("q0", 3), ("p0", 3), ("p1", 3)]
        CROSS_TURNS = [("kv", 0), ("p0", 0), ("p1", 0), ("ln", 1), ("p0", 1), ("p1", 1)]

        def turn_bank(turns, kind, u):
            return turn_ps[turns.index((kind, u)) % 2]

        def wait_turn_bank(eng, s, turns, b, kind, u, exists):
            i = turns.index((kind, u))
            while True:
                i -= 2
                if i < 0:
                    i += len(turns)
                    b = b + -1
                k, w = turns[i]
                if b.turn is None and not exists(b.c, k, w):
                    if b.c < -1:
                        return
                    continue
                break
            if k == "p0":
                eng.wait_ge(s.p_t0_ready, b.at(s.U, w - 2 + 1))
            elif k == "p1":
                eng.wait_ge(s.p_t1_ready, b.at(s.U, w - 2 + 1))
            elif k == "ln":
                eng.wait_ge(s.xn_t_ready, b.at(1, 2 if s is A else 3))
            elif k == "kv":
                eng.wait_ge(kv_t_ready, b.at(1, 2))
            elif k == "k":
                eng.wait_ge(k_ready, b.at(1, 2))
            elif k == "q0":
                eng.wait_ge(q_ready, b.at(4, 4 + 1))
            else:
                eng.wait_ge(q_ready, b.at(4, int(k[1]) + 1))

        def self_exists(c, kind, u):
            if kind in ("p0", "p1"):
                return 4 * c + u - 2 >= 0
            if kind in ("q1", "q2", "q3"):
                return 0 <= c < NB
            return 0 <= c + 1 < NB

        def cross_exists(c, kind, u):
            if kind in ("p0", "p1"):
                return 2 * c + u - 2 >= 0
            return 0 <= c + (2 if kind == "ln" else 1) < NB

        def self_inputs(b, u, more):
            own, next_ = lambda *what: [(b, w) for w in what], lambda *what: [(b + 1, w) for w in what if more]
            return [(own("q3", "v"), own("q2"), own("q1")),
                    (next_("k", "q0"), own("q3"), own("q2")),
                    (next_("q1"), next_("k", "q0"), own("q3")),
                    (next_("q2"), next_("q1"), next_("k", "q0"))][u]

        def step_before(s, b, u):
            return (b, u - 1) if u else (b + -1, s.U - 1)

        def unit_buf(s, b, u):
            return (u if s.U == 4 else 2 * b.parity + u) % 4

        block = stack.enter_context(nc.Block())

        @block.sync
        def _(sp):
            def load_chunk(k, src):
                n = staged(k)
                if n - NSTAGE == SPLIT_FFN:
                    sp.wait_ge(kv_done, 1)
                elif n >= NSTAGE:
                    before = n - NSTAGE if n - NSTAGE < SPLIT_FFN else n - NSTAGE - 1
                    sp.wait_ge(w_lo, before + 1)
                sp.dma_start(stage[n % NSTAGE][:], src).then_inc(ld_stage[n % NSTAGE], 16)

            x_v = x.rearrange("b s d -> s b d")
            X_v = X[:].rearrange("p (b d) -> p b d", d=D)
            sp.dma_start(X_v[:, 0:2], x_v[:, 0:2]).then_inc(ld_x0, 16)
            load_chunk(0, wqkv[:, 0])
            sp.dma_start(ident_sb[:], ident).then_inc(ld_const, 16)
            load_chunk(1, wqkv[:, 1])
            sp.dma_start(rope_sb[:], rope).then_inc(ld_const, 16)
            load_chunk(2, wqkv[:, 2])
            sp.dma_start(mask_sb[:], mask).then_inc(ld_const, 16)
            sp.dma_start(sink_sb[:], sink.partition_broadcast(P)).then_inc(ld_const, 16)
            for k in range(3, NPROJ):
                load_chunk(k, wqkv[:, k])
            for k in range(4):
                load_chunk(SPLIT_OUT + k, wout[:, k])
            sp.wait_ge(w_lo, SPLIT_FFN + 1 - NSTAGE)
            sp.dma_start(ctx_sb, ctx.rearrange("b l d -> l b d")).then_inc(ld_stage[SPLIT_FFN % NSTAGE], 16)
            sp.wait_ge(projected, NPROJ * NB)
            for dst, src in ((wkcq_sb, wkcq_t), (wq_sb, wq), (wo_sb, wo_t)):
                sp.dma_start(dst[:], src).then_inc(ld_fold, 16)
            for k in range(SPLIT_FFN, NSPLIT):
                load_chunk(k, experts[:, k - SPLIT_FFN])

            def store(b):
                sp.wait_ge(F.x_added, b.at(1, 1))
                if b.turn is None:
                    dst = out[b.c]
                else:
                    dst = out[bass.ds(b.turn * 2 + b.c, 1)].rearrange("a s d -> (a s) d")
                sp.dma_start(dst, x_of(b)).then_inc(stored, 16)

            loop(sp, store, 0, NB)
            sp.wait_ge(stored, 16 * NB)

        @block.tensor
        def _(pe):
            def turn(dst, src):
                return nc.tensor.transpose(dst, src, ident_sb[:])

            def product(ps, left, right, start, stop):
                nc.tensor.matmul(ps, left[0], right[0], start=start, stop=False)
                nc.tensor.matmul(ps, left[0], right[1], start=False, stop=False)
                return nc.tensor.matmul(ps, left[1], right[0], start=False, stop=stop)

            def layernorm_turn(s, b, ps):
                pe.wait_ge(s.xn_ready, b.at(1, 1))
                for c in range(DC):
                    last = turn(ps[:, c * P:(c + 1) * P], xn[b.parity][:, c * P:(c + 1) * P])
                last.then_inc(s.ln_turned, 1)

            def scores(s, b, u, queries, keys):
                for half in range(2):
                    if b.after(1) or u:
                        pe.wait_ge(s.peaked, b.at(2 * s.U, 2 * u - 1 + half))
                    for m in (2 * half, 2 * half + 1):
                        last = product(score_ps[half][:, (m % 2) * D:(m % 2 + 1) * D],
                                       [q[:, m, :] for q in queries], keys, True, True)
                    last.then_inc(s.scored, 1)

            def turn_weights(s, b, u, turns, exists):
                pe.wait_ge(s.normed, b.at(s.U, u - 2 + 1))
                for j in range(2):
                    wait_turn_bank(pe, s, turns, b, f"p{j}", u, exists)
                    ps = turn_bank(turns, f"p{j}", u)
                    for m in range(4):
                        last = turn(ps[:, m * P:(m + 1) * P], probs[unit_buf(s, b, u - 2)][:, 2 * m + j, :])
                    last.then_inc(s.p_turned, 1)

            def weigh_values(s, b, u, values):
                pe.wait_ge(s.p_t0_ready, b.at(s.U, u - 2))
                pe.wait_ge(s.p_t1_ready, b.at(s.U, u - 2))
                if b.turn is not None or b.c * s.U + u - 3 > 0:
                    pe.wait_ge(s.o_ready, b.at(s.U, u - 3))
                for j in range(2):
                    last = nc.tensor.matmul(pv_ps[j * HD:(j + 1) * HD, :], values(j), probs_t[j][:],
                                            start=True, stop=True)
                last.then_inc(s.pv_done, 1)

            def project_out(s, b, u, weights):
                first, w = (u - 3) % s.U == 0, (u - 3) % s.U
                pe.wait_ge(s.o_ready, b.at(s.U, u - 2))
                if first:
                    done = (u - 3) // s.U
                    if b.c + done > 0 or b.turn is not None:
                        pe.wait_ge(s.x_added, b.at(1, done))
                for m in range(4):
                    last = product(y_ps[:, 0:D], [o[:, m, :] for o in head_out[(u - 3) % 2]],
                                   [x[:, 4 * w + m, :] for x in weights], first and m == 0,
                                   w == s.U - 1 and m == 3)
                last.then_inc(s.o_used, 1)

            def project(b, seq, wait_load=False):
                if seq == 0:
                    pe.wait_ge(A.xn_t_ready, b.at(1, 1))
                if wait_load:
                    pe.wait_ge(w_lo, seq + 1)
                if b.after(1) or seq >= 2:
                    pe.wait_ge(proj_out, b.at(NPROJ, seq - 1))
                for c in range(DC):
                    last = product(proj_ps[seq % 2][:], [t[:, c, :] for t in xn_t[b.parity]],
                                   [w[:, seq, c, :] for w in wqkv_sb], c == 0, c == DC - 1)
                last.then_inc(projected, 1)

            def turn_qk(b, what, step_b, u):
                r = ROPED.index(what)
                pe.wait_ge(roped_done, b.at(NROPE, r + 1))
                wait_turn_bank(pe, A, SELF_TURNS, step_b, what, u, self_exists)
                ps = turn_bank(SELF_TURNS, what, u)
                src = roped[ROPE_BUF[what]][:].rearrange("p a b c -> p (a b c)")
                for m in range(4):
                    last = turn(ps[:, m * P:(m + 1) * P], src[:, m * P:(m + 1) * P])
                last.then_inc(qk_turned, 1)

            def weigh_self(b, u):
                vb, w = (b, 0) if u == 3 else (b + -1, u + 1)
                weigh_values(A, b, u, lambda j: v_n[vb.parity][:, 2 * w + j, :])

            def self_step(b, u, more=True, more2=True):
                pe.wait_ge(q_ready, b.at(4, u + 1))
                if u == 0:
                    pe.wait_ge(k_ready, b.at(1, 1))
                scores(A, b, u, q_t[u % 2], [k[:, u].rearrange("p j k -> p (j k)") for k in k_bd[b.parity]])
                made, _, turned = self_inputs(b, u, more)
                first = b.turn is None and b.c == 0 and u == 0
                for tb, what in turned:
                    turn_qk(tb, what, b, u)
                if u == 0 and more:
                    wait_turn_bank(pe, A, SELF_TURNS, b, "ln", 0, self_exists)
                    layernorm_turn(A, b + 1, turn_bank(SELF_TURNS, "ln", 0))
                if b.after(1) or u >= 3:
                    weigh_self(b, u)
                for mb, what in made[:1]:
                    project(mb, PROJ.index(what), first)
                if b.after(1) or u >= 2:
                    turn_weights(A, b, u, SELF_TURNS, self_exists)
                for mb, what in made[1:]:
                    project(mb, PROJ.index(what), first)
                if b.after(1) or u >= 3:
                    if b.turn is None and b.c == 0:
                        pe.wait_ge(w_lo, SPLIT_FFN)
                    project_out(A, b, u, wout_sb)

            def self_batch(b, more=True, more2=True):
                for u in range(4):
                    self_step(b, u, more, more2)

            b0, before = Batch(None, 0), Batch(None, -1)
            pe.wait_ge(ld_const, 16 * 4)
            layernorm_turn(A, b0, turn_bank(SELF_TURNS, "ln", 0))
            project(b0, 0, True)
            project(b0, 1, True)
            turn_qk(b0, "k", before, 3)
            project(b0, 2, True)
            turn_qk(b0, "q0", before, 3)
            project(b0, 3, True)
            pe.wait_ge(zeroed, 1)
            self_batch(b0)
            self_batch(b0 + 1)
            loop(pe, self_batch, 2, NB - 2)
            self_batch(Batch(None, NB - 2), True, False)
            self_batch(Batch(None, NB - 1), False, False)
            end = Batch(None, NB)
            for u in range(3):
                weigh_self(end, u)
                if u < 2:
                    turn_weights(A, end, u, SELF_TURNS, self_exists)
                project_out(A, end, u, wout_sb)

            pe.wait_ge(ld_small, 16 * 4)
            pe.wait_ge(ld_fold, 16 * 3)
            pe.wait_ge(A.p_t0_ready, 4 * NB)
            pe.wait_ge(A.p_t1_ready, 4 * NB)
            pe.wait_ge(A.o_ready, 4 * NB)
            for t in range(4):
                v, e = t // 2, t % 2
                heads = [8 * v + e + 2 * i for i in range(4)]
                if t >= 2:
                    pe.wait_ge(f1_out, t - 1)
                for i, h in enumerate(heads):
                    rows = slice(e * HD, (e + 1) * HD)
                    for c in range(2):
                        last = nc.tensor.matmul(score_ps[e][0:96, (2 * i + c) * HD:(2 * i + c + 1) * HD],
                                                wqr_sb[rows, h // 2, c * 96:(c + 1) * 96],
                                                wkr_sb[rows, h // 2, :], start=True, stop=True)
                last.then_inc(f1_done, 1)
                if t >= 2:
                    pe.wait_ge(f4_out, t - 1)
                for i in range(2):
                    m = 2 * e + i
                    for j in range(2):
                        h = 8 * v + 4 * j + m
                        last = nc.tensor.matmul(turn_ps[e][j * HD:(j + 1) * HD, i * D:(i + 1) * D],
                                                wkckv_sb[:, h, :], wo_sb[:, h, :], start=True, stop=True)
                last.then_inc(f4_done, 1)
                pe.wait_ge(f1_out, t + 1)
                if t >= 2:
                    pe.wait_ge(f2_out, t - 1)
                for i, h in enumerate(heads):
                    for c in range(2):
                        last = nc.tensor.matmul(proj_ps[e][:, i * HD:(i + 1) * HD], wkcq_sb[:, c, h, :],
                                                fold_b1[e][:, (2 * i + c) * HD:(2 * i + c + 1) * HD],
                                                start=(c == 0), stop=(c == 1))
                last.then_inc(f2_done, 1)
                pe.wait_ge(f2_out, t + 1)
                if t >= 1:
                    pe.wait_ge(f3_out, t)
                for c in range(DC):
                    for i, h in enumerate(heads):
                        last = nc.tensor.matmul(pv_ps[:, (4 * c + i) * HD:(4 * c + i + 1) * HD],
                                                wq_sb[:, h, c * P:(c + 1) * P],
                                                fold_b2[e][:, i * HD:(i + 1) * HD], start=True, stop=True)
                last.then_inc(f3_done, 1)

            def latent_queries(b, u):
                if u == 0:
                    pe.wait_ge(C.xn_t_ready, b.at(1, 1))
                if b.after(1):
                    pe.wait_ge(cq_ready, b.at(2, u - 1))
                for m in range(4):
                    for c in range(DC):
                        last = nc.tensor.matmul(proj_ps[u][:, m * P:(m + 1) * P],
                                                fold_a[:, c, 4 * u + m, :], xn_tf[b.parity][:, c, :],
                                                start=(c == 0), stop=(c == DC - 1))
                last.then_inc(cq_done, 1)

            def turn_latents(b, step_b):
                pe.wait_ge(kv_copied, b.at(1, 1))
                wait_turn_bank(pe, C, CROSS_TURNS, step_b, "kv", 0, cross_exists)
                turn(turn_bank(CROSS_TURNS, "kv", 0)[:, 0:P],
                     kv_dup[b.parity][:].rearrange("p a b -> p (a b)")).then_inc(kv_turned, 1)

            def weigh_cross(b, u):
                vb = b + (-1 if u else -2)
                pe.wait_ge(v_copied, vb.at(1, 1))
                weigh_values(C, b, u, lambda j: v_n[vb.parity][:, 0, :])

            def cross_step(b, u, more=True, more2=True):
                pe.wait_ge(cq_ready, b.at(2, u + 1))
                if u == 0:
                    pe.wait_ge(kv_t_ready, b.at(1, 1))
                scores(C, b, u, q_t[u], [k[:, 0].rearrange("p j k -> p (j k)") for k in k_bd[b.parity]])
                if u == 0 and more:
                    turn_latents(b + 1, b)
                if u == 1 and more2:
                    wait_turn_bank(pe, C, CROSS_TURNS, b, "ln", 1, cross_exists)
                    layernorm_turn(C, b + 2, turn_bank(CROSS_TURNS, "ln", 1))
                ahead = b.after(2) or (b.after(1) and u >= 1)
                if ahead:
                    weigh_cross(b, u)
                if more:
                    latent_queries(b + 1, u)
                if b.after(1):
                    turn_weights(C, b, u, CROSS_TURNS, cross_exists)
                if ahead:
                    project_out(C, b, u, fold_n)

            def cross_batch(b, more=True, more2=True):
                for u in range(2):
                    cross_step(b, u, more, more2)

            pe.wait_ge(f4_out, 4)
            layernorm_turn(C, b0, turn_bank(CROSS_TURNS, "ln", 1))
            turn_latents(b0, before)
            pe.wait_ge(f3_out, 4)
            latent_queries(b0, 0)
            latent_queries(b0, 1)
            wait_turn_bank(pe, C, CROSS_TURNS, before, "ln", 1, cross_exists)
            layernorm_turn(C, b0 + 1, turn_bank(CROSS_TURNS, "ln", 1))
            cross_batch(b0)
            cross_batch(b0 + 1)
            loop(pe, cross_batch, 2, NB - 2)
            cross_batch(Batch(None, NB - 2), True, False)
            cross_batch(Batch(None, NB - 1), False, False)
            for u in range(2):
                weigh_cross(end, u)
                turn_weights(C, end, u, CROSS_TURNS, cross_exists)
                project_out(C, end, u, fold_n)
            weigh_cross(end + 1, 0)
            project_out(C, end + 1, 0, fold_n)

            def ffn_turn(b):
                if b.after(1):
                    pe.wait_ge(logit_read, b.at(1, 0))
                layernorm_turn(F, b, pv_ps[:, P:3 * P])

            def experts_in(b, half):
                cols = slice(half * 512, (half + 1) * 512)
                if b.after(1):
                    pe.wait_ge(silu_ready, b.at(2, half - 1))
                for c in range(DC):
                    last = product(score_ps[half][:], [t[:, c, :] for t in xn_t[b.parity]],
                                   [w[:, c, cols] for w in gate_sb], c == 0, c == DC - 1)
                last.then_inc(gate_done, 1)
                if b.after(1):
                    pe.wait_ge(hidden_ready, b.at(2, half - 1))
                for c in range(DC):
                    last = product(proj_ps[half][:], [t[:, c, :] for t in xn_t[b.parity]],
                                   [w[:, c, cols] for w in up_sb], c == 0, c == DC - 1)
                last.then_inc(up_done, 1)

            def turn_hidden(b, half):
                pe.wait_ge(hidden_ready, b.at(2, half + 1))
                if b.after(1):
                    pe.wait_ge(h_t_ready, b.at(2, half - 1))
                for e in range(4):
                    last = turn(turn_ps[half][:, e * P:(e + 1) * P], hidden[half][:, e * P:(e + 1) * P])
                last.then_inc(h_turned, 1)

            def experts_out(b, half):
                pe.wait_ge(h_t_ready, b.at(2, half + 1))
                if half == 0 and b.after(1):
                    pe.wait_ge(F.x_added, b.at(1, 0))
                for e in range(4):
                    last = product(y_ps[:, 0:D], [t[:, e, :] for t in hidden_t[half]],
                                   [w[:, 4 * half + e, :] for w in down_sb], half == 0 and e == 0,
                                   half == 1 and e == 3)
                last.then_inc(down_done, 1)

            def ffn_batch(b, more=True):
                pe.wait_ge(F.xn_t_ready, b.at(1, 1))
                for c in range(DC):
                    last = product(pv_ps[:, 0:8], [t[:, c, :] for t in xn_t[b.parity]],
                                   [w[:, c, :] for w in router_w], c == 0, c == DC - 1)
                last.then_inc(logit_done, 1)
                experts_in(b, 0)
                if b.after(1):
                    turn_hidden(b + -1, 1)
                    experts_out(b + -1, 0)
                if more:
                    ffn_turn(b + 1)
                experts_in(b, 1)
                turn_hidden(b, 0)
                if b.after(1):
                    experts_out(b + -1, 1)

            pe.wait_ge(C.x_added, NB)
            pe.wait_ge(rw_ready, 4)
            pe.wait_ge(w_lo, NSPLIT)
            ffn_turn(b0)
            ffn_batch(b0)
            ffn_batch(b0 + 1)
            loop(pe, ffn_batch, 2, NB - 2)
            ffn_batch(Batch(None, NB - 2))
            ffn_batch(Batch(None, NB - 1), False)
            turn_hidden(Batch(None, NB - 1), 1)
            experts_out(Batch(None, NB - 1), 0)
            experts_out(Batch(None, NB - 1), 1)

        @block.vector
        def _(dve):
            steps = [0]

            def then(ins):
                steps[0] += 1
                ins.then_inc(norm_step, 1)
                dve.wait_ge(norm_step, steps[0])

            def statistics(s, b):
                dst = (ln_st[:, b.c * 6:(b.c + 1) * 6] if b.turn is None else
                       ln_st[:, bass.ds(b.turn * 12 + b.c * 6, 6)])
                nc.vector.bn_stats(dst, x_of(b)).then_inc(s.stats, 1)

            def inverse_root(group, cols, dst):
                steps[0] += 1
                nc.vector.tensor_copy(ln_tmp[:, cols], ln_var[:, cols]).then_inc(norm_step, 1)
                dve.wait_ge(std_ready, group + 1)
                then(nc.vector.reciprocal(dst[:, cols], ln_std[:, cols]))
                then(nc.vector.tensor_tensor(ln_tmp[:, cols], ln_tmp[:, cols], dst[:, cols], ALU.mult))
                then(nc.vector.tensor_tensor(ln_tmp[:, cols], ln_tmp[:, cols], dst[:, cols], ALU.mult))
                then(nc.vector.tensor_scalar(ln_tmp[:, cols], ln_tmp[:, cols], -0.5, 1.5, ALU.mult, ALU.add))
                then(nc.vector.tensor_tensor(dst[:, cols], dst[:, cols], ln_tmp[:, cols], ALU.mult))

            def deviations(s, group, first, last):
                dve.wait_ge(s.stats, last)
                for b in range(first, last):
                    ins = nc.vector.bn_aggr(ln_mv[:, b, :], ln_st[:, b * 6:(b + 1) * 6])
                then(ins)
                cols = slice(first, last)
                nc.vector.tensor_scalar(ln_var[:, cols], ln_mv[:, cols, 1], LN_EPS, None, ALU.add)\
                    .then_inc(var_ready, 1)
                dve.wait_ge(var_ready, group + 1)
                inverse_root(group, cols, ln_rs)

            def layernorm(s, b):
                p = b.parity
                if b.turn is None:
                    mean, rs = ln_mv[:, b.c, 0:1], ln_rs[:, b.c:b.c + 1]
                else:
                    mean = ln_mv[:].rearrange("p b k -> p (b k)")[:, bass.ds(b.turn * 4 + b.c * 2, 1)]
                    rs = ln_rs[:, bass.ds(b.turn * 2 + b.c, 1)]
                if b.after(2):
                    dve.wait_ge(s.ln_turned, b.at(1, -1))
                nc.vector.tensor_scalar(xn[p][:], x_of(b), mean, rs, ALU.subtract, ALU.mult)\
                    .then_inc(s.xn_ready, 1)

            def peaks(s, b, u, between):
                buf = unit_buf(s, b, u)
                if b.after(1 if s.U == 4 else 2):
                    dve.wait_ge(s.p_turned, b.at(2 * s.U, 2 * (u - 3)))
                for half in range(2):
                    dve.wait_ge(s.scored, b.at(2 * s.U, 2 * u + half + 1))
                    nc.vector.memset(gate_keeper[:, 2 * buf + half:2 * buf + half + 1], 0.0)
                    for i in range(4):
                        h = 4 * half + i
                        start = sink_sb[:, 8 * u + h:8 * u + h + 1] if s.masked else MASKED
                        last = nc.vector.tensor_tensor_reduce(
                            out=probs[buf][:, h, :], in0=score_ps[half][:, i * P:(i + 1) * P],
                            in1=mask_sb[:], scale=1.0, scalar=start,
                            op0=ALU.add, op1=ALU.max, accum_out=peak[:, buf, h:h + 1])
                    last.then_inc(s.peaked, 1)
                    cols = slice(4 * half, 4 * half + 4)
                    dve.wait_ge(s.peaked, b.at(2 * s.U, 2 * u + half + 1))
                    last = nc.vector.tensor_scalar(neg_peak[:, buf, cols], peak[:, buf, cols], -1.0, None,
                                                   ALU.mult)
                    if s.masked:
                        last = nc.vector.tensor_tensor(
                            sink_arg[:, buf, cols], sink_sb[:, 8 * u + 4 * half:8 * u + 4 * half + 4],
                            peak[:, buf, cols], ALU.subtract)
                    last.then_inc(s.shift_ready, 1)
                    if half == 0:
                        between()

            def inverse_sums(s, b, u):
                buf = unit_buf(s, b, u)
                dve.wait_ge(s.exped, b.at(s.U, u + 1))
                if s.masked:
                    nc.vector.tensor_tensor(denom[:, buf, :], row_sum[:, buf, :], sink_exp[:, buf, :],
                                            ALU.add).then_inc(s.summed, 1)
                    dve.wait_ge(s.summed, b.at(s.U, u + 1))
                nc.vector.reciprocal(inv_sum[:, buf, :], (denom if s.masked else row_sum)[:, buf, :])\
                    .then_inc(s.inv_ready, 1)

            def take_weights(s, b, u, turns):
                dve.wait_ge(s.p_turned, b.at(2 * s.U, 2 * (u - 2) + 1))
                if b.turn is not None or b.c * s.U + u - 3 >= 0:
                    dve.wait_ge(s.pv_done, b.at(s.U, u - 2))
                nc.vector.tensor_copy(probs_t[0][:], turn_bank(turns, "p0", u)[:]).then_inc(s.p_t0_ready, 1)

            def low_half(dst, whole, hi):
                return nc.vector.tensor_tensor(dst, whole, hi.bitcast(F32), ALU.subtract)

            def split(k):
                dve.wait_ge(w_hi, k + 1)
                hi, lo = split_place(k)
                low_half(lo, stage[staged(k) % NSTAGE][:], hi).then_inc(w_lo, 1)

            def take_tokens(s, b, ps):
                dve.wait_ge(s.xn_t_hi, b.at(1, 1))
                hi, lo = xn_t[b.parity]
                low_half(flat(lo), ps, flat(hi)).then_inc(s.xn_t_ready, 1)

            def take_heads(s, b, u):
                dve.wait_ge(s.o_hi, b.at(s.U, u - 2))
                hi, lo = head_out[(u - 3) % 2]
                low_half(flat(lo), pv_ps[:], flat(hi)).then_inc(s.o_ready, 1)

            def add_residual(s, b):
                dve.wait_ge(s.o_used, b.at(s.U, s.U))
                nc.vector.tensor_tensor(x_of(b), y_ps[:, 0:D], x_of(b), ALU.add).then_inc(s.x_added, 1)

            def statistics_after(s, after, b):
                dve.wait_ge(s.x_added, b.at(1, 1))
                statistics(after, b)

            def rotate(b, what):
                r, seq = ROPED.index(what), PROJ.index(what)
                buf = (b.parity + r) % 2
                src = roped[ROPE_BUF[what]][:].rearrange("p h (t a) d -> p h t a d", a=2)[:, :, :, 0, :]
                dve.wait_ge(proj_out, b.at(NPROJ, seq + 1))
                if b.turn is not None or b.c * NROPE + r >= 2:
                    dve.wait_ge(roped_done, b.at(NROPE, r - 1))
                nc.vector.tensor_tensor(rot_a[buf][:], src, rope_sb[:, 0][:, None].to_broadcast([P, 8, 2, 16]),
                                        ALU.mult)
                nc.vector.tensor_tensor(rot_b[buf][:], src, rope_sb[:, 1][:, None].to_broadcast([P, 8, 2, 16]),
                                        ALU.mult).then_inc(rot_done, 1)

            def take_qk(b, what, u):
                ps = turn_bank(SELF_TURNS, what, u)
                if what == "k":
                    dve.wait_ge(k_hi, b.at(1, 1))
                    hi, lo = k_bd[b.parity]
                    src = ps[:].rearrange("p (g k) -> p g k", g=4)
                    low_half(lo[0:HD, :, 0, :], src[0:HD], hi[0:HD, :, 0, :])
                    low_half(lo[HD:P, :, 1, :], src[HD:P], hi[HD:P, :, 1, :]).then_inc(k_ready, 1)
                else:
                    g = int(what[1])
                    dve.wait_ge(q_hi, b.at(4, g + 1))
                    hi, lo = q_t[g % 2]
                    low_half(flat(lo), ps[:], flat(hi)).then_inc(q_ready, 1)

            def self_step(b, u, more=True, more2=True):
                _, rotated, turned = self_inputs(b, u, more)

                def low_halves():
                    for tb, what in turned:
                        take_qk(tb, what, u)
                    if u == 0 and more:
                        take_tokens(A, b + 1, turn_bank(SELF_TURNS, "ln", 0)[:, 0:D])

                peaks(A, b, u, low_halves)
                if u == 3 and b.after(1):
                    add_residual(A, b + -1)
                if b.after(1) or u >= 3:
                    take_heads(A, b, u)
                if b.after(1) or u >= 2:
                    take_weights(A, b, u, SELF_TURNS)
                for tb, what in rotated:
                    rotate(tb, what)
                if u == 0 and b.after(2):
                    statistics_after(A, C, b + -2)
                if u == 1 and more2:
                    layernorm(A, b + 2)
                if b.turn is None and b.c == 0 and u < 2:
                    for k in range(2):
                        split(SPLIT_OUT + 2 * u + k)
                inverse_sums(A, b, u)

            def self_batch(b, more=True, more2=True):
                for u in range(4):
                    self_step(b, u, more, more2)

            b0 = Batch(None, 0)
            for p in range(2):
                for k in k_bd[p]:
                    nc.vector.memset(k[:].bitcast(F32), 0.0)
            nc.vector.memset(gate_keeper[:], 0.0).then_inc(zeroed, 1)
            dve.wait_ge(ld_x0, 16)
            statistics(A, b0)
            statistics(A, b0 + 1)
            deviations(A, 0, 0, 2)
            layernorm(A, b0)
            layernorm(A, b0 + 1)
            split(0)
            take_tokens(A, b0, turn_bank(SELF_TURNS, "ln", 0)[:, 0:D])
            split(1)
            dve.wait_ge(ld_const, 16 * 4)
            split(2)
            rotate(b0, "k")
            split(3)
            rotate(b0, "q0")
            take_qk(b0, "k", 3)
            rotate(b0, "q1")
            take_qk(b0, "q0", 3)
            split(4)
            split(5)
            dve.wait_ge(ld_x, 16)
            for b in range(2, NB):
                statistics(A, Batch(None, b))
            deviations(A, 1, 2, NB)
            self_batch(b0)
            self_batch(b0 + 1)
            loop(dve, self_batch, 2, NB - 2)
            self_batch(Batch(None, NB - 2), True, False)
            self_batch(Batch(None, NB - 1), False, False)
            end = Batch(None, NB)
            for u in range(3):
                take_heads(A, end, u)
                if u < 2:
                    take_weights(A, end, u, SELF_TURNS)
                if u == 0:
                    statistics_after(A, C, end + -2)
            add_residual(A, end + -1)
            statistics_after(A, C, end + -1)

            for t in range(4):
                v, e = t // 2, t % 2
                dve.wait_ge(f4_hi, t + 1)
                hi, lo = [flat(n)[:, t * 512:(t + 1) * 512] for n in fold_n]
                low_half(lo, turn_ps[e][:], hi).then_inc(f4_out, 1)
                dve.wait_ge(f2_done, t + 1)
                if t >= 2:
                    dve.wait_ge(f3_done, t - 1)
                nc.vector.tensor_copy(fold_b2[e], proj_ps[e][:, 0:4 * HD]).then_inc(f2_out, 1)

            def take_queries(b, u):
                dve.wait_ge(cq_hi, b.at(2, u + 1))
                hi, lo = q_t[u]
                low_half(flat(lo), proj_ps[u][:], flat(hi)).then_inc(cq_ready, 1)

            def take_latents(b):
                dve.wait_ge(kv_t_hi, b.at(1, 1))
                hi, lo = k_bd[b.parity]
                ps = turn_bank(CROSS_TURNS, "kv", 0)
                low_half(lo[0:HD, 0, 0, :], ps[0:HD, 0:P], hi[0:HD, 0, 0, :])
                low_half(lo[HD:P, 0, 1, :], ps[HD:P, 0:P], hi[HD:P, 0, 1, :]).then_inc(kv_t_ready, 1)

            def cross_step(b, u, more=True, more2=True):
                def low_halves():
                    if u == 0:
                        if more:
                            take_latents(b + 1)
                        take_queries(b, 1)
                    elif more:
                        take_queries(b + 1, 0)

                peaks(C, b, u, low_halves)
                if u == 1 and b.after(2):
                    add_residual(C, b + -2)
                if b.after(2) or (b.after(1) and u >= 1):
                    take_heads(C, b, u)
                if b.after(1):
                    take_weights(C, b, u, CROSS_TURNS)
                if u == 0 and more2:
                    layernorm(C, b + 2)
                inverse_sums(C, b, u)
                if u == 1 and b.after(2):
                    statistics_after(C, F, b + -2)
                if b.turn is None:
                    if b.c < 2:
                        split(SPLIT_FFN + 2 * b.c + u)
                    elif u == 0:
                        split(NSPLIT - NB + b.c)

            def cross_batch(b, more=True, more2=True):
                for u in range(2):
                    cross_step(b, u, more, more2)

            nc.vector.memset(mask_sb[:], 0.0).then_inc(zeroed, 1)
            deviations(C, 2, 0, NB)
            dve.wait_ge(zeroed, 2)
            layernorm(C, b0)
            layernorm(C, b0 + 1)
            take_latents(b0)
            take_queries(b0, 0)
            cross_batch(b0)
            cross_batch(b0 + 1)
            loop(dve, cross_batch, 2, NB - 2)
            cross_batch(Batch(None, NB - 2), True, False)
            cross_batch(Batch(None, NB - 1), False, False)
            for u in range(2):
                take_heads(C, end, u)
                take_weights(C, end, u, CROSS_TURNS)
            add_residual(C, end + -2)
            statistics_after(C, F, end + -2)
            take_heads(C, end + 1, 0)
            add_residual(C, end + -1)
            statistics_after(C, F, end + -1)

            def router(b):
                p = b.parity
                k = [0]
                rs = (rms_rs[:, b.c:b.c + 1] if b.turn is None else
                      rms_rs[:, bass.ds(b.turn * 2 + b.c, 1)])

                def then(ins):
                    k[0] += 1
                    ins.then_inc(r_step, 1)
                    dve.wait_ge(r_step, b.at(RSTEPS, k[0]))

                dve.wait_ge(logit_done, b.at(1, 1))
                nc.vector.tensor_scalar(r_log[:], pv_ps[:, 0:8], rs, None, ALU.mult).then_inc(logit_read, 1)
                dve.wait_ge(logit_read, b.at(1, 1))
                then(nc.vector.reduce_max(r_max[:], r_log[:], AX.X))
                nc.vector.tensor_scalar(r_arg[:], r_log[:], r_max[:], None, ALU.subtract)\
                    .then_inc(r_arg_ready, 1)
                other = r_log[:, None, :].to_broadcast([P, 8, 8])
                own = r_log[:, :, None].to_broadcast([P, 8, 8])
                nc.vector.tensor_tensor(r_gt[:], other, own, ALU.is_gt)
                then(nc.vector.tensor_tensor(r_eq[:], other, own, ALU.is_equal))
                then(nc.vector.tensor_tensor(r_eq[:], r_eq[:], tri_sb[:], ALU.mult))
                then(nc.vector.tensor_tensor(r_gt[:], r_gt[:], r_eq[:], ALU.add))
                then(nc.vector.reduce_sum(r_rank[:], r_gt[:], AX.X))
                dve.wait_ge(r_exped, b.at(1, 1))
                then(nc.vector.scalar_tensor_tensor(out=r_sel[:], in0=r_rank[:], scalar=2.0, in1=r_exp[:],
                                                    op0=ALU.is_lt, op1=ALU.mult))
                then(nc.vector.reduce_sum(r_sum[:], r_sel[:], AX.X))
                then(nc.vector.reciprocal(r_inv[:], r_sum[:]))
                assert k[0] == RSTEPS
                nc.vector.tensor_scalar(r_cw[p][:], r_sel[:], r_inv[:], 2.0, ALU.mult, ALU.mult)\
                    .then_inc(r_ready, 1)

            def expert_act(b, half):
                dve.wait_ge(gate_tanh, b.at(2, half + 1))
                if b.after(1):
                    dve.wait_ge(hidden_ready, b.at(2, half - 1))
                nc.vector.scalar_tensor_tensor(out=gate_s[half], in0=gate_t[half], scalar=1.0,
                                               in1=score_ps[half][:], op0=ALU.add, op1=ALU.mult)\
                    .then_inc(silu_ready, 1)
                dve.wait_ge(silu_ready, b.at(2, half + 1))
                dve.wait_ge(up_done, b.at(2, half + 1))
                dve.wait_ge(r_ready, b.at(1, 1))
                if b.after(1):
                    dve.wait_ge(h_turned, b.at(2, half - 1))
                for e in range(4):
                    cols = slice(e * P, (e + 1) * P)
                    last = nc.vector.scalar_tensor_tensor(
                        out=hidden[half][:, cols], in0=gate_s[half][:, cols],
                        scalar=r_cw[b.parity][:, 4 * half + e:4 * half + e + 1],
                        in1=proj_ps[half][:, cols], op0=ALU.mult, op1=ALU.mult)
                last.then_inc(hidden_ready, 1)

            def take_hidden(b, half):
                dve.wait_ge(h_t_hi, b.at(2, half + 1))
                hi, lo = hidden_t[half]
                low_half(flat(lo), turn_ps[half][:], flat(hi)).then_inc(h_t_ready, 1)

            def ffn_residual(b):
                dve.wait_ge(down_done, b.at(2, 2))
                nc.vector.tensor_tensor(x_of(b), y_ps[:, 0:D], x_of(b), ALU.add).then_inc(F.x_added, 1)

            def ffn_batch(b, more=True, more2=True):
                router(b)
                expert_act(b, 0)
                if b.after(1):
                    take_hidden(b + -1, 1)
                if more:
                    take_tokens(F, b + 1, pv_ps[:, P:3 * P])
                if more2:
                    layernorm(F, b + 2)
                expert_act(b, 1)
                take_hidden(b, 0)
                if b.after(1):
                    ffn_residual(b + -1)

            dve.wait_ge(ld_ffn, 16 * 3)
            for c in range(DC):
                nc.vector.tensor_scalar(router_f[:, c, :], router_sb[:, c, :], norm_sb[:, c:c + 1], None,
                                        ALU.mult).then_inc(rw_ready, 1)
            dve.wait_ge(rw_ready, 2)
            nc.vector.tensor_copy(router_w[0][:], router_f[:]).then_inc(rw_ready, 1)
            dve.wait_ge(rw_ready, 3)
            low_half(router_w[1][:], router_f[:], router_w[0][:]).then_inc(rw_ready, 1)
            deviations(F, 3, 0, NB)
            then(nc.vector.tensor_tensor(ln_var[:], ln_mv[:, :, 1], ln_rs[:], ALU.mult))
            then(nc.vector.tensor_tensor(ln_var[:], ln_var[:], ln_rs[:], ALU.mult))
            nc.vector.tensor_scalar(ln_var[:], ln_var[:], RMS_EPS, None, ALU.add).then_inc(var_ready, 1)
            dve.wait_ge(var_ready, 5)
            inverse_root(4, slice(0, NB), rms_rs)
            layernorm(F, b0)
            layernorm(F, b0 + 1)
            take_tokens(F, b0, pv_ps[:, P:3 * P])
            ffn_batch(b0)
            ffn_batch(b0 + 1)
            loop(dve, ffn_batch, 2, NB - 2)
            ffn_batch(Batch(None, NB - 2), True, False)
            ffn_batch(Batch(None, NB - 1), False, False)
            take_hidden(Batch(None, NB - 1), 1)
            ffn_residual(Batch(None, NB - 1))

        @block.scalar
        def _(act):
            def split(k):
                wait_staged(act, staged(k))
                nc.scalar.activation(split_place(k)[0], stage[staged(k) % NSTAGE][:], ACT.Copy).then_inc(w_hi, 1)

            def take_tokens(s, b, ps):
                act.wait_ge(s.ln_turned, b.at(1, 1))
                if s is C:
                    nc.scalar.activation(flat(xn_tf[b.parity]), ps, ACT.Copy).then_inc(s.xn_t_ready, 1)
                else:
                    nc.scalar.activation(flat(xn_t[b.parity][0]), ps, ACT.Copy).then_inc(s.xn_t_hi, 1)

            def take_heads(s, b, u):
                act.wait_ge(s.pv_done, b.at(s.U, u - 2))
                if b.turn is not None or b.c * s.U + u - 5 >= 0:
                    act.wait_ge(s.o_used, b.at(s.U, u - 4))
                nc.scalar.activation(flat(head_out[(u - 3) % 2][0]), pv_ps[:], ACT.Copy).then_inc(s.o_hi, 1)

            def exponentials(s, b, u, between):
                buf = unit_buf(s, b, u)
                act.wait_ge(s.shift_ready, b.at(2 * s.U, 2 * u + 1))
                for h in range(8):
                    if h == 4:
                        between()
                        act.wait_ge(s.shift_ready, b.at(2 * s.U, 2 * u + 2))
                        if s.masked:
                            nc.scalar.activation(sink_exp[:, buf, :], sink_arg[:, buf, :], ACT.Exp)
                    last = nc.scalar.activation(probs[buf][:, h, :], probs[buf][:, h, :], ACT.Exp,
                                                bias=neg_peak[:, buf, h:h + 1],
                                                accum_out=row_sum[:, buf, h:h + 1])
                last.then_inc(s.exped, 1)

            def take_weights(s, b, u, turns):
                act.wait_ge(s.p_turned, b.at(2 * s.U, 2 * (u - 2) + 2))
                if b.turn is not None or b.c * s.U + u - 3 >= 0:
                    act.wait_ge(s.pv_done, b.at(s.U, u - 2))
                nc.scalar.activation(probs_t[1][:], turn_bank(turns, "p1", u)[:], ACT.Copy)\
                    .then_inc(s.p_t1_ready, 1)

            def take_plain(b, seq):
                act.wait_ge(projected, b.at(NPROJ, seq + 1))
                what = PROJ[seq]
                if what == "v":
                    if b.after(2):
                        act.wait_ge(A.pv_done, b.at(4, -4))
                    nc.scalar.activation(v_n[b.parity][:].rearrange("p a b -> p (a b)"), proj_ps[seq % 2][:],
                                         ACT.Copy).then_inc(proj_out, 1)
                    return
                r = ROPED.index(what)
                if b.after(1) or ROPE_BEFORE[what] >= 0:
                    act.wait_ge(qk_turned, b.at(NROPE, ROPE_BEFORE[what] + 1))
                nc.scalar.activation(roped[ROPE_BUF[what]][:].rearrange("p a b c -> p (a b c)"),
                                     proj_ps[seq % 2][:], ACT.Copy, scale=1.0 if what == "k" else HD ** -0.5)\
                    .then_inc(proj_out, 1)

            def take_qk(b, what, u):
                r = ROPED.index(what)
                act.wait_ge(qk_turned, b.at(NROPE, r + 1))
                ps = turn_bank(SELF_TURNS, what, u)
                if what == "k":
                    if b.after(2):
                        act.wait_ge(A.scored, b.at(8, -8))
                    src = ps[:].rearrange("p (g k) -> p g k", g=4)
                    nc.scalar.activation(k_bd[b.parity][0][0:HD, :, 0, :], src[0:HD], ACT.Copy)
                    nc.scalar.activation(k_bd[b.parity][0][HD:P, :, 1, :], src[HD:P], ACT.Copy)\
                        .then_inc(k_hi, 1)
                else:
                    g = int(what[1])
                    if b.after(1) or g >= 2:
                        act.wait_ge(A.scored, b.at(8, 2 * (g - 2) + 2))
                    nc.scalar.activation(flat(q_t[g % 2][0]), ps[:], ACT.Copy).then_inc(q_hi, 1)

            def self_step(b, u, more=True, more2=True):
                def between():
                    if b.after(1) or u >= 3:
                        take_heads(A, b, u)
                    for mb, what in made[:1]:
                        take_plain(mb, PROJ.index(what))
                    if b.after(1) or u >= 2:
                        take_weights(A, b, u, SELF_TURNS)
                made, _, turned = self_inputs(b, u, more)
                for tb, what in turned:
                    take_qk(tb, what, u)
                if u == 0 and more:
                    if b.after(1):
                        act.wait_ge(projected, b.at(NPROJ, 0))
                    take_tokens(A, b + 1, turn_bank(SELF_TURNS, "ln", 0)[:, 0:D])
                exponentials(A, b, u, between)
                for mb, what in made[1:]:
                    take_plain(mb, PROJ.index(what))
                if b.turn is None and b.c == 0 and u < 2:
                    for k in range(2):
                        split(SPLIT_OUT + 2 * u + k)

            def self_batch(b, more=True, more2=True):
                for u in range(4):
                    self_step(b, u, more, more2)

            def roots(group, cols):
                act.wait_ge(var_ready, group + 1)
                nc.scalar.activation(ln_std[:, cols], ln_var[:, cols], ACT.Sqrt).then_inc(std_ready, 1)

            b0 = Batch(None, 0)
            roots(0, slice(0, 2))
            split(0)
            take_tokens(A, b0, turn_bank(SELF_TURNS, "ln", 0)[:, 0:D])
            split(1)
            split(2)
            act.wait_ge(zeroed, 1)
            take_plain(b0, 0)
            split(3)
            take_plain(b0, 1)
            take_plain(b0, 2)
            take_qk(b0, "k", 3)
            take_qk(b0, "q0", 3)
            take_plain(b0, 3)
            split(4)
            split(5)
            roots(1, slice(2, NB))
            self_batch(b0)
            self_batch(b0 + 1)
            loop(act, self_batch, 2, NB - 2)
            self_batch(Batch(None, NB - 2), True, False)
            self_batch(Batch(None, NB - 1), False, False)
            end = Batch(None, NB)
            for u in range(3):
                take_heads(A, end, u)
                if u < 2:
                    take_weights(A, end, u, SELF_TURNS)

            for t in range(4):
                v, e = t // 2, t % 2
                act.wait_ge(f1_done, t + 1)
                if t >= 2:
                    act.wait_ge(f2_done, t - 1)
                nc.scalar.activation(fold_b1[e], score_ps[e][0:96, :], ACT.Copy).then_inc(f1_out, 1)
                act.wait_ge(f4_done, t + 1)
                nc.scalar.activation(flat(fold_n[0])[:, t * 512:(t + 1) * 512], turn_ps[e][:], ACT.Copy)\
                    .then_inc(f4_hi, 1)
                act.wait_ge(f3_done, t + 1)
                for c in range(DC):
                    dst = fold_a[:, c, 4 * v:4 * v + 4, :].rearrange("p (a e) (j d) -> p e j a d", e=2, j=2)[:, e]
                    src = pv_ps[:, c * D:(c + 1) * D].rearrange("p (j a d) -> p j a d", j=2, a=2)
                    last = nc.scalar.activation(dst, src, ACT.Copy)
                last.then_inc(f3_out, 1)

            def take_latents(b):
                act.wait_ge(kv_turned, b.at(1, 1))
                if b.after(2):
                    act.wait_ge(C.scored, b.at(4, -4))
                ps = turn_bank(CROSS_TURNS, "kv", 0)
                nc.scalar.activation(k_bd[b.parity][0][0:HD, 0, 0, :], ps[0:HD, 0:P], ACT.Copy)
                nc.scalar.activation(k_bd[b.parity][0][HD:P, 0, 1, :], ps[HD:P, 0:P], ACT.Copy)\
                    .then_inc(kv_t_hi, 1)

            def take_queries(b, u):
                act.wait_ge(cq_done, b.at(2, u + 1))
                if b.after(1):
                    act.wait_ge(C.scored, b.at(4, 2 * (u - 2) + 2))
                nc.scalar.activation(flat(q_t[u][0]), proj_ps[u][:], ACT.Copy)\
                    .then_inc(cq_hi, 1)

            def cross_step(b, u, more=True, more2=True):
                def between():
                    if b.after(2) or (b.after(1) and u >= 1):
                        take_heads(C, b, u)
                    if b.after(1):
                        take_weights(C, b, u, CROSS_TURNS)
                if u == 0 and more:
                    take_latents(b + 1)
                if u == 1 and more2:
                    act.wait_ge(cq_done, b.at(2, 2))
                    take_tokens(C, b + 2, turn_bank(CROSS_TURNS, "ln", 1)[:, 0:D])
                exponentials(C, b, u, between)
                if more:
                    take_queries(b + 1, u)
                if b.turn is None:
                    if b.c < 2:
                        split(SPLIT_FFN + 2 * b.c + u)
                    elif u == 0:
                        split(NSPLIT - NB + b.c)

            def cross_batch(b, more=True, more2=True):
                for u in range(2):
                    cross_step(b, u, more, more2)

            roots(2, slice(0, NB))
            take_tokens(C, b0, turn_bank(CROSS_TURNS, "ln", 1)[:, 0:D])
            take_latents(b0)
            take_queries(b0, 0)
            take_queries(b0, 1)
            take_tokens(C, b0 + 1, turn_bank(CROSS_TURNS, "ln", 1)[:, 0:D])
            cross_batch(b0)
            cross_batch(b0 + 1)
            loop(act, cross_batch, 2, NB - 2)
            cross_batch(Batch(None, NB - 2), True, False)
            cross_batch(Batch(None, NB - 1), False, False)
            for u in range(2):
                take_heads(C, end, u)
                take_weights(C, end, u, CROSS_TURNS)
            take_heads(C, end + 1, 0)

            def ffn_tokens(b):
                if b.after(2):
                    act.wait_ge(up_done, b.at(2, -2))
                take_tokens(F, b, pv_ps[:, P:3 * P])

            def gate_tanhs(b, half):
                act.wait_ge(gate_done, b.at(2, half + 1))
                if b.after(1):
                    act.wait_ge(silu_ready, b.at(2, half - 1))
                nc.scalar.activation(gate_t[half], score_ps[half][:], ACT.Tanh, scale=0.5)\
                    .then_inc(gate_tanh, 1)

            def take_hidden(b, half):
                act.wait_ge(h_turned, b.at(2, half + 1))
                if b.after(1):
                    act.wait_ge(down_done, b.at(2, half - 1))
                nc.scalar.activation(flat(hidden_t[half][0]), turn_ps[half][:], ACT.Copy).then_inc(h_t_hi, 1)

            def ffn_batch(b, more=True):
                act.wait_ge(r_arg_ready, b.at(1, 1))
                if b.after(1):
                    act.wait_ge(r_ready, b.at(1, 0))
                nc.scalar.activation(r_exp[:], r_arg[:], ACT.Exp).then_inc(r_exped, 1)
                gate_tanhs(b, 0)
                if b.after(1):
                    take_hidden(b + -1, 1)
                if more:
                    ffn_tokens(b + 1)
                gate_tanhs(b, 1)
                take_hidden(b, 0)

            act.wait_ge(C.x_added, NB)
            roots(3, slice(0, NB))
            roots(4, slice(0, NB))
            ffn_tokens(b0)
            ffn_batch(b0)
            ffn_batch(b0 + 1)
            loop(act, ffn_batch, 2, NB - 2)
            ffn_batch(Batch(None, NB - 2))
            ffn_batch(Batch(None, NB - 1), False)
            take_hidden(Batch(None, NB - 1), 1)

        @block.gpsimd
        def _(pool):
            def normalise(s, b, u):
                buf = unit_buf(s, b, u)
                pool.wait_ge(s.inv_ready, b.at(s.U, u + 1))
                nc.gpsimd.tensor_tensor(probs[buf][:], probs[buf][:],
                                        inv_sum[:, buf, :][:, :, None].to_broadcast([P, 8, P]), ALU.mult)\
                    .then_inc(s.normed, 1)

            def add_rotated(b, what):
                r = ROPED.index(what)
                buf = (b.parity + r) % 2
                pool.wait_ge(rot_done, b.at(NROPE, r + 1))
                dst = roped[ROPE_BUF[what]][:].rearrange("p h (t a) d -> p h t a d", a=2)[:, :, :, 0, :]
                for t in range(2):
                    last = nc.gpsimd.tensor_tensor(dst[:, :, t, :], rot_a[buf][:, :, t, :],
                                                   rot_b[buf][:, :, 1 - t, :], ALU.add)
                last.then_inc(roped_done, 1)

            def self_step(b, u, more=True):
                if b.after(1) or u:
                    normalise(A, b, u - 1)
                for tb, what in self_inputs(b, u, more)[1]:
                    add_rotated(tb, what)

            def self_batch(b, more=True):
                for u in range(4):
                    self_step(b, u, more)

            b0 = Batch(None, 0)
            for what in ROPED[:3]:
                add_rotated(b0, what)
            pool.dma_start(X[:].rearrange("p (b d) -> p b d", d=D)[:, 2:NB],
                           x.rearrange("b s d -> s b d")[:, 2:NB]).then_inc(ld_x, 16)
            for dst, src in ((wqr_sb, wqr_t), (wkr_sb, wkr_t), (wkckv_sb, wkckv), (rope_c_sb, rope_c)):
                pool.dma_start(dst[:], src).then_inc(ld_small, 16)
            for dst, src in ((router_sb, router), (norm_sb, norm_w), (tri_sb, tri)):
                pool.dma_start(dst[:], src).then_inc(ld_ffn, 16)
            self_batch(b0)
            self_batch(b0 + 1)
            loop(pool, self_batch, 2, NB - 2)
            self_batch(Batch(None, NB - 2))
            self_batch(Batch(None, NB - 1), False)
            end = Batch(None, NB)
            normalise(A, end, -1)

            wait_staged(pool, SPLIT_FFN)
            pool.wait_ge(ld_small, 16 * 4)
            kv_v = kv_rope[:].rearrange("p (b d) -> p b d", d=HD)
            half = HD // 2
            wide = [P, NB, half]
            nc.gpsimd.tensor_tensor(kv_v, ctx_sb, rope_c_sb[:, 0][:, None].to_broadcast([P, NB, HD]),
                                    ALU.mult).then_inc(kv_part, 1)
            pool.wait_ge(kv_part, 1)
            nc.gpsimd.tensor_tensor(ctx_sb, ctx_sb, rope_c_sb[:, 1][:, None].to_broadcast([P, NB, HD]),
                                    ALU.mult).then_inc(kv_part, 1)
            pool.wait_ge(kv_part, 2)
            nc.gpsimd.tensor_tensor(kv_v[:, :, 0:half], kv_v[:, :, 0:half], ctx_sb[:, :, half:HD], ALU.add)
            nc.gpsimd.tensor_tensor(kv_v[:, :, half:HD], kv_v[:, :, half:HD], ctx_sb[:, :, 0:half], ALU.add)\
                .then_inc(kv_done, 1)

            def latents_of(b):
                if b.turn is None:
                    return kv_rope[:, b.c * HD:(b.c + 1) * HD]
                return kv_rope[:, bass.ds(b.turn * (2 * HD) + b.c * HD, HD)]

            def copy_keys(b):
                if b.after(2):
                    pool.wait_ge(kv_turned, b.at(1, -1))
                nc.gpsimd.tensor_copy(kv_dup[b.parity][:, 0, :], latents_of(b))
                nc.gpsimd.tensor_copy(kv_dup[b.parity][:, 1, :], latents_of(b)).then_inc(kv_copied, 1)

            def copy_values(b):
                if b.after(2):
                    pool.wait_ge(C.pv_done, b.at(2, -2))
                nc.gpsimd.tensor_copy(v_n[b.parity][:, 0, :], latents_of(b)).then_inc(v_copied, 1)

            def cross_step(b, u, more2=True):
                if b.after(1) or u:
                    normalise(C, b, u - 1)
                if u == 0:
                    copy_values(b)
                elif more2:
                    copy_keys(b + 2)

            def cross_batch(b, more2=True):
                for u in range(2):
                    cross_step(b, u, more2)

            pool.wait_ge(kv_done, 1)
            copy_keys(b0)
            copy_keys(b0 + 1)
            cross_batch(b0)
            cross_batch(b0 + 1)
            loop(pool, cross_batch, 2, NB - 2)
            cross_batch(Batch(None, NB - 2), False)
            cross_batch(Batch(None, NB - 1), False)
            normalise(C, end, -1)


def _rope_tables():
    inv = np.power(np.float32(1.0 / 1024.0), np.linspace(0.0, 1.0, 16, dtype=np.float32)).astype(np.float32)
    theta = (np.arange(P, dtype=np.float32)[:, None] * inv[None, :]).astype(np.float32)
    cos, sin = np.cos(theta.astype(np.float64)), np.sin(theta.astype(np.float64))
    rope = np.stack([np.stack([cos, cos], 1), np.stack([-sin, sin], 1)], 1)
    inv_c = (np.float32(1.0) / np.power(np.float32(10000.0), np.arange(0, HD, 2, dtype=np.float32)
                                        / np.float32(HD))).astype(np.float32)
    freqs = (np.arange(P, dtype=np.float32)[:, None] * inv_c[None, :]).astype(np.float32).astype(np.float64)
    sin_c, cos_c = np.repeat(np.sin(freqs), 2, -1), np.repeat(np.cos(freqs), 2, -1)
    signed = np.concatenate([sin_c[:, HD // 2:], -sin_c[:, :HD // 2]], -1)
    return (rope.astype(np.float32),
            np.stack([cos_c, signed], 1).astype(np.float32))


def _layouts(x, ctx_512, L0_attn_W_qkv, L0_attn_W_out, L0_attn_s, L0_xattn_Wq, L0_xattn_w_kc_q,
             L0_xattn_w_kc_kv, L0_xattn_W_qr, L0_xattn_W_kr, L0_xattn_Wo, L0_ffn_router_w,
             L0_ffn_norm_w, L0_ffn_gate_w, L0_ffn_up_w, L0_ffn_down_w):
    def rows(w):
        return w.reshape(-1, P, *w.shape[1:]).swapaxes(0, 1)

    wq = L0_attn_W_qkv[:, :2048].reshape(D, 4, 2, 4, HD).transpose(0, 1, 3, 2, 4).reshape(D, 4, 512)
    wk, wv = L0_attn_W_qkv[:, 2048:2560], L0_attn_W_qkv[:, 2560:3072]
    banks = np.stack([{"k": wk, "v": wv}.get(s) if s in "kv" else wq[:, int(s[1])] for s in PROJ], 1)
    wqkv = banks.reshape(DC, P, NPROJ, 512).transpose(1, 2, 0, 3).reshape(P, NPROJ, 1024)
    wout = L0_attn_W_out.reshape(4, 2, 4, HD, D).transpose(0, 2, 1, 3, 4).reshape(2048, D)
    sink = L0_attn_s.reshape(4, 2, 4).transpose(0, 2, 1).reshape(32)
    rope, rope_c = _rope_tables()
    pos = np.arange(P)
    q, k = pos[:, None], pos[None, :]
    mask = np.where((q >= k) & (q < k + 64), MASKED, 0.0).astype(np.float32)
    by_head = lambda w: w.transpose(2, 0, 1)
    pairs = lambda w: by_head(w).reshape(HD, 8, 2, -1).transpose(2, 0, 1, 3).reshape(P, 8, -1)
    wkcq = by_head(L0_xattn_w_kc_q).reshape(2, 96, 16, P).transpose(1, 0, 2, 3)
    inward = lambda w: rows(w.transpose(1, 0, 2).reshape(D, 1024))
    down = L0_ffn_down_w.transpose(1, 0, 2).reshape(P, 2, 1024)
    experts = np.concatenate([inward(L0_ffn_gate_w), inward(L0_ffn_up_w), down], 1)
    tri = np.broadcast_to((pos[None, :8] < pos[:8, None]).astype(np.float32), (P, 8, 8))
    return dict(
        x=x, ctx=ctx_512, wqkv=wqkv, wout=rows(wout).reshape(P, 4, 1024), sink=sink, wqr_t=pairs(L0_xattn_W_qr),
        wkr_t=pairs(L0_xattn_W_kr), wkcq_t=wkcq, wq=rows(L0_xattn_Wq),
        wkckv=L0_xattn_w_kc_kv.transpose(1, 0, 2), wo_t=rows(L0_xattn_Wo.T),
        router=rows(L0_ffn_router_w.T), norm_w=rows(L0_ffn_norm_w), experts=experts,
        ident=np.eye(P, dtype=np.float32), mask=mask, rope=rope, rope_c=rope_c,
        tri=tri)


def kernel(**inputs):
    import concourse.bacc as bacc
    from concourse.bass_utils import run_bass_kernel_spmd

    nc = bacc.Bacc("TRN2", target_bir_lowering=False, num_devices=1)
    arrays, args = {}, {}
    for name, a in _layouts(**{k: np.asarray(v) for k, v in inputs.items()}).items():
        a = np.ascontiguousarray(a)
        arrays[f"in_{name}"] = a
        args[name] = nc.dram_tensor(f"in_{name}", a.shape, mybir.dt.from_np(a.dtype), kind="ExternalInput").ap()
    args["out"] = nc.dram_tensor("out_y", (NB, P, D), F32, kind="ExternalOutput").ap()
    decoder_layer(nc, **args)
    return run_bass_kernel_spmd(nc, [arrays], core_ids=[0]).results[0]["out_y"]
```

```python
import numpy as np
import concourse.bass as bass
from concourse import mybir
from contextlib import ExitStack

F32 = mybir.dt.float32
ALU = mybir.AluOpType
ACT = mybir.ActivationFunctionType
AX = mybir.AxisListType

F32R = mybir.dt.float32r
P = 128
NB = 16
D = 256
DC = D // P
HD = 64
LN_EPS = 1e-5
RMS_EPS = 1e-6
MASKED = -3.0e38
NSTAGE = 3
SPLIT_OUT, SPLIT_FFN, NSPLIT = 6, 10, 16

PROJ = ["k", "q0", "q1", "q2", "q3", "v"]
ROPED = ["k", "q0", "q1", "q2", "q3"]
NPROJ, NROPE = len(PROJ), len(ROPED)
ROPE_BUF = {"k": 0, "q0": 1, "q1": 2, "q2": 0, "q3": 2}
ROPE_BEFORE = {"k": 3 - NROPE, "q0": 1 - NROPE, "q1": 4 - NROPE, "q2": 0, "q3": 2}


class Batch:

    def __init__(self, turn, c):
        self.turn, self.c = turn, c

    def __add__(self, k):
        return Batch(self.turn, self.c + k)

    def at(self, per, k):
        fixed = self.c * per + k
        return fixed if self.turn is None else self.turn * (2 * per) + fixed

    @property
    def parity(self):
        return self.c % 2

    def after(self, first):
        return self.turn is not None or self.c >= first


def decoder_layer(nc, x, ctx, wqkv, wout, sink, wqr_t, wkr_t, wkcq_t, wq, wkckv, wo_t, router, norm_w,
                  experts, ident, mask, rope, rope_c, tri, out):
    with ExitStack() as stack:
        def sb(name, shape, dt=F32):
            return stack.enter_context(nc.sbuf_tensor(name, shape, dt))

        def sem(name):
            return stack.enter_context(nc.semaphore(name))

        def bank(name):
            return stack.enter_context(nc.psum_tensor(name, [P, 512], F32))

        X = sb("X", [P, NB * D])
        stage = [sb(f"stage{i}", [P, 1024]) for i in range(NSTAGE)]
        big_w = [sb(f"big_w_{x}", [P, 6144], F32R) for x in ("hi", "lo")]
        wqkv_sb = [w[:].rearrange("p (s c n) -> p s c n", s=NPROJ, c=DC) for w in big_w]
        gate_sb = [w[:, 0:2048].rearrange("p (c n) -> p c n", c=DC) for w in big_w]
        up_sb = [w[:, 2048:4096].rearrange("p (c n) -> p c n", c=DC) for w in big_w]
        down_sb = [w[:, 4096:6144].rearrange("p (e n) -> p e n", e=8) for w in big_w]
        wout_sb = [sb(f"wout_{x}", [P, 16, D], F32R) for x in ("hi", "lo")]
        ctx_sb = stage[SPLIT_FFN % NSTAGE][:].rearrange("p (b d) -> p b d", b=NB)
        kv_rope = sb("kv_rope", [P, NB * HD])
        wqr_sb = sb("wqr_sb", [96, 2, 16, HD])
        wkr_sb = sb("wkr_sb", [P, 8, 2 * HD])
        wkckv_sb = sb("wkckv_sb", [P, 16, HD])

        def over(name, shape, dt, host, skip):
            return nc.alloc_sbuf_tensor_at(name, shape, dt, offset=nc.lookup_mloc(host).addr + skip)

        KB16 = 16 * D * 4
        wkcq_sb = over("wkcq_sb", [96, 2, 16, P], F32, "big_w_hi", 0)
        wq_sb = over("wq_sb", [P, 16, D], F32, "big_w_hi", KB16)
        wo_sb = over("wo_sb", [P, 16, D], F32, "big_w_hi", 2 * KB16)
        fold_a = over("fold_a", [P, DC, 8, P], F32, "wout_hi", 0)
        fold_n = [over("fold_n_hi", [P, 8, D], F32R, "wout_hi", KB16 // 2),
                  over("fold_n_lo", [P, 8, D], F32R, "wout_lo", 0)]
        ident_sb = sb("ident_sb", [P, P])
        mask_sb = sb("mask_sb", [P, P])
        sink_sb = sb("sink_sb", [P, 32])
        rope_sb = sb("rope_sb", [P, 2, 2, 16])
        rope_c_sb = sb("rope_c_sb", [P, 2, HD])
        router_sb = sb("router_sb", [P, DC, 8])
        norm_sb = sb("norm_sb", [P, DC])
        router_f = sb("router_f", [P, DC, 8])
        router_w = [sb(f"router_w_{x}", [P, DC, 8], F32R) for x in ("hi", "lo")]
        tri_sb = sb("tri_sb", [P, 8, 8])

        xn = [sb(f"xn{i}", [P, D]) for i in range(2)]
        xn_t = [[sb(f"xn_t{i}_{x}", [P, DC, P], F32R) for x in ("hi", "lo")] for i in range(2)]
        xn_tf = [over(f"xn_tf{i}", [P, DC, P], F32, f"xn_t{i}_hi", 0) for i in range(2)]
        ln_st = sb("ln_st", [P, NB * 6])
        ln_mv = sb("ln_mv", [P, NB, 2])
        ln_var = sb("ln_var", [P, 2, NB])
        ln_std = sb("ln_std", [P, 2, NB])
        ln_tmp = sb("ln_tmp", [P, 2, NB])
        ln_rs = sb("ln_rs", [P, 2, NB])
        q_t = [[sb(f"q_t{i}_{x}", [P, 4, P], F32R) for x in ("hi", "lo")] for i in range(2)]
        k_bd = [[sb(f"k_bd{i}_{x}", [P, 4, 2, P], F32R) for x in ("hi", "lo")] for i in range(2)]
        v_n = [sb(f"v_n{i}", [P, 8, HD]) for i in range(2)]
        roped = [sb(f"roped{i}", [P, 8, 4, 16]) for i in range(3)]
        rot_a = [sb(f"rot_a{i}", [P, 8, 2, 16]) for i in range(2)]
        rot_b = [sb(f"rot_b{i}", [P, 8, 2, 16]) for i in range(2)]
        probs = [sb(f"probs{i}", [P, 8, P]) for i in range(4)]
        gate_keeper = sb("gate_keeper", [P, 8])
        table_keeper = sb("table_keeper", [P, 4])
        peak = sb("peak", [P, 4, 8])
        neg_peak = sb("neg_peak", [P, 4, 8])
        sink_arg = sb("sink_arg", [P, 4, 8])
        sink_exp = sb("sink_exp", [P, 4, 8])
        row_sum = sb("row_sum", [P, 4, 8])
        denom = sb("denom", [P, 4, 8])
        inv_sum = sb("inv_sum", [P, 4, 8])
        probs_t = [sb(f"probs_t{j}", [P, 512]) for j in range(2)]
        head_out = [[sb(f"head_out{i}_{x}", [P, 4, P], F32R) for x in ("hi", "lo")] for i in range(2)]
        kv_dup = [over(f"kv_dup{i}", [P, 2, HD], F32, f"rot_b{i}", 0) for i in range(2)]
        fold_g = [roped[i][:].rearrange("p a b c -> p (a b c)") for i in (0, 1)]
        fold_b = [roped[i][:].rearrange("p a b c -> p (a b c)") for i in (2, 0)]
        fold_at = [probs[i][:].rearrange("p a b -> p (a b)")[:, 0:512] for i in range(2)]
        gate_t = [probs[i][:].rearrange("p a b -> p (a b)")[:, 0:512] for i in range(2)]
        gate_s = [probs[i][:].rearrange("p a b -> p (a b)")[:, 512:1024] for i in range(2)]
        hidden = [probs[2 + i][:].rearrange("p a b -> p (a b)")[:, 0:512] for i in range(2)]
        hidden_t = head_out
        r_log = sb("r_log", [P, 8])
        r_max = sb("r_max", [P, 1])
        r_arg = sb("r_arg", [P, 8])
        r_exp = sb("r_exp", [P, 8])
        r_gt = sb("r_gt", [P, 8, 8])
        r_eq = sb("r_eq", [P, 8, 8])
        r_rank = sb("r_rank", [P, 8])
        r_sel = sb("r_sel", [P, 8])
        r_sum = sb("r_sum", [P, 1])
        r_inv = sb("r_inv", [P, 1])
        r_cw = [sb(f"r_cw{i}", [P, 8]) for i in range(2)]

        proj_ps = [bank("proj_ps0"), bank("proj_ps1")]
        score_ps = [bank("score_ps0"), bank("score_ps1")]
        turn_ps = [bank("turn_ps0"), bank("turn_ps1")]
        pv_ps = bank("pv_ps")
        y_ps = bank("y_ps")

        ld_const, ld_ident = sem("ld_const"), sem("ld_ident")
        ld_x = [sem(f"ld_x{i}") for i in range(3)]
        ld_stage = [sem(f"ld_stage{i}") for i in range(NSTAGE)]
        ld_wkcq, ld_fold, ld_small, ld_ffn = sem("ld_wkcq"), sem("ld_fold"), sem("ld_small"), sem("ld_ffn")
        w_hi, w_lo = sem("w_hi"), sem("w_lo")
        stored = sem("stored")
        zeroed = sem("zeroed")
        kv_part, kv_done = sem("kv_part"), sem("kv_done")

        class Sems:

            def __init__(self, name, units, masked):
                self.U, self.masked = units, masked
                s = lambda what: sem(f"{name}_{what}")
                self.stats = s("stats")
                self.xn_ready = s("xn_ready")
                self.ln_turned = s("ln_turned")
                self.xn_t_hi = s("xn_t_hi")
                self.xn_t_ready = s("xn_t_ready")
                self.x_added = s("x_added")
                if units:
                    self.scored = s("scored")
                    self.peaked = s("peaked")
                    self.shift_ready = s("shift_ready")
                    self.exped = s("exped")
                    self.summed = s("summed")
                    self.inv_ready = s("inv_ready")
                    self.normed = s("normed")
                    self.p_turned = s("p_turned")
                    self.p_t0_ready = s("p_t0_ready")
                    self.p_t1_ready = s("p_t1_ready")
                    self.pv_done = s("pv_done")
                    self.o_hi = s("o_hi")
                    self.o_ready = s("o_ready")
                    self.o_used = s("o_used")

        A = Sems("self", 4, True)
        C = Sems("cross", 2, False)
        F = Sems("ffn", 0, False)
        EARLY = NB - 4
        projected = sem("self_projected")
        proj_out = sem("self_proj_out")
        rot_done = sem("self_rot_done")
        roped_done = sem("self_roped_done")
        qk_turned = sem("self_qk_turned")
        k_hi = sem("self_k_hi")
        q_hi = sem("self_q_hi")
        k_ready = sem("self_k_ready")
        q_ready = sem("self_q_ready")
        g_done, g_out = sem("fold_g_done"), sem("fold_g_out")
        b_done, b_out = sem("fold_b_done"), sem("fold_b_out")
        at_done, at_out = sem("fold_at_done"), sem("fold_at_out")
        a_done, a_out = sem("fold_a_done"), sem("fold_a_out")
        n_done, n_hi, n_out = sem("fold_n_done"), sem("fold_n_hi"), sem("fold_n_out")
        kv_copied = sem("cross_kv_copied")
        v_copied = sem("cross_v_copied")
        kv_turned = sem("cross_kv_turned")
        kv_t_hi = sem("cross_kv_t_hi")
        kv_t_ready = sem("cross_kv_t_ready")
        cq_done = sem("cross_cq_done")
        cq_hi = sem("cross_cq_hi")
        cq_ready = sem("cross_cq_ready")
        logit_done = sem("ffn_logit_done")
        logit_read = sem("ffn_logit_read")
        norm_step = sem("norm_step")
        var_ready = sem("var_ready")
        std_ready = sem("std_ready")
        r_step = sem("ffn_router_step")
        r_arg_ready = sem("ffn_arg_ready")
        r_exped = sem("ffn_r_exped")
        gate_done = sem("ffn_gate_done")
        up_done = sem("ffn_up_done")
        gate_tanh = sem("ffn_gate_tanh")
        silu_ready = sem("ffn_silu_ready")
        hidden_ready = sem("ffn_hidden_ready")
        h_turned = sem("ffn_h_turned")
        h_t_hi = sem("ffn_h_t_hi")
        h_t_ready = sem("ffn_h_t_ready")
        down_done = sem("ffn_down_done")
        r_ready = sem("ffn_r_ready")
        rw_ready = sem("ffn_rw_ready")
        RSTEPS = 8

        def flat(t):
            return t[:].rearrange("p a b -> p (a b)")

        def split_place(k):
            if SPLIT_OUT <= k < SPLIT_FFN:
                return [flat(w)[:, (k - SPLIT_OUT) * 1024:(k - SPLIT_OUT + 1) * 1024] for w in wout_sb]
            k = k if k < SPLIT_OUT else k - SPLIT_FFN
            return [w[:, k * 1024:(k + 1) * 1024] for w in big_w]

        def staged(k):
            return k if k < SPLIT_FFN else k + 1

        def wait_staged(eng, n):
            eng.wait_ge(ld_stage[n % NSTAGE], 16 * (n // NSTAGE + 1))

        def x_of(b):
            if b.turn is None:
                return X[:, b.c * D:(b.c + 1) * D]
            return X[:, bass.ds(b.turn * (2 * D) + b.c * D, D)]

        def loop(eng, body, first, last):
            with eng.Fori(first // 2, last // 2) as turn:
                for c in range(2):
                    body(Batch(turn, c))

        SELF_TURNS = [("q1", 0), ("ln", 0), ("p0", 0), ("p1", 0),
                      ("q2", 1), ("p0", 1), ("p1", 1),
                      ("q3", 2), ("p0", 2), ("p1", 2),
                      ("k", 3), ("q0", 3), ("p0", 3), ("p1", 3)]
        CROSS_TURNS = [("kv", 0), ("p0", 0), ("p1", 0), ("ln", 1), ("p0", 1), ("p1", 1)]

        def turn_bank(turns, kind, u):
            return turn_ps[turns.index((kind, u)) % 2]

        def wait_turn_bank(eng, s, turns, b, kind, u, exists):
            i = turns.index((kind, u))
            while True:
                i -= 2
                if i < 0:
                    i += len(turns)
                    b = b + -1
                k, w = turns[i]
                if b.turn is None and not exists(b.c, k, w):
                    if b.c < -1:
                        return
                    continue
                break
            if k == "p0":
                eng.wait_ge(s.p_t0_ready, b.at(s.U, w - 2 + 1))
            elif k == "p1":
                eng.wait_ge(s.p_t1_ready, b.at(s.U, w - 2 + 1))
            elif k == "ln":
                eng.wait_ge(s.xn_t_ready, b.at(1, 2 if s is A else 3))
            elif k == "kv":
                eng.wait_ge(kv_t_ready, b.at(1, 2))
            elif k == "k":
                eng.wait_ge(k_ready, b.at(1, 2))
            elif k == "q0":
                eng.wait_ge(q_ready, b.at(4, 4 + 1))
            else:
                eng.wait_ge(q_ready, b.at(4, int(k[1]) + 1))

        def self_exists(c, kind, u):
            if kind in ("p0", "p1"):
                return 4 * c + u - 2 >= 0
            if kind in ("q1", "q2", "q3"):
                return 0 <= c < NB
            return 0 <= c + 1 < NB

        def cross_exists(c, kind, u):
            if kind in ("p0", "p1"):
                return 2 * c + u - 2 >= 0
            return 0 <= c + (2 if kind == "ln" else 1) < NB

        def self_inputs(b, u, more):
            own, next_ = lambda *what: [(b, w) for w in what], lambda *what: [(b + 1, w) for w in what if more]
            return [(own("q3", "v"), own("q2"), own("q1")),
                    (next_("k", "q0"), own("q3"), own("q2")),
                    (next_("q1"), next_("k", "q0"), own("q3")),
                    (next_("q2"), next_("q1"), next_("k", "q0"))][u]

        def split_in(b, u, lag):
            n = 2 * b.c + u if b.turn is None else NB
            if 0 <= n - lag < 3:
                return SPLIT_FFN + n - lag
            if 0 <= n - 2 * (NB - 2) < 3:
                return SPLIT_FFN + 3 + n - 2 * (NB - 2)
            return None

        def unit_buf(s, b, u):
            return (u if s.U == 4 else 2 * b.parity + u) % 4

        block = stack.enter_context(nc.Block())

        @block.sync
        def _(sp):
            def load_chunk(k, src):
                n = staged(k)
                if n - NSTAGE == SPLIT_FFN:
                    sp.wait_ge(kv_done, 1)
                elif n >= NSTAGE:
                    before = n - NSTAGE if n - NSTAGE < SPLIT_FFN else n - NSTAGE - 1
                    sp.wait_ge(w_lo, before + 1)
                sp.dma_start(stage[n % NSTAGE][:], src).then_inc(ld_stage[n % NSTAGE], 16)

            x_v = x.rearrange("b s d -> s b d")
            X_v = X[:].rearrange("p (b d) -> p b d", d=D)
            sp.dma_start(X_v[:, 0:2], x_v[:, 0:2]).then_inc(ld_x[0], 16)
            load_chunk(0, wqkv[:, 0])
            sp.dma_start(ident_sb[:], ident).then_inc(ld_ident, 16)
            sp.dma_start(X_v[:, 2:4], x_v[:, 2:4]).then_inc(ld_x[1], 16)
            load_chunk(1, wqkv[:, 1])
            sp.dma_start(rope_sb[:], rope).then_inc(ld_const, 16)
            load_chunk(2, wqkv[:, 2])
            sp.dma_start(mask_sb[:], mask).then_inc(ld_const, 16)
            sp.dma_start(sink_sb[:], sink.partition_broadcast(P)).then_inc(ld_const, 16)
            for k in range(3, NPROJ):
                load_chunk(k, wqkv[:, k])
            for k in range(4):
                load_chunk(SPLIT_OUT + k, wout[:, k])
            sp.wait_ge(w_lo, SPLIT_FFN + 1 - NSTAGE)
            sp.dma_start(ctx_sb, ctx.rearrange("b l d -> l b d")).then_inc(ld_stage[SPLIT_FFN % NSTAGE], 16)
            for dst, src in ((wqr_sb, wqr_t), (wkr_sb, wkr_t), (wkckv_sb, wkckv), (rope_c_sb, rope_c)):
                sp.dma_start(dst[:], src).then_inc(ld_small, 16)
            for dst, src in ((router_sb, router), (norm_sb, norm_w), (tri_sb, tri)):
                sp.dma_start(dst[:], src).then_inc(ld_ffn, 16)
            sp.wait_ge(projected, NPROJ * NB)
            sp.dma_start(wkcq_sb[:], wkcq_t).then_inc(ld_wkcq, 16)
            sp.dma_start(wo_sb[:], wo_t).then_inc(ld_fold, 16)
            sp.dma_start(wq_sb[:], wq).then_inc(ld_fold, 16)
            for k in range(SPLIT_FFN, NSPLIT):
                load_chunk(k, experts[:, k - SPLIT_FFN])

            def store(b):
                sp.wait_ge(F.x_added, b.at(1, 1))
                if b.turn is None:
                    dst = out[b.c]
                else:
                    dst = out[bass.ds(b.turn * 2 + b.c, 1)].rearrange("a s d -> (a s) d")
                sp.dma_start(dst, x_of(b)).then_inc(stored, 16)

            loop(sp, store, 0, NB)
            sp.wait_ge(stored, 16 * NB)

        @block.tensor
        def _(pe):
            def turn(dst, src):
                return nc.tensor.transpose(dst, src, ident_sb[:])

            def product(ps, left, right, start, stop):
                nc.tensor.matmul(ps, left[0], right[0], start=start, stop=False)
                nc.tensor.matmul(ps, left[0], right[1], start=False, stop=False)
                return nc.tensor.matmul(ps, left[1], right[0], start=False, stop=stop)

            def layernorm_turn(s, b, ps):
                pe.wait_ge(s.xn_ready, b.at(1, 1))
                for c in range(DC):
                    last = turn(ps[:, c * P:(c + 1) * P], xn[b.parity][:, c * P:(c + 1) * P])
                last.then_inc(s.ln_turned, 1)

            def scores(s, b, u, queries, keys):
                for half in range(2):
                    if b.after(1) or u:
                        pe.wait_ge(s.peaked, b.at(2 * s.U, 2 * u - 1 + half))
                    for m in (2 * half, 2 * half + 1):
                        last = product(score_ps[half][:, (m % 2) * D:(m % 2 + 1) * D],
                                       [q[:, m, :] for q in queries], keys, True, True)
                    last.then_inc(s.scored, 1)

            def turn_weights(s, b, u, turns, exists):
                pe.wait_ge(s.normed, b.at(s.U, u - 2 + 1))
                for j in range(2):
                    wait_turn_bank(pe, s, turns, b, f"p{j}", u, exists)
                    ps = turn_bank(turns, f"p{j}", u)
                    for m in range(4):
                        last = turn(ps[:, m * P:(m + 1) * P], probs[unit_buf(s, b, u - 2)][:, 2 * m + j, :])
                    last.then_inc(s.p_turned, 1)

            def weigh_values(s, b, u, values):
                pe.wait_ge(s.p_t0_ready, b.at(s.U, u - 2))
                pe.wait_ge(s.p_t1_ready, b.at(s.U, u - 2))
                if b.turn is not None or b.c * s.U + u - 3 > 0:
                    pe.wait_ge(s.o_ready, b.at(s.U, u - 3))
                for j in range(2):
                    last = nc.tensor.matmul(pv_ps[j * HD:(j + 1) * HD, :], values(j), probs_t[j][:],
                                            start=True, stop=True)
                last.then_inc(s.pv_done, 1)

            def project_out(s, b, u, weights):
                first, w = (u - 3) % s.U == 0, (u - 3) % s.U
                pe.wait_ge(s.o_ready, b.at(s.U, u - 2))
                if first:
                    done = (u - 3) // s.U
                    if b.c + done > 0 or b.turn is not None:
                        pe.wait_ge(s.x_added, b.at(1, done))
                for m in range(4):
                    last = product(y_ps[:, 0:D], [o[:, m, :] for o in head_out[(u - 3) % 2]],
                                   [x[:, 4 * w + m, :] for x in weights], first and m == 0,
                                   w == s.U - 1 and m == 3)
                last.then_inc(s.o_used, 1)

            def project(b, seq, wait_load=False):
                if seq == 0:
                    pe.wait_ge(A.xn_t_ready, b.at(1, 1))
                if wait_load:
                    pe.wait_ge(w_lo, seq + 1)
                if b.after(1) or seq >= 2:
                    pe.wait_ge(proj_out, b.at(NPROJ, seq - 1))
                for c in range(DC):
                    last = product(proj_ps[seq % 2][:], [t[:, c, :] for t in xn_t[b.parity]],
                                   [w[:, seq, c, :] for w in wqkv_sb], c == 0, c == DC - 1)
                last.then_inc(projected, 1)

            def turn_qk(b, what, step_b, u):
                r = ROPED.index(what)
                pe.wait_ge(roped_done, b.at(NROPE, r + 1))
                wait_turn_bank(pe, A, SELF_TURNS, step_b, what, u, self_exists)
                ps = turn_bank(SELF_TURNS, what, u)
                src = roped[ROPE_BUF[what]][:].rearrange("p a b c -> p (a b c)")
                for m in range(4):
                    last = turn(ps[:, m * P:(m + 1) * P], src[:, m * P:(m + 1) * P])
                last.then_inc(qk_turned, 1)

            def weigh_self(b, u):
                vb, w = (b, 0) if u == 3 else (b + -1, u + 1)
                weigh_values(A, b, u, lambda j: v_n[vb.parity][:, 2 * w + j, :])

            def self_step(b, u, more=True, more2=True, filler=None):
                pe.wait_ge(q_ready, b.at(4, u + 1))
                if u == 0:
                    pe.wait_ge(k_ready, b.at(1, 1))
                scores(A, b, u, q_t[u % 2], [k[:, u].rearrange("p j k -> p (j k)") for k in k_bd[b.parity]])
                made, _, turned = self_inputs(b, u, more)
                first = b.turn is None and b.c == 0 and u == 0
                for tb, what in turned:
                    turn_qk(tb, what, b, u)
                if u == 0 and more:
                    wait_turn_bank(pe, A, SELF_TURNS, b, "ln", 0, self_exists)
                    layernorm_turn(A, b + 1, turn_bank(SELF_TURNS, "ln", 0))
                if b.after(1) or u >= 3:
                    weigh_self(b, u)
                for mb, what in made[:1]:
                    project(mb, PROJ.index(what), first)
                if b.after(1) or u >= 2:
                    turn_weights(A, b, u, SELF_TURNS, self_exists)
                for mb, what in made[1:]:
                    project(mb, PROJ.index(what), first)
                if filler:
                    filler()
                if b.after(1) or u >= 3:
                    if b.turn is None and b.c == 0:
                        pe.wait_ge(w_lo, SPLIT_FFN)
                    project_out(A, b, u, wout_sb)

            def self_batch(b, more=True, more2=True):
                for u in range(4):
                    self_step(b, u, more, more2)

            b0, before = Batch(None, 0), Batch(None, -1)
            pe.wait_ge(ld_ident, 16)
            layernorm_turn(A, b0, turn_bank(SELF_TURNS, "ln", 0))
            project(b0, 0, True)
            project(b0, 1, True)
            turn_qk(b0, "k", before, 3)
            project(b0, 2, True)
            turn_qk(b0, "q0", before, 3)
            project(b0, 3, True)
            pe.wait_ge(zeroed, 1)
            self_batch(b0)
            self_batch(b0 + 1)
            loop(pe, self_batch, 2, NB - 2)
            self_batch(Batch(None, NB - 2), True, False)
            for u in range(3):
                self_step(Batch(None, NB - 1), u, False, False)
            end = Batch(None, NB)

            def head(i, j):
                return 8 * (i // 4) + 4 * j + i % 4

            def fold_first(v):
                pe.wait_ge(A.peaked, 8 * NB - 1 + v)
                for m in range(4):
                    for c in range(2):
                        for j in range(2):
                            h = head(4 * v + m, j)
                            last = nc.tensor.matmul(score_ps[v][j * HD:(j + 1) * HD, m * P:(m + 1) * P],
                                                    wqr_sb[:, c, h, :], wkcq_sb[:, c, h, :],
                                                    start=(c == 0), stop=(c == 1))
                last.then_inc(g_done, 1)

            def fold_second(v):
                pe.wait_ge(g_out, v + 1)
                for m in range(4):
                    last = nc.tensor.matmul(proj_ps[v][:, m * P:(m + 1) * P], fold_g[v][:, m * P:(m + 1) * P],
                                            wkr_sb[:, 4 * v + m, :], start=True, stop=True)
                last.then_inc(b_done, 1)

            def fold_third(t):
                pe.wait_ge(b_out, t // 2 + 1)
                if t >= 2:
                    pe.wait_ge(at_out, t - 1)
                for i in range(2):
                    for j in range(2):
                        cols = slice(((2 * t + i) % 4) * P + j * HD, ((2 * t + i) % 4) * P + (j + 1) * HD)
                        last = nc.tensor.matmul(score_ps[t % 2][j * HD:(j + 1) * HD, i * D:(i + 1) * D],
                                                fold_b[t // 2][:, cols], wq_sb[:, head(2 * t + i, j), :],
                                                start=True, stop=True)
                last.then_inc(at_done, 1)

            def fold_last(t):
                pe.wait_ge(at_out, t + 1)
                if t >= 2:
                    pe.wait_ge(a_out, t - 1)
                for c in range(DC):
                    for i in range(2):
                        last = turn(proj_ps[t % 2][:, (2 * c + i) * P:(2 * c + i + 1) * P],
                                    fold_at[t % 2][:, i * D + c * P:i * D + (c + 1) * P])
                last.then_inc(a_done, 1)

            def fold_out(t):
                if t >= 2:
                    pe.wait_ge(n_out, t - 1)
                for i in range(2):
                    for j in range(2):
                        h = head(2 * t + i, j)
                        last = nc.tensor.matmul(turn_ps[t % 2][j * HD:(j + 1) * HD, i * D:(i + 1) * D],
                                                wkckv_sb[:, h, :], wo_sb[:, h, :], start=True, stop=True)
                last.then_inc(n_done, 1)

            def turn_latents(b, step_b):
                pe.wait_ge(kv_copied, b.at(1, 1))
                wait_turn_bank(pe, C, CROSS_TURNS, step_b, "kv", 0, cross_exists)
                turn(turn_bank(CROSS_TURNS, "kv", 0)[:, 0:P],
                     kv_dup[b.parity][:].rearrange("p a b -> p (a b)")).then_inc(kv_turned, 1)

            def first_load():
                pe.wait_ge(ld_small, 16 * 4)
                pe.wait_ge(ld_wkcq, 16)
                fold_first(0)

            self_step(Batch(None, NB - 1), 3, False, False, first_load)
            for u, filler in enumerate(((fold_first, 1), (fold_second, 0))):
                weigh_self(end, u)
                turn_weights(A, end, u, SELF_TURNS, self_exists)
                filler[0](filler[1])
                project_out(A, end, u, wout_sb)
            weigh_self(end, 2)
            fold_second(1)
            pe.wait_ge(ld_fold, 16 * 2)
            fold_third(0)
            project_out(A, end, 2, wout_sb)
            pe.wait_ge(A.p_t0_ready, 4 * NB)
            pe.wait_ge(A.p_t1_ready, 4 * NB)
            for t in range(1, 4):
                fold_third(t)
                fold_out(t - 1)
                fold_last(t - 1)
            fold_out(3)
            fold_last(3)
            pe.wait_ge(n_out, 4)
            layernorm_turn(C, b0, turn_bank(CROSS_TURNS, "ln", 1))
            turn_latents(b0, before)

            def latent_queries(b, u):
                if u == 0:
                    pe.wait_ge(C.xn_t_ready, b.at(1, 1))
                if b.after(1):
                    pe.wait_ge(cq_ready, b.at(2, u - 1))
                for m in range(4):
                    for c in range(DC):
                        last = nc.tensor.matmul(proj_ps[u][:, m * P:(m + 1) * P],
                                                fold_a[:, c, 4 * u + m, :], xn_tf[b.parity][:, c, :],
                                                start=(c == 0), stop=(c == DC - 1))
                last.then_inc(cq_done, 1)

            def weigh_cross(b, u):
                vb = b + (-1 if u else -2)
                pe.wait_ge(v_copied, vb.at(1, 1))
                weigh_values(C, b, u, lambda j: v_n[vb.parity][:, 0, :])

            def cross_step(b, u, more=True, more2=True, filler=None):
                pe.wait_ge(cq_ready, b.at(2, u + 1))
                if u == 0:
                    pe.wait_ge(kv_t_ready, b.at(1, 1))
                scores(C, b, u, q_t[u], [k[:, 0].rearrange("p j k -> p (j k)") for k in k_bd[b.parity]])
                if u == 0 and more:
                    turn_latents(b + 1, b)
                if u == 1 and more2:
                    wait_turn_bank(pe, C, CROSS_TURNS, b, "ln", 1, cross_exists)
                    layernorm_turn(C, b + 2, turn_bank(CROSS_TURNS, "ln", 1))
                ahead = b.after(2) or (b.after(1) and u >= 1)
                if ahead:
                    weigh_cross(b, u)
                if more:
                    latent_queries(b + 1, u)
                if b.after(1):
                    turn_weights(C, b, u, CROSS_TURNS, cross_exists)
                if filler:
                    filler()
                if ahead:
                    project_out(C, b, u, fold_n)

            def cross_batch(b, more=True, more2=True):
                for u in range(2):
                    cross_step(b, u, more, more2)

            pe.wait_ge(a_out, 3)
            latent_queries(b0, 0)
            pe.wait_ge(a_out, 4)
            latent_queries(b0, 1)
            wait_turn_bank(pe, C, CROSS_TURNS, before, "ln", 1, cross_exists)
            layernorm_turn(C, b0 + 1, turn_bank(CROSS_TURNS, "ln", 1))
            cross_batch(b0)
            cross_batch(b0 + 1)
            loop(pe, cross_batch, 2, NB - 2)
            cross_batch(Batch(None, NB - 2), True, False)
            cross_step(Batch(None, NB - 1), 0, False, False)

            def ffn_turn(b):
                if b.after(1):
                    pe.wait_ge(logit_read, b.at(1, 0))
                layernorm_turn(F, b, pv_ps[:, P:3 * P])

            def experts_in(b, half):
                cols = slice(half * 512, (half + 1) * 512)
                if b.after(1):
                    pe.wait_ge(silu_ready, b.at(2, half - 1))
                for c in range(DC):
                    last = product(score_ps[half][:], [t[:, c, :] for t in xn_t[b.parity]],
                                   [w[:, c, cols] for w in gate_sb], c == 0, c == DC - 1)
                last.then_inc(gate_done, 1)
                if b.after(1):
                    pe.wait_ge(hidden_ready, b.at(2, half - 1))
                for c in range(DC):
                    last = product(proj_ps[half][:], [t[:, c, :] for t in xn_t[b.parity]],
                                   [w[:, c, cols] for w in up_sb], c == 0, c == DC - 1)
                last.then_inc(up_done, 1)

            def turn_hidden(b, half):
                pe.wait_ge(hidden_ready, b.at(2, half + 1))
                if b.after(1):
                    pe.wait_ge(h_t_ready, b.at(2, half - 1))
                for e in range(4):
                    last = turn(turn_ps[half][:, e * P:(e + 1) * P], hidden[half][:, e * P:(e + 1) * P])
                last.then_inc(h_turned, 1)

            def experts_out(b, half):
                pe.wait_ge(h_t_ready, b.at(2, half + 1))
                if half == 0 and b.after(1):
                    pe.wait_ge(F.x_added, b.at(1, 0))
                for e in range(4):
                    last = product(y_ps[:, 0:D], [t[:, e, :] for t in hidden_t[half]],
                                   [w[:, 4 * half + e, :] for w in down_sb], half == 0 and e == 0,
                                   half == 1 and e == 3)
                last.then_inc(down_done, 1)

            def logits(b, ps):
                pe.wait_ge(F.xn_t_ready, b.at(1, 1))
                for c in range(DC):
                    last = product(ps[:, 0:8], [t[:, c, :] for t in xn_t[b.parity]],
                                   [w[:, c, :] for w in router_w], c == 0, c == DC - 1)
                last.then_inc(logit_done, 1)

            def ffn_batch(b, more=True, first=False):
                if not first:
                    logits(b, pv_ps)
                    experts_in(b, 0)
                if b.after(1):
                    turn_hidden(b + -1, 1)
                    experts_out(b + -1, 0)
                if more:
                    ffn_turn(b + 1)
                if not first:
                    experts_in(b, 1)
                turn_hidden(b, 0)
                if b.after(1):
                    experts_out(b + -1, 1)

            def first_tokens():
                pe.wait_ge(C.peaked, 4 * NB)
                layernorm_turn(F, b0, score_ps[1][:, 0:D])

            def first_products():
                pe.wait_ge(rw_ready, 4)
                logits(b0, proj_ps[1])
                pe.wait_ge(w_lo, NSPLIT)
                experts_in(b0, 0)

            cross_step(Batch(None, NB - 1), 1, False, False, first_tokens)
            for u in range(2):
                weigh_cross(end, u)
                turn_weights(C, end, u, CROSS_TURNS, cross_exists)
                if u == 1:
                    first_products()
                project_out(C, end, u, fold_n)
            weigh_cross(end + 1, 0)
            pe.wait_ge(logit_read, 1)
            experts_in(b0, 1)
            project_out(C, end + 1, 0, fold_n)
            pe.wait_ge(C.x_added, NB)
            ffn_batch(b0, first=True)
            ffn_batch(b0 + 1)
            loop(pe, ffn_batch, 2, NB - 2)
            ffn_batch(Batch(None, NB - 2))
            ffn_batch(Batch(None, NB - 1), False)
            turn_hidden(Batch(None, NB - 1), 1)
            experts_out(Batch(None, NB - 1), 0)
            experts_out(Batch(None, NB - 1), 1)

        @block.vector
        def _(dve):
            steps = [0]

            def then(ins):
                steps[0] += 1
                ins.then_inc(norm_step, 1)
                dve.wait_ge(norm_step, steps[0])

            def statistics(s, b):
                dst = (ln_st[:, b.c * 6:(b.c + 1) * 6] if b.turn is None else
                       ln_st[:, bass.ds(b.turn * 12 + b.c * 6, 6)])
                nc.vector.bn_stats(dst, x_of(b)).then_inc(s.stats, 1)

            def start_deviations(s, first, last, n=1):
                dve.wait_ge(s.stats, last)
                for b in range(first, last):
                    ins = nc.vector.bn_aggr(ln_mv[:, b, :], ln_st[:, b * 6:(b + 1) * 6])
                then(ins)
                cols = slice(first, last)
                last_op = nc.vector.tensor_scalar(ln_var[:, 0, cols], ln_mv[:, cols, 1], LN_EPS, None, ALU.add)
                if n == 2:
                    then(last_op)
                    then(nc.vector.reciprocal(ln_tmp[:, 1, cols], ln_var[:, 0, cols]))
                    then(nc.vector.tensor_tensor(ln_var[:, 1, cols], ln_mv[:, cols, 1], ln_tmp[:, 1, cols],
                                                 ALU.mult))
                    last_op = nc.vector.tensor_scalar(ln_var[:, 1, cols], ln_var[:, 1, cols], RMS_EPS, None,
                                                      ALU.add)
                last_op.then_inc(var_ready, 1)

            def finish_deviations(group, first, last, n=1):
                v, std, tmp, dst = [t[:, 0:n, first:last] for t in (ln_var, ln_std, ln_tmp, ln_rs)]
                dve.wait_ge(var_ready, group + 1)
                steps[0] += 1
                nc.vector.tensor_copy(tmp, v).then_inc(norm_step, 1)
                dve.wait_ge(std_ready, group + 1)
                then(nc.vector.reciprocal(dst, std))
                then(nc.vector.tensor_tensor(tmp, tmp, dst, ALU.mult))
                then(nc.vector.tensor_tensor(tmp, tmp, dst, ALU.mult))
                then(nc.vector.tensor_scalar(tmp, tmp, -0.5, 1.5, ALU.mult, ALU.add))
                then(nc.vector.tensor_tensor(dst, dst, tmp, ALU.mult))

            def deviations(s, group, first, last):
                start_deviations(s, first, last)
                finish_deviations(group, first, last)

            def layernorm(s, b):
                p = b.parity
                if b.turn is None:
                    mean, rs = ln_mv[:, b.c, 0:1], ln_rs[:, 0, b.c:b.c + 1]
                else:
                    mean = ln_mv[:].rearrange("p b k -> p (b k)")[:, bass.ds(b.turn * 4 + b.c * 2, 1)]
                    rs = ln_rs[:, 0, bass.ds(b.turn * 2 + b.c, 1)]
                if b.after(2):
                    dve.wait_ge(s.ln_turned, b.at(1, -1))
                nc.vector.tensor_scalar(xn[p][:], x_of(b), mean, rs, ALU.subtract, ALU.mult)\
                    .then_inc(s.xn_ready, 1)

            def peaks(s, b, u, between):
                buf = unit_buf(s, b, u)
                if b.after(1 if s.U == 4 else 2):
                    dve.wait_ge(s.p_turned, b.at(2 * s.U, 2 * (u - 3)))
                for half in range(2):
                    dve.wait_ge(s.scored, b.at(2 * s.U, 2 * u + half + 1))
                    nc.vector.memset(gate_keeper[:, 2 * buf + half:2 * buf + half + 1], 0.0)
                    for i in range(4):
                        h = 4 * half + i
                        start = sink_sb[:, 8 * u + h:8 * u + h + 1] if s.masked else MASKED
                        last = nc.vector.tensor_tensor_reduce(
                            out=probs[buf][:, h, :], in0=score_ps[half][:, i * P:(i + 1) * P],
                            in1=mask_sb[:], scale=1.0, scalar=start,
                            op0=ALU.add, op1=ALU.max, accum_out=peak[:, buf, h:h + 1])
                    last.then_inc(s.peaked, 1)
                    cols = slice(4 * half, 4 * half + 4)
                    dve.wait_ge(s.peaked, b.at(2 * s.U, 2 * u + half + 1))
                    last = nc.vector.tensor_scalar(neg_peak[:, buf, cols], peak[:, buf, cols], -1.0, None,
                                                   ALU.mult)
                    if s.masked:
                        last = nc.vector.tensor_tensor(
                            sink_arg[:, buf, cols], sink_sb[:, 8 * u + 4 * half:8 * u + 4 * half + 4],
                            peak[:, buf, cols], ALU.subtract)
                    last.then_inc(s.shift_ready, 1)
                    if half == 0:
                        between()

            def inverse_sums(s, b, u):
                buf = unit_buf(s, b, u)
                dve.wait_ge(s.exped, b.at(s.U, u + 1))
                if s.masked:
                    nc.vector.tensor_tensor(denom[:, buf, :], row_sum[:, buf, :], sink_exp[:, buf, :],
                                            ALU.add).then_inc(s.summed, 1)
                    dve.wait_ge(s.summed, b.at(s.U, u + 1))
                nc.vector.reciprocal(inv_sum[:, buf, :], (denom if s.masked else row_sum)[:, buf, :])\
                    .then_inc(s.inv_ready, 1)

            def take_weights(s, b, u, turns):
                dve.wait_ge(s.p_turned, b.at(2 * s.U, 2 * (u - 2) + 1))
                if b.turn is not None or b.c * s.U + u - 3 >= 0:
                    dve.wait_ge(s.pv_done, b.at(s.U, u - 2))
                nc.vector.tensor_copy(probs_t[0][:], turn_bank(turns, "p0", u)[:]).then_inc(s.p_t0_ready, 1)

            def low_half(dst, whole, hi):
                return nc.vector.tensor_tensor(dst, whole, hi.bitcast(F32), ALU.subtract)

            def split(k):
                dve.wait_ge(w_hi, k + 1)
                hi, lo = split_place(k)
                low_half(lo, stage[staged(k) % NSTAGE][:], hi).then_inc(w_lo, 1)

            def take_tokens(s, b, ps):
                dve.wait_ge(s.xn_t_hi, b.at(1, 1))
                hi, lo = xn_t[b.parity]
                low_half(flat(lo), ps, flat(hi)).then_inc(s.xn_t_ready, 1)

            def take_heads(s, b, u):
                dve.wait_ge(s.o_hi, b.at(s.U, u - 2))
                hi, lo = head_out[(u - 3) % 2]
                low_half(flat(lo), pv_ps[:], flat(hi)).then_inc(s.o_ready, 1)

            def add_residual(s, b):
                dve.wait_ge(s.o_used, b.at(s.U, s.U))
                nc.vector.tensor_tensor(x_of(b), y_ps[:, 0:D], x_of(b), ALU.add).then_inc(s.x_added, 1)

            def statistics_after(s, after, b):
                dve.wait_ge(s.x_added, b.at(1, 1))
                statistics(after, b)

            def rotate(b, what):
                r, seq = ROPED.index(what), PROJ.index(what)
                buf = (b.parity + r) % 2
                src = roped[ROPE_BUF[what]][:].rearrange("p h (t a) d -> p h t a d", a=2)[:, :, :, 0, :]
                dve.wait_ge(proj_out, b.at(NPROJ, seq + 1))
                if b.turn is not None or b.c * NROPE + r >= 2:
                    dve.wait_ge(roped_done, b.at(NROPE, r - 1))
                nc.vector.tensor_tensor(rot_a[buf][:], src, rope_sb[:, 0][:, None].to_broadcast([P, 8, 2, 16]),
                                        ALU.mult)
                nc.vector.tensor_tensor(rot_b[buf][:], src, rope_sb[:, 1][:, None].to_broadcast([P, 8, 2, 16]),
                                        ALU.mult).then_inc(rot_done, 1)

            def take_qk(b, what, u):
                ps = turn_bank(SELF_TURNS, what, u)
                if what == "k":
                    dve.wait_ge(k_hi, b.at(1, 1))
                    hi, lo = k_bd[b.parity]
                    src = ps[:].rearrange("p (g k) -> p g k", g=4)
                    low_half(lo[0:HD, :, 0, :], src[0:HD], hi[0:HD, :, 0, :])
                    low_half(lo[HD:P, :, 1, :], src[HD:P], hi[HD:P, :, 1, :]).then_inc(k_ready, 1)
                else:
                    g = int(what[1])
                    dve.wait_ge(q_hi, b.at(4, g + 1))
                    hi, lo = q_t[g % 2]
                    low_half(flat(lo), ps[:], flat(hi)).then_inc(q_ready, 1)

            def self_step(b, u, more=True, more2=True):
                _, rotated, turned = self_inputs(b, u, more)

                def low_halves():
                    for tb, what in turned:
                        take_qk(tb, what, u)
                    if u == 0 and more:
                        take_tokens(A, b + 1, turn_bank(SELF_TURNS, "ln", 0)[:, 0:D])
                    if u == 3 or b.after(1):
                        take_heads(A, b, u)

                if u == 3 and b.after(1):
                    add_residual(A, b + -1)
                peaks(A, b, u, low_halves)
                for tb, what in rotated:
                    rotate(tb, what)
                if b.after(1) or u >= 2:
                    take_weights(A, b, u, SELF_TURNS)
                if u == 0 and b.after(2):
                    statistics_after(A, C, b + -2)
                if u == 1 and more2:
                    layernorm(A, b + 2)
                inverse_sums(A, b, u)
                n = 4 * b.c + u if b.turn is None else NB
                if n == 1:
                    dve.wait_ge(ld_x[2], 16)
                for k in range(3 * n + 1, 3 * n + 4) if 1 <= n < 5 else ():
                    statistics(A, Batch(None, k))
                if n == 5:
                    deviations(A, 2, 4, NB)

            def self_batch(b, more=True, more2=True):
                for u in range(4):
                    self_step(b, u, more, more2)

            b0 = Batch(None, 0)
            dve.wait_ge(ld_x[0], 16)
            statistics(A, b0)
            statistics(A, b0 + 1)
            deviations(A, 0, 0, 2)
            layernorm(A, b0)
            layernorm(A, b0 + 1)
            split(0)
            take_tokens(A, b0, turn_bank(SELF_TURNS, "ln", 0)[:, 0:D])
            split(1)
            dve.wait_ge(ld_const, 16 * 3)
            split(2)
            dve.wait_ge(ld_x[1], 16)
            statistics(A, b0 + 2)
            statistics(A, b0 + 3)
            rotate(b0, "k")
            split(3)
            rotate(b0, "q0")
            deviations(A, 1, 2, 4)
            take_qk(b0, "k", 3)
            rotate(b0, "q1")
            take_qk(b0, "q0", 3)
            split(4)
            split(5)
            self_batch(b0)
            self_batch(b0 + 1)
            loop(dve, self_batch, 2, NB - 2)
            self_batch(Batch(None, NB - 2), True, False)
            self_batch(Batch(None, NB - 1), False, False)
            end = Batch(None, NB)
            def fold_b_out(v):
                dve.wait_ge(b_done, v + 1)
                nc.vector.tensor_copy(fold_b[v], proj_ps[v][:]).then_inc(b_out, 1)

            def fold_out(t):
                dve.wait_ge(n_hi, t + 1)
                hi, lo = [flat(n)[:, t * 512:(t + 1) * 512] for n in fold_n]
                low_half(lo, turn_ps[t % 2][:], hi).then_inc(n_out, 1)

            def fold_a_out(t):
                dve.wait_ge(a_done, t + 1)
                nc.vector.tensor_copy(fold_a[:, :, 2 * t:2 * t + 2, :],
                                      proj_ps[t % 2][:].rearrange("p (c i k) -> p c i k", c=DC, i=2))\
                    .then_inc(a_out, 1)

            take_heads(A, end, 0)
            take_weights(A, end, 0, SELF_TURNS)
            statistics_after(A, C, end + -2)
            take_heads(A, end, 1)
            take_weights(A, end, 1, SELF_TURNS)
            fold_b_out(0)
            take_heads(A, end, 2)
            fold_b_out(1)
            add_residual(A, end + -1)
            statistics_after(A, C, end + -1)
            deviations(C, 3, 0, NB)
            nc.vector.memset(mask_sb[:], 0.0).then_inc(zeroed, 1)
            layernorm(C, b0)
            layernorm(C, b0 + 1)
            for t in range(0, 4):
                fold_out(t)
                fold_a_out(t)

            def take_queries(b, u):
                dve.wait_ge(cq_hi, b.at(2, u + 1))
                hi, lo = q_t[u]
                low_half(flat(lo), proj_ps[u][:], flat(hi)).then_inc(cq_ready, 1)

            def take_latents(b):
                dve.wait_ge(kv_t_hi, b.at(1, 1))
                hi, lo = k_bd[b.parity]
                ps = turn_bank(CROSS_TURNS, "kv", 0)
                low_half(lo[0:HD, 0, 0, :], ps[0:HD, 0:P], hi[0:HD, 0, 0, :])
                low_half(lo[HD:P, 0, 1, :], ps[HD:P, 0:P], hi[HD:P, 0, 1, :]).then_inc(kv_t_ready, 1)

            def cross_step(b, u, more=True, more2=True):
                def low_halves():
                    if u == 0:
                        if more:
                            take_latents(b + 1)
                        take_queries(b, 1)
                    elif more:
                        take_queries(b + 1, 0)
                    if b.after(2) or (b.after(1) and u >= 1):
                        take_heads(C, b, u)

                if u == 1 and b.after(2):
                    add_residual(C, b + -2)
                peaks(C, b, u, low_halves)
                if b.after(1):
                    take_weights(C, b, u, CROSS_TURNS)
                if u == 0 and more2:
                    layernorm(C, b + 2)
                inverse_sums(C, b, u)
                if u == 1 and b.after(2):
                    statistics_after(C, F, b + -2)

            def cross_batch(b, more=True, more2=True):
                for u in range(2):
                    cross_step(b, u, more, more2)

            dve.wait_ge(zeroed, 2)
            take_latents(b0)
            take_queries(b0, 0)
            cross_batch(b0)
            cross_batch(b0 + 1)
            loop(dve, cross_batch, 2, NB - 2)
            cross_step(Batch(None, NB - 2), 0, True, False)
            start_deviations(F, 0, EARLY, 2)
            cross_step(Batch(None, NB - 2), 1, True, False)
            finish_deviations(4, 0, EARLY, 2)
            layernorm(F, b0)
            layernorm(F, b0 + 1)
            cross_batch(Batch(None, NB - 1), False, False)
            dve.wait_ge(ld_ffn, 16 * 3)
            for c in range(DC):
                nc.vector.tensor_scalar(router_f[:, c, :], router_sb[:, c, :], norm_sb[:, c:c + 1], None,
                                        ALU.mult).then_inc(rw_ready, 1)
            dve.wait_ge(rw_ready, 2)
            nc.vector.tensor_copy(router_w[0][:], router_f[:]).then_inc(rw_ready, 1)
            dve.wait_ge(rw_ready, 3)
            low_half(router_w[1][:], router_f[:], router_w[0][:]).then_inc(rw_ready, 1)

            def expert_act(b, half):
                dve.wait_ge(gate_tanh, b.at(2, half + 1))
                if b.after(1):
                    dve.wait_ge(hidden_ready, b.at(2, half - 1))
                nc.vector.scalar_tensor_tensor(out=gate_s[half], in0=gate_t[half], scalar=1.0,
                                               in1=score_ps[half][:], op0=ALU.add, op1=ALU.mult)\
                    .then_inc(silu_ready, 1)
                dve.wait_ge(silu_ready, b.at(2, half + 1))
                dve.wait_ge(up_done, b.at(2, half + 1))
                dve.wait_ge(r_ready, b.at(1, 1))
                if b.after(1):
                    dve.wait_ge(h_turned, b.at(2, half - 1))
                for e in range(4):
                    cols = slice(e * P, (e + 1) * P)
                    last = nc.vector.scalar_tensor_tensor(
                        out=hidden[half][:, cols], in0=gate_s[half][:, cols],
                        scalar=r_cw[b.parity][:, 4 * half + e:4 * half + e + 1],
                        in1=proj_ps[half][:, cols], op0=ALU.mult, op1=ALU.mult)
                last.then_inc(hidden_ready, 1)

            def router(b, ps=pv_ps):
                p = b.parity
                k = [0]
                rs = (ln_rs[:, 1, b.c:b.c + 1] if b.turn is None else
                      ln_rs[:, 1, bass.ds(b.turn * 2 + b.c, 1)])

                def then(ins):
                    k[0] += 1
                    ins.then_inc(r_step, 1)
                    dve.wait_ge(r_step, b.at(RSTEPS, k[0]))

                dve.wait_ge(logit_done, b.at(1, 1))
                nc.vector.tensor_scalar(r_log[:], ps[:, 0:8], rs, None, ALU.mult).then_inc(logit_read, 1)
                dve.wait_ge(logit_read, b.at(1, 1))
                then(nc.vector.reduce_max(r_max[:], r_log[:], AX.X))
                nc.vector.tensor_scalar(r_arg[:], r_log[:], r_max[:], None, ALU.subtract)\
                    .then_inc(r_arg_ready, 1)
                other = r_log[:, None, :].to_broadcast([P, 8, 8])
                own = r_log[:, :, None].to_broadcast([P, 8, 8])
                nc.vector.tensor_tensor(r_gt[:], other, own, ALU.is_gt)
                then(nc.vector.tensor_tensor(r_eq[:], other, own, ALU.is_equal))
                then(nc.vector.tensor_tensor(r_eq[:], r_eq[:], tri_sb[:], ALU.mult))
                then(nc.vector.tensor_tensor(r_gt[:], r_gt[:], r_eq[:], ALU.add))
                then(nc.vector.reduce_sum(r_rank[:], r_gt[:], AX.X))
                dve.wait_ge(r_exped, b.at(1, 1))
                then(nc.vector.scalar_tensor_tensor(out=r_sel[:], in0=r_rank[:], scalar=2.0, in1=r_exp[:],
                                                    op0=ALU.is_lt, op1=ALU.mult))
                then(nc.vector.reduce_sum(r_sum[:], r_sel[:], AX.X))
                then(nc.vector.reciprocal(r_inv[:], r_sum[:]))
                assert k[0] == RSTEPS
                nc.vector.tensor_scalar(r_cw[p][:], r_sel[:], r_inv[:], 2.0, ALU.mult, ALU.mult)\
                    .then_inc(r_ready, 1)

            for u in range(2):
                if u == 0:
                    take_tokens(F, b0, score_ps[1][:, 0:D])
                take_heads(C, end, u)
                take_weights(C, end, u, CROSS_TURNS)
            router(b0, proj_ps[1])
            add_residual(C, end + -2)
            statistics_after(C, F, end + -2)
            take_heads(C, end + 1, 0)
            expert_act(b0, 0)
            add_residual(C, end + -1)
            statistics_after(C, F, end + -1)

            def take_hidden(b, half):
                dve.wait_ge(h_t_hi, b.at(2, half + 1))
                hi, lo = hidden_t[half]
                low_half(flat(lo), turn_ps[half][:], flat(hi)).then_inc(h_t_ready, 1)

            def ffn_residual(b):
                dve.wait_ge(down_done, b.at(2, 2))
                nc.vector.tensor_tensor(x_of(b), y_ps[:, 0:D], x_of(b), ALU.add).then_inc(F.x_added, 1)

            def ffn_batch(b, more=True, more2=True):
                if b.after(1):
                    router(b)
                    expert_act(b, 0)
                if b.after(1):
                    take_hidden(b + -1, 1)
                if more:
                    take_tokens(F, b + 1, pv_ps[:, P:3 * P])
                if more2:
                    layernorm(F, b + 2)
                expert_act(b, 1)
                take_hidden(b, 0)
                if b.after(1):
                    ffn_residual(b + -1)

            ffn_batch(b0)
            start_deviations(F, EARLY, NB, 2)
            ffn_batch(b0 + 1)
            finish_deviations(5, EARLY, NB, 2)
            loop(dve, ffn_batch, 2, NB - 2)
            ffn_batch(Batch(None, NB - 2), True, False)
            ffn_batch(Batch(None, NB - 1), False, False)
            take_hidden(Batch(None, NB - 1), 1)
            ffn_residual(Batch(None, NB - 1))

        @block.scalar
        def _(act):
            def split(k):
                wait_staged(act, staged(k))
                nc.scalar.activation(split_place(k)[0], stage[staged(k) % NSTAGE][:], ACT.Copy).then_inc(w_hi, 1)

            def take_tokens(s, b, ps):
                act.wait_ge(s.ln_turned, b.at(1, 1))
                if s is C:
                    nc.scalar.activation(flat(xn_tf[b.parity]), ps, ACT.Copy).then_inc(s.xn_t_ready, 1)
                else:
                    nc.scalar.activation(flat(xn_t[b.parity][0]), ps, ACT.Copy).then_inc(s.xn_t_hi, 1)

            def take_heads(s, b, u):
                act.wait_ge(s.pv_done, b.at(s.U, u - 2))
                if b.turn is not None or b.c * s.U + u - 5 >= 0:
                    act.wait_ge(s.o_used, b.at(s.U, u - 4))
                nc.scalar.activation(flat(head_out[(u - 3) % 2][0]), pv_ps[:], ACT.Copy).then_inc(s.o_hi, 1)

            def exponentials(s, b, u, between):
                buf = unit_buf(s, b, u)
                act.wait_ge(s.shift_ready, b.at(2 * s.U, 2 * u + 1))
                for h in range(8):
                    if h == 4:
                        between()
                        act.wait_ge(s.shift_ready, b.at(2 * s.U, 2 * u + 2))
                        if s.masked:
                            nc.scalar.activation(sink_exp[:, buf, :], sink_arg[:, buf, :], ACT.Exp)
                    last = nc.scalar.activation(probs[buf][:, h, :], probs[buf][:, h, :], ACT.Exp,
                                                bias=neg_peak[:, buf, h:h + 1],
                                                accum_out=row_sum[:, buf, h:h + 1])
                last.then_inc(s.exped, 1)

            def take_weights(s, b, u, turns):
                act.wait_ge(s.p_turned, b.at(2 * s.U, 2 * (u - 2) + 2))
                if b.turn is not None or b.c * s.U + u - 3 >= 0:
                    act.wait_ge(s.pv_done, b.at(s.U, u - 2))
                nc.scalar.activation(probs_t[1][:], turn_bank(turns, "p1", u)[:], ACT.Copy)\
                    .then_inc(s.p_t1_ready, 1)

            def roots(group, first, last, n=1):
                act.wait_ge(var_ready, group + 1)
                nc.scalar.activation(ln_std[:, 0:n, first:last], ln_var[:, 0:n, first:last], ACT.Sqrt)\
                    .then_inc(std_ready, 1)

            def fetch_exp_table(k):
                nc.scalar.activation(table_keeper[:, k:k + 1], ident_sb[:, 0:1], ACT.Exp)

            def take_plain(b, seq):
                act.wait_ge(projected, b.at(NPROJ, seq + 1))
                what = PROJ[seq]
                if what == "v":
                    if b.after(2):
                        act.wait_ge(A.pv_done, b.at(4, -4))
                    nc.scalar.activation(v_n[b.parity][:].rearrange("p a b -> p (a b)"), proj_ps[seq % 2][:],
                                         ACT.Copy).then_inc(proj_out, 1)
                    return
                r = ROPED.index(what)
                if b.after(1) or ROPE_BEFORE[what] >= 0:
                    act.wait_ge(qk_turned, b.at(NROPE, ROPE_BEFORE[what] + 1))
                nc.scalar.activation(roped[ROPE_BUF[what]][:].rearrange("p a b c -> p (a b c)"),
                                     proj_ps[seq % 2][:], ACT.Copy, scale=1.0 if what == "k" else HD ** -0.5)\
                    .then_inc(proj_out, 1)

            def take_qk(b, what, u):
                r = ROPED.index(what)
                act.wait_ge(qk_turned, b.at(NROPE, r + 1))
                ps = turn_bank(SELF_TURNS, what, u)
                if what == "k":
                    if b.after(2):
                        act.wait_ge(A.scored, b.at(8, -8))
                    src = ps[:].rearrange("p (g k) -> p g k", g=4)
                    nc.scalar.activation(k_bd[b.parity][0][0:HD, :, 0, :], src[0:HD], ACT.Copy)
                    nc.scalar.activation(k_bd[b.parity][0][HD:P, :, 1, :], src[HD:P], ACT.Copy)\
                        .then_inc(k_hi, 1)
                else:
                    g = int(what[1])
                    if b.after(1) or g >= 2:
                        act.wait_ge(A.scored, b.at(8, 2 * (g - 2) + 2))
                    nc.scalar.activation(flat(q_t[g % 2][0]), ps[:], ACT.Copy).then_inc(q_hi, 1)

            def self_step(b, u, more=True, more2=True):
                def between():
                    for mb, what in made[:1]:
                        take_plain(mb, PROJ.index(what))
                    if b.after(1) or u >= 2:
                        take_weights(A, b, u, SELF_TURNS)
                made, _, turned = self_inputs(b, u, more)
                for tb, what in turned:
                    take_qk(tb, what, u)
                if u == 0 and more:
                    if b.after(1):
                        act.wait_ge(projected, b.at(NPROJ, 0))
                    take_tokens(A, b + 1, turn_bank(SELF_TURNS, "ln", 0)[:, 0:D])
                if u == 3 or b.after(1):
                    take_heads(A, b, u)
                exponentials(A, b, u, between)
                for mb, what in made[1:]:
                    take_plain(mb, PROJ.index(what))
                if b.turn is None and b.c == 0:
                    for k in ((0, 1), (2,), (3,), ())[u]:
                        split(SPLIT_OUT + k)
                if b.turn is None and (b.c, u) == (1, 1):
                    roots(2, 4, NB)

            def self_batch(b, more=True, more2=True):
                for u in range(4):
                    self_step(b, u, more, more2)

            b0 = Batch(None, 0)
            roots(0, 0, 2)
            split(0)
            take_tokens(A, b0, turn_bank(SELF_TURNS, "ln", 0)[:, 0:D])
            split(1)
            split(2)
            act.wait_ge(zeroed, 1)
            take_plain(b0, 0)
            split(3)
            take_plain(b0, 1)
            roots(1, 2, 4)
            fetch_exp_table(0)
            take_plain(b0, 2)
            take_qk(b0, "k", 3)
            take_qk(b0, "q0", 3)
            take_plain(b0, 3)
            split(4)
            split(5)
            self_batch(b0)
            self_batch(b0 + 1)
            loop(act, self_batch, 2, NB - 2)
            self_batch(Batch(None, NB - 2), True, False)
            self_batch(Batch(None, NB - 1), False, False)
            end = Batch(None, NB)
            def fold_g_out(v):
                act.wait_ge(g_done, v + 1)
                nc.scalar.activation(fold_g[v], score_ps[v][:], ACT.Copy).then_inc(g_out, 1)

            def fold_at_out(t):
                act.wait_ge(at_done, t + 1)
                if t >= 2:
                    act.wait_ge(a_done, t - 1)
                nc.scalar.activation(fold_at[t % 2], score_ps[t % 2][:], ACT.Copy).then_inc(at_out, 1)

            def fold_out(t):
                act.wait_ge(n_done, t + 1)
                nc.scalar.activation(flat(fold_n[0])[:, t * 512:(t + 1) * 512], turn_ps[t % 2][:], ACT.Copy)\
                    .then_inc(n_hi, 1)

            for u in range(2):
                fold_g_out(u)
                take_heads(A, end, u)
                take_weights(A, end, u, SELF_TURNS)
            take_heads(A, end, 2)
            fold_at_out(0)
            fold_at_out(1)
            roots(3, 0, NB)
            fetch_exp_table(1)
            fold_out(0)
            fold_at_out(2)
            fold_out(1)
            fold_at_out(3)
            fold_out(2)
            fold_out(3)

            def take_latents(b):
                act.wait_ge(kv_turned, b.at(1, 1))
                if b.after(2):
                    act.wait_ge(C.scored, b.at(4, -4))
                ps = turn_bank(CROSS_TURNS, "kv", 0)
                nc.scalar.activation(k_bd[b.parity][0][0:HD, 0, 0, :], ps[0:HD, 0:P], ACT.Copy)
                nc.scalar.activation(k_bd[b.parity][0][HD:P, 0, 1, :], ps[HD:P, 0:P], ACT.Copy)\
                    .then_inc(kv_t_hi, 1)

            def take_queries(b, u):
                act.wait_ge(cq_done, b.at(2, u + 1))
                if b.after(1):
                    act.wait_ge(C.scored, b.at(4, 2 * (u - 2) + 2))
                nc.scalar.activation(flat(q_t[u][0]), proj_ps[u][:], ACT.Copy)\
                    .then_inc(cq_hi, 1)

            def cross_step(b, u, more=True, more2=True):
                def between():
                    if b.after(1):
                        take_weights(C, b, u, CROSS_TURNS)
                if u == 0 and more:
                    take_latents(b + 1)
                if u == 1 and more2:
                    act.wait_ge(cq_done, b.at(2, 2))
                    take_tokens(C, b + 2, turn_bank(CROSS_TURNS, "ln", 1)[:, 0:D])
                if b.after(2) or (b.after(1) and u >= 1):
                    take_heads(C, b, u)
                exponentials(C, b, u, between)
                if more:
                    take_queries(b + 1, u)
                k = split_in(b, u, 0)
                if k:
                    split(k)

            def cross_batch(b, more=True, more2=True):
                for u in range(2):
                    cross_step(b, u, more, more2)

            take_tokens(C, b0, turn_bank(CROSS_TURNS, "ln", 1)[:, 0:D])
            take_latents(b0)
            take_queries(b0, 0)
            take_queries(b0, 1)
            take_tokens(C, b0 + 1, turn_bank(CROSS_TURNS, "ln", 1)[:, 0:D])
            cross_batch(b0)
            cross_batch(b0 + 1)
            loop(act, cross_batch, 2, NB - 2)
            cross_step(Batch(None, NB - 2), 0, True, False)
            roots(4, 0, EARLY, 2)
            fetch_exp_table(2)
            cross_step(Batch(None, NB - 2), 1, True, False)
            cross_batch(Batch(None, NB - 1), False, False)
            take_tokens(F, b0, score_ps[1][:, 0:D])
            for u in range(2):
                take_heads(C, end, u)
                take_weights(C, end, u, CROSS_TURNS)

            def router_exp(b):
                act.wait_ge(r_arg_ready, b.at(1, 1))
                nc.scalar.activation(r_exp[:], r_arg[:], ACT.Exp).then_inc(r_exped, 1)

            router_exp(b0)
            take_heads(C, end + 1, 0)

            def ffn_tokens(b):
                if b.after(2):
                    act.wait_ge(up_done, b.at(2, -2))
                take_tokens(F, b, pv_ps[:, P:3 * P])

            def gate_tanhs(b, half):
                act.wait_ge(gate_done, b.at(2, half + 1))
                if b.after(1):
                    act.wait_ge(silu_ready, b.at(2, half - 1))
                nc.scalar.activation(gate_t[half], score_ps[half][:], ACT.Tanh, scale=0.5)\
                    .then_inc(gate_tanh, 1)

            def take_hidden(b, half):
                act.wait_ge(h_turned, b.at(2, half + 1))
                if b.after(1):
                    act.wait_ge(down_done, b.at(2, half - 1))
                nc.scalar.activation(flat(hidden_t[half][0]), turn_ps[half][:], ACT.Copy).then_inc(h_t_hi, 1)

            def ffn_batch(b, more=True):
                if b.after(1):
                    act.wait_ge(r_ready, b.at(1, 0))
                    router_exp(b)
                gate_tanhs(b, 0)
                if b.after(1):
                    take_hidden(b + -1, 1)
                if more:
                    ffn_tokens(b + 1)
                gate_tanhs(b, 1)
                take_hidden(b, 0)

            ffn_batch(b0)
            roots(5, EARLY, NB, 2)
            fetch_exp_table(3)
            ffn_batch(b0 + 1)
            loop(act, ffn_batch, 2, NB - 2)
            ffn_batch(Batch(None, NB - 2))
            ffn_batch(Batch(None, NB - 1), False)
            take_hidden(Batch(None, NB - 1), 1)

        @block.gpsimd
        def _(pool):
            def normalise(s, b, u):
                buf = unit_buf(s, b, u)
                pool.wait_ge(s.inv_ready, b.at(s.U, u + 1))
                nc.gpsimd.tensor_tensor(probs[buf][:], probs[buf][:],
                                        inv_sum[:, buf, :][:, :, None].to_broadcast([P, 8, P]), ALU.mult)\
                    .then_inc(s.normed, 1)

            def add_rotated(b, what):
                r = ROPED.index(what)
                buf = (b.parity + r) % 2
                pool.wait_ge(rot_done, b.at(NROPE, r + 1))
                dst = roped[ROPE_BUF[what]][:].rearrange("p h (t a) d -> p h t a d", a=2)[:, :, :, 0, :]
                for t in range(2):
                    last = nc.gpsimd.tensor_tensor(dst[:, :, t, :], rot_a[buf][:, :, t, :],
                                                   rot_b[buf][:, :, 1 - t, :], ALU.add)
                last.then_inc(roped_done, 1)

            def split(k):
                pool.wait_ge(w_hi, k + 1)
                pool.wait_ge(w_lo, k)
                hi, lo = split_place(k)
                nc.gpsimd.tensor_tensor(lo, stage[staged(k) % NSTAGE][:], hi.bitcast(F32), ALU.subtract)\
                    .then_inc(w_lo, 1)

            def self_step(b, u, more=True):
                if b.after(1) or u:
                    normalise(A, b, u - 1)
                for tb, what in self_inputs(b, u, more)[1]:
                    add_rotated(tb, what)
                if b.turn is None and b.c == 0:
                    for k in ((0,), (1, 2), (3,), ())[u]:
                        split(SPLIT_OUT + k)

            def self_batch(b, more=True):
                for u in range(4):
                    self_step(b, u, more)

            b0 = Batch(None, 0)
            for p in range(2):
                for k in k_bd[p]:
                    last = nc.gpsimd.memset(k[:].bitcast(F32), 0.0)
            last.then_inc(zeroed, 1)
            add_rotated(b0, "k")
            pool.dma_start(X[:].rearrange("p (b d) -> p b d", d=D)[:, 4:NB],
                           x.rearrange("b s d -> s b d")[:, 4:NB]).then_inc(ld_x[2], 16)
            add_rotated(b0, "q0")
            add_rotated(b0, "q1")
            self_batch(b0)
            self_batch(b0 + 1)
            loop(pool, self_batch, 2, NB - 2)
            self_batch(Batch(None, NB - 2))
            self_batch(Batch(None, NB - 1), False)
            end = Batch(None, NB)
            normalise(A, end, -1)

            wait_staged(pool, SPLIT_FFN)
            pool.wait_ge(ld_small, 16 * 4)
            kv_v = kv_rope[:].rearrange("p (b d) -> p b d", d=HD)
            half = HD // 2
            nc.gpsimd.tensor_tensor(kv_v, ctx_sb, rope_c_sb[:, 0][:, None].to_broadcast([P, NB, HD]),
                                    ALU.mult).then_inc(kv_part, 1)
            pool.wait_ge(kv_part, 1)
            nc.gpsimd.tensor_tensor(ctx_sb, ctx_sb, rope_c_sb[:, 1][:, None].to_broadcast([P, NB, HD]),
                                    ALU.mult).then_inc(kv_part, 1)
            pool.wait_ge(kv_part, 2)
            nc.gpsimd.tensor_tensor(kv_v[:, :, 0:half], kv_v[:, :, 0:half], ctx_sb[:, :, half:HD], ALU.add)
            nc.gpsimd.tensor_tensor(kv_v[:, :, half:HD], kv_v[:, :, half:HD], ctx_sb[:, :, 0:half], ALU.add)\
                .then_inc(kv_done, 1)

            def latents_of(b):
                if b.turn is None:
                    return kv_rope[:, b.c * HD:(b.c + 1) * HD]
                return kv_rope[:, bass.ds(b.turn * (2 * HD) + b.c * HD, HD)]

            def copy_keys(b):
                if b.after(2):
                    pool.wait_ge(kv_turned, b.at(1, -1))
                nc.gpsimd.tensor_copy(kv_dup[b.parity][:, 0, :], latents_of(b))
                nc.gpsimd.tensor_copy(kv_dup[b.parity][:, 1, :], latents_of(b)).then_inc(kv_copied, 1)

            def copy_values(b):
                if b.after(2):
                    pool.wait_ge(C.pv_done, b.at(2, -2))
                nc.gpsimd.tensor_copy(v_n[b.parity][:, 0, :], latents_of(b)).then_inc(v_copied, 1)

            def cross_step(b, u, more2=True):
                if b.after(1) or u:
                    normalise(C, b, u - 1)
                if u == 0:
                    copy_values(b)
                elif more2:
                    copy_keys(b + 2)
                k = split_in(b, u, 1)
                if k:
                    split(k)

            def cross_batch(b, more2=True):
                for u in range(2):
                    cross_step(b, u, more2)

            pool.wait_ge(kv_done, 1)
            copy_keys(b0)
            copy_keys(b0 + 1)
            cross_batch(b0)
            cross_batch(b0 + 1)
            loop(pool, cross_batch, 2, NB - 2)
            cross_batch(Batch(None, NB - 2), False)
            cross_batch(Batch(None, NB - 1), False)
            normalise(C, end, -1)


def _rope_tables():
    inv = np.power(np.float32(1.0 / 1024.0), np.linspace(0.0, 1.0, 16, dtype=np.float32)).astype(np.float32)
    theta = (np.arange(P, dtype=np.float32)[:, None] * inv[None, :]).astype(np.float32)
    cos, sin = np.cos(theta.astype(np.float64)), np.sin(theta.astype(np.float64))
    rope = np.stack([np.stack([cos, cos], 1), np.stack([-sin, sin], 1)], 1)
    inv_c = (np.float32(1.0) / np.power(np.float32(10000.0), np.arange(0, HD, 2, dtype=np.float32)
                                        / np.float32(HD))).astype(np.float32)
    freqs = (np.arange(P, dtype=np.float32)[:, None] * inv_c[None, :]).astype(np.float32).astype(np.float64)
    sin_c, cos_c = np.repeat(np.sin(freqs), 2, -1), np.repeat(np.cos(freqs), 2, -1)
    signed = np.concatenate([sin_c[:, HD // 2:], -sin_c[:, :HD // 2]], -1)
    return (rope.astype(np.float32),
            np.stack([cos_c, signed], 1).astype(np.float32))


def _layouts(x, ctx_512, L0_attn_W_qkv, L0_attn_W_out, L0_attn_s, L0_xattn_Wq, L0_xattn_w_kc_q,
             L0_xattn_w_kc_kv, L0_xattn_W_qr, L0_xattn_W_kr, L0_xattn_Wo, L0_ffn_router_w,
             L0_ffn_norm_w, L0_ffn_gate_w, L0_ffn_up_w, L0_ffn_down_w):
    def rows(w):
        return w.reshape(-1, P, *w.shape[1:]).swapaxes(0, 1)

    wq = L0_attn_W_qkv[:, :2048].reshape(D, 4, 2, 4, HD).transpose(0, 1, 3, 2, 4).reshape(D, 4, 512)
    wk, wv = L0_attn_W_qkv[:, 2048:2560], L0_attn_W_qkv[:, 2560:3072]
    banks = np.stack([{"k": wk, "v": wv}.get(s) if s in "kv" else wq[:, int(s[1])] for s in PROJ], 1)
    wqkv = banks.reshape(DC, P, NPROJ, 512).transpose(1, 2, 0, 3).reshape(P, NPROJ, 1024)
    wout = L0_attn_W_out.reshape(4, 2, 4, HD, D).transpose(0, 2, 1, 3, 4).reshape(2048, D)
    sink = L0_attn_s.reshape(4, 2, 4).transpose(0, 2, 1).reshape(32)
    rope, rope_c = _rope_tables()
    pos = np.arange(P)
    q, k = pos[:, None], pos[None, :]
    mask = np.where((q >= k) & (q < k + 64), MASKED, 0.0).astype(np.float32)
    by_head = lambda w: w.transpose(2, 0, 1)
    wqr = L0_xattn_W_qr.transpose(1, 0, 2).reshape(2, 96, 16, HD).swapaxes(0, 1)
    wkr = np.zeros((2, HD, 2, 4, 2, HD), np.float32)
    for j in range(2):
        wkr[j, :, :, :, j, :] = by_head(L0_xattn_W_kr).reshape(HD, 2, 2, 4, HD)[:, :, j]
    wkr = wkr.reshape(P, 8, 2 * HD)
    wkcq = by_head(L0_xattn_w_kc_q).reshape(2, 96, 16, P).transpose(1, 0, 2, 3)
    inward = lambda w: rows(w.transpose(1, 0, 2).reshape(D, 1024))
    down = L0_ffn_down_w.transpose(1, 0, 2).reshape(P, 2, 1024)
    experts = np.concatenate([inward(L0_ffn_gate_w), inward(L0_ffn_up_w), down], 1)
    tri = np.broadcast_to((pos[None, :8] < pos[:8, None]).astype(np.float32), (P, 8, 8))
    return dict(
        x=x, ctx=ctx_512, wqkv=wqkv, wout=rows(wout).reshape(P, 4, 1024), sink=sink, wqr_t=wqr,
        wkr_t=wkr, wkcq_t=wkcq, wq=rows(L0_xattn_Wq),
        wkckv=L0_xattn_w_kc_kv.transpose(1, 0, 2), wo_t=rows(L0_xattn_Wo.T),
        router=rows(L0_ffn_router_w.T), norm_w=rows(L0_ffn_norm_w), experts=experts,
        ident=np.eye(P, dtype=np.float32), mask=mask, rope=rope, rope_c=rope_c,
        tri=tri)


def kernel(**inputs):
    import concourse.bacc as bacc
    from concourse.bass_utils import run_bass_kernel_spmd

    nc = bacc.Bacc("TRN2", target_bir_lowering=False, num_devices=1)
    arrays, args = {}, {}
    for name, a in _layouts(**{k: np.asarray(v) for k, v in inputs.items()}).items():
        a = np.ascontiguousarray(a)
        arrays[f"in_{name}"] = a
        args[name] = nc.dram_tensor(f"in_{name}", a.shape, mybir.dt.from_np(a.dtype), kind="ExternalInput").ap()
    args["out"] = nc.dram_tensor("out_y", (NB, P, D), F32, kind="ExternalOutput").ap()
    decoder_layer(nc, **args)
    return run_bass_kernel_spmd(nc, [arrays], core_ids=[0]).results[0]["out_y"]
```
